# Optimizing a Trainium2 kernel written in Bass

```python
import numpy as np
import jax
import jax.numpy as jnp

def _softmax(x, axis=-1):
    return jax.nn.softmax(x, axis=axis)

def _gelu(x):
    return jax.nn.gelu(x, approximate=True)

def _silu(x):
    return jax.nn.silu(x)

def _sigmoid(x):
    return jax.nn.sigmoid(x)

def _layernorm(x, axis=-1, eps=1e-05):
    m = jnp.mean(x, axis=axis, keepdims=True)
    v = jnp.var(x, axis=axis, keepdims=True)
    return (x - m) / jnp.sqrt(v + eps)

def _scatter_add(tgt, idx, src, axis=0):
    return tgt.at[idx].add(src)

def _segment_sum(src, seg, n):
    return jax.ops.segment_sum(src, seg, n)
kernel_name = 'mk_conv_seq_d2_conv_nhwc512_r2_5fb94e'

def setup_inputs(seed: int=0):
    np.random.seed(seed)
    _w = jnp.asarray

    def _rec_inputs():
        import jax
        import jax.numpy as jnp
        _gk = jax.random.key(seed)
        x = 7.22e-05 + 1 * jax.random.normal(jax.random.fold_in(_gk, 1), (4, 32, 32, 256), jnp.float32)
        return x
    x = _rec_inputs()

    def _L0_conv_setup():
        import jax, jax.numpy as jnp
        import numpy as np
        B, H, W, C = (4, 32, 32, 256)
        R, NH, KS = (2, 8, 7)
        S = 1.0

        def layernorm(t, g, b):
            m = t.mean(-1, keepdims=True)
            v = ((t - m) ** 2).mean(-1, keepdims=True)
            return (t - m) / jnp.sqrt(v + 1e-05) * g + b

        def grid_sample_bilinear_zeros(img, grid):
            b, c, h, w = img.shape
            gh, gw = (grid.shape[1], grid.shape[2])
            x = (grid[..., 0] + 1.0) * 0.5 * (w - 1)
            y = (grid[..., 1] + 1.0) * 0.5 * (h - 1)
            x0 = jnp.floor(x)
            y0 = jnp.floor(y)
            wx1 = x - x0
            wy1 = y - y0
            x0i = x0.astype(jnp.int32)
            y0i = y0.astype(jnp.int32)
            flat = img.reshape(b, c, h * w)

            def corner(xi, yi, wt):
                valid = ((xi >= 0) & (xi < w) & (yi >= 0) & (yi < h)).astype(img.dtype)
                idx = jnp.clip(yi, 0, h - 1) * w + jnp.clip(xi, 0, w - 1)
                vals = jnp.take_along_axis(flat, idx.reshape(b, 1, gh * gw), axis=2)
                return vals * (valid * wt).reshape(b, 1, gh * gw)
            out = corner(x0i, y0i, (1 - wx1) * (1 - wy1)) + corner(x0i + 1, y0i, wx1 * (1 - wy1)) + corner(x0i, y0i + 1, (1 - wx1) * wy1) + corner(x0i + 1, y0i + 1, wx1 * wy1)
            return out.reshape(b, c, gh, gw)
        key = jax.random.key(seed)
        ks = jax.random.split(key, 12)
        sd = 0.02
        f32 = jnp.float32
        return {'x': jax.random.normal(ks[0], (B, H, W, C), f32), 'ln_g': jnp.ones((C,), f32), 'ln_b': jnp.zeros((C,), f32), 'wq': jax.random.normal(ks[1], (C, C), f32) * sd, 'bq': jnp.zeros((C,), f32), 'wv': jax.random.normal(ks[2], (C, C), f32) * sd, 'bv': jnp.zeros((C,), f32), 'dw_w': jax.random.normal(ks[3], (C, 1, KS, KS), f32) * sd, 'dw_b': jnp.zeros((C,), f32), 'pw_w': jax.random.normal(ks[4], (2, C, 1, 1), f32) * sd, 'mq_w': jax.random.normal(ks[5], (C, C), f32) * sd, 'mq_b': jnp.zeros((C,), f32), 'mk_w': jax.random.normal(ks[6], (C, C), f32) * sd, 'mk_b': jnp.zeros((C,), f32), 'mv_w': jax.random.normal(ks[7], (C, C), f32) * sd, 'mv_b': jnp.zeros((C,), f32), 'mo_w': jax.random.normal(ks[8], (C, C), f32) * sd, 'mo_b': jnp.zeros((C,), f32), 'mlp_w': jax.random.normal(ks[9], (C, C), f32) * sd, 'mlp_b': jnp.zeros((C,), f32)}
    _L0_conv_all = _L0_conv_setup()
    _L0_conv_in = {k: v for k, v in _L0_conv_all.items() if k in ('ln_g', 'ln_b', 'wq', 'bq', 'wv', 'bv', 'dw_w', 'dw_b', 'pw_w', 'mq_w', 'mq_b', 'mk_w', 'mk_b', 'mv_w', 'mv_b', 'mo_w', 'mo_b', 'mlp_w', 'mlp_b')}
    del _L0_conv_all

    def _L1_conv_setup():
        import jax, jax.numpy as jnp
        import numpy as np
        B, H, W, C = (8, 32, 32, 256)

        def maxpool2x2(x):
            b, h, w, c = x.shape
            return x.reshape(b, h // 2, 2, w // 2, 2, c).max(axis=(2, 4))
        key = jax.random.key(seed)
        ks = jax.random.split(key, 9)
        c8, c2 = (C // 8, C // 2)
        s_in = 1.0 / np.sqrt(C)
        s_g = 1.0 / np.sqrt(c2)
        return {'x': jax.random.normal(ks[0], (B, H, W, C), jnp.float32), 'w_theta': jax.random.normal(ks[1], (C, c8), jnp.float32) * s_in, 'b_theta': jnp.zeros((c8,), jnp.float32), 'w_phi': jax.random.normal(ks[2], (C, c8), jnp.float32) * s_in, 'b_phi': jnp.zeros((c8,), jnp.float32), 'w_g': jax.random.normal(ks[3], (C, c2), jnp.float32) * s_in, 'b_g': jnp.zeros((c2,), jnp.float32), 'w_o': jax.random.normal(ks[4], (c2, C), jnp.float32) * s_g, 'b_o': jnp.zeros((C,), jnp.float32), 'sigma': jnp.array(0.7, jnp.float32)}
    _L1_conv_all = _L1_conv_setup()
    _L1_conv_in = {k: v for k, v in _L1_conv_all.items() if k in ('w_theta', 'b_theta', 'w_phi', 'b_phi', 'w_g', 'b_g', 'w_o', 'b_o', 'sigma')}
    del _L1_conv_all
    return {'x': x, 'L0_conv_ln_g': _L0_conv_in['ln_g'], 'L0_conv_ln_b': _L0_conv_in['ln_b'], 'L0_conv_wq': _L0_conv_in['wq'], 'L0_conv_bq': _L0_conv_in['bq'], 'L0_conv_wv': _L0_conv_in['wv'], 'L0_conv_bv': _L0_conv_in['bv'], 'L0_conv_dw_w': _L0_conv_in['dw_w'], 'L0_conv_dw_b': _L0_conv_in['dw_b'], 'L0_conv_pw_w': _L0_conv_in['pw_w'], 'L0_conv_mq_w': _L0_conv_in['mq_w'], 'L0_conv_mq_b': _L0_conv_in['mq_b'], 'L0_conv_mk_w': _L0_conv_in['mk_w'], 'L0_conv_mk_b': _L0_conv_in['mk_b'], 'L0_conv_mv_w': _L0_conv_in['mv_w'], 'L0_conv_mv_b': _L0_conv_in['mv_b'], 'L0_conv_mo_w': _L0_conv_in['mo_w'], 'L0_conv_mo_b': _L0_conv_in['mo_b'], 'L0_conv_mlp_w': _L0_conv_in['mlp_w'], 'L0_conv_mlp_b': _L0_conv_in['mlp_b'], 'L1_conv_w_theta': _L1_conv_in['w_theta'], 'L1_conv_b_theta': _L1_conv_in['b_theta'], 'L1_conv_w_phi': _L1_conv_in['w_phi'], 'L1_conv_b_phi': _L1_conv_in['b_phi'], 'L1_conv_w_g': _L1_conv_in['w_g'], 'L1_conv_b_g': _L1_conv_in['b_g'], 'L1_conv_w_o': _L1_conv_in['w_o'], 'L1_conv_b_o': _L1_conv_in['b_o'], 'L1_conv_sigma': _L1_conv_in['sigma']}

def reference(x, L0_conv_ln_g, L0_conv_ln_b, L0_conv_wq, L0_conv_bq, L0_conv_wv, L0_conv_bv, L0_conv_dw_w, L0_conv_dw_b, L0_conv_pw_w, L0_conv_mq_w, L0_conv_mq_b, L0_conv_mk_w, L0_conv_mk_b, L0_conv_mv_w, L0_conv_mv_b, L0_conv_mo_w, L0_conv_mo_b, L0_conv_mlp_w, L0_conv_mlp_b, L1_conv_w_theta, L1_conv_b_theta, L1_conv_w_phi, L1_conv_b_phi, L1_conv_w_g, L1_conv_b_g, L1_conv_w_o, L1_conv_b_o, L1_conv_sigma):
    import jax
    import jax.numpy as jnp

    def _L0_conv_ref(x, ln_g, ln_b, wq, bq, wv, bv, dw_w, dw_b, pw_w, mq_w, mq_b, mk_w, mk_b, mv_w, mv_b, mo_w, mo_b, mlp_w, mlp_b):
        import jax, jax.numpy as jnp
        import numpy as np
        B, H, W, C = (4, 32, 32, 256)
        R, NH, KS = (2, 8, 7)
        S = 1.0

        def layernorm(t, g, b):
            m = t.mean(-1, keepdims=True)
            v = ((t - m) ** 2).mean(-1, keepdims=True)
            return (t - m) / jnp.sqrt(v + 1e-05) * g + b

        def grid_sample_bilinear_zeros(img, grid):
            b, c, h, w = img.shape
            gh, gw = (grid.shape[1], grid.shape[2])
            x = (grid[..., 0] + 1.0) * 0.5 * (w - 1)
            y = (grid[..., 1] + 1.0) * 0.5 * (h - 1)
            x0 = jnp.floor(x)
            y0 = jnp.floor(y)
            wx1 = x - x0
            wy1 = y - y0
            x0i = x0.astype(jnp.int32)
            y0i = y0.astype(jnp.int32)
            flat = img.reshape(b, c, h * w)

            def corner(xi, yi, wt):
                valid = ((xi >= 0) & (xi < w) & (yi >= 0) & (yi < h)).astype(img.dtype)
                idx = jnp.clip(yi, 0, h - 1) * w + jnp.clip(xi, 0, w - 1)
                vals = jnp.take_along_axis(flat, idx.reshape(b, 1, gh * gw), axis=2)
                return vals * (valid * wt).reshape(b, 1, gh * gw)
            out = corner(x0i, y0i, (1 - wx1) * (1 - wy1)) + corner(x0i + 1, y0i, wx1 * (1 - wy1)) + corner(x0i, y0i + 1, (1 - wx1) * wy1) + corner(x0i + 1, y0i + 1, wx1 * wy1)
            return out.reshape(b, c, gh, gw)
        b, h, w, c = x.shape
        x_ln = layernorm(x, ln_g, ln_b).transpose(0, 3, 1, 2)
        x_flat = x_ln.reshape(b, h * w, c)
        q = x_flat @ wq + bq
        q_img = q.reshape(b, c, h, w)
        o = jax.lax.conv_general_dilated(q_img, dw_w, (R, R), [(KS // 2, KS // 2)] * 2, dimension_numbers=('NCHW', 'OIHW', 'NCHW'), feature_group_count=c)
        o = jax.nn.gelu(o + dw_b[None, :, None, None], approximate=False)
        offsets = jax.lax.conv_general_dilated(o, pw_w, (1, 1), [(0, 0), (0, 0)], dimension_numbers=('NCHW', 'OIHW', 'NCHW'))
        hg, wg = (offsets.shape[2], offsets.shape[3])
        ref_x = (jnp.arange(wg, dtype=x.dtype) + 0.5) * (2.0 / wg) - 1.0
        ref_y = (jnp.arange(hg, dtype=x.dtype) + 0.5) * (2.0 / hg) - 1.0
        gx, gy = jnp.meshgrid(ref_x, ref_y, indexing='ij')
        refs = jnp.stack([gx, gy], axis=0)
        deformed = refs[None] + S * jnp.tanh(offsets)
        deformed = (deformed + 1.0) * (h / R) / 2.0
        grid = deformed[:, ::-1].transpose(0, 2, 3, 1)
        interp = grid_sample_bilinear_zeros(x.transpose(0, 3, 1, 2), grid)
        interp_flat = interp.reshape(b, hg * wg, c)
        v = interp_flat @ wv + bv
        k = interp_flat @ wv + bv
        hd = c // NH

        def heads(t):
            return t.reshape(b, -1, NH, hd).transpose(0, 2, 1, 3)
        qh = heads(q @ mq_w + mq_b)
        kh = heads(k @ mk_w + mk_b)
        vh = heads(v @ mv_w + mv_b)
        attn = jax.nn.softmax(jnp.einsum('bnqd,bnkd->bnqk', qh, kh), axis=-1)
        att = jnp.einsum('bnqk,bnkd->bnqd', attn, vh).transpose(0, 2, 1, 3).reshape(b, h * w, c)
        msa = att @ mo_w + mo_b
        z = msa + x.reshape(b, h * w, c)
        z_ln = layernorm(z, ln_g, ln_b)
        out = jax.nn.gelu(z_ln @ mlp_w + mlp_b, approximate=False) + z
        return out.reshape(b, w, h, c)

    def _L1_conv_ref(x, w_theta, b_theta, w_phi, b_phi, w_g, b_g, w_o, b_o, sigma):
        import jax, jax.numpy as jnp
        import numpy as np
        B, H, W, C = (8, 32, 32, 256)

        def maxpool2x2(x):
            b, h, w, c = x.shape
            return x.reshape(b, h // 2, 2, w // 2, 2, c).max(axis=(2, 4))
        b, h, w, c = x.shape
        loc = h * w
        down = loc // 4
        c8, c2 = (c // 8, c // 2)
        theta = (jnp.einsum('bhwc,cd->bhwd', x, w_theta) + b_theta).reshape(b, loc, c8)
        phi = maxpool2x2(jnp.einsum('bhwc,cd->bhwd', x, w_phi) + b_phi).reshape(b, down, c8)
        g = maxpool2x2(jnp.einsum('bhwc,cd->bhwd', x, w_g) + b_g).reshape(b, down, c2)
        attn = jax.nn.softmax(jnp.einsum('bnd,bmd->bnm', theta, phi), axis=-1)
        attn_g = jnp.einsum('bnm,bmd->bnd', attn, g).reshape(b, h, w, c2)
        out = jnp.einsum('bhwd,dc->bhwc', attn_g, w_o) + b_o
        return x + out * sigma

    def _gn(v, G=32, eps=1e-05):
        B_, H_, W_, C_ = v.shape
        g = v.reshape(B_, H_, W_, G, C_ // G)
        m = jnp.mean(g, axis=(1, 2, 4), keepdims=True)
        s = jnp.var(g, axis=(1, 2, 4), keepdims=True)
        return ((g - m) / jnp.sqrt(s + eps)).reshape(v.shape)

    def _ln_c(v, eps=1e-06):
        m = jnp.mean(v, axis=-1, keepdims=True)
        s = jnp.var(v, axis=-1, keepdims=True)
        return (v - m) / jnp.sqrt(s + eps)

    def _ln_t(v, eps=1e-05):
        m = jnp.mean(v, axis=-1, keepdims=True)
        s = jnp.var(v, axis=-1, keepdims=True)
        return (v - m) / jnp.sqrt(s + eps)

    def _to_tokens(v):
        B_, H_, W_, C_ = v.shape
        return v.reshape(B_, H_ * W_, C_)

    def _from_tokens(t, like):
        return t.reshape(like.shape)
    x = _L0_conv_ref(x, L0_conv_ln_g, L0_conv_ln_b, L0_conv_wq, L0_conv_bq, L0_conv_wv, L0_conv_bv, L0_conv_dw_w, L0_conv_dw_b, L0_conv_pw_w, L0_conv_mq_w, L0_conv_mq_b, L0_conv_mk_w, L0_conv_mk_b, L0_conv_mv_w, L0_conv_mv_b, L0_conv_mo_w, L0_conv_mo_b, L0_conv_mlp_w, L0_conv_mlp_b)
    x = _L1_conv_ref(x, L1_conv_w_theta, L1_conv_b_theta, L1_conv_w_phi, L1_conv_b_phi, L1_conv_w_g, L1_conv_b_g, L1_conv_w_o, L1_conv_b_o, L1_conv_sigma)
    return x

_drawn_inputs = setup_inputs


def setup_inputs(seed=0):
    import zlib

    import numpy as np

    out = dict(_drawn_inputs(seed))
    spreads = {'L0_conv_ln_g': (1.0, 0.2),
     'L0_conv_ln_b': (0.0, 0.468),
     'L0_conv_bq': (0.0, 0.8),
     'L0_conv_bv': (0.0, 0.752),
     'L0_conv_dw_b': (0.0, 0.8),
     'L0_conv_mq_b': (0.0, 0.8),
     'L0_conv_mk_b': (0.0, 0.8),
     'L0_conv_mv_b': (0.0, 0.1),
     'L0_conv_mo_b': (0.0, 0.1),
     'L0_conv_mlp_b': (0.0, 0.1),
     'L1_conv_b_theta': (0.0, 0.1),
     'L1_conv_b_phi': (0.0, 0.8),
     'L1_conv_b_g': (0.0, 0.1),
     'L1_conv_b_o': (0.0, 0.1)}
    factors = {'L0_conv_wq': 8.0,
     'L0_conv_wv': 8.0,
     'L0_conv_dw_w': 8.0,
     'L0_conv_pw_w': 8.0,
     'L0_conv_mq_w': 8.0,
     'L0_conv_mk_w': 8.0,
     'L0_conv_mv_w': 5.506}
    for name, (base, spread) in spreads.items():
        noise = np.random.default_rng([zlib.crc32(name.encode()), seed]).standard_normal(out[name].shape)
        drawn = base * np.exp(spread * noise) if base else spread * noise
        out[name] = jnp.asarray(drawn.astype(out[name].dtype))
    for name, factor in factors.items():
        out[name] = (out[name] * factor).astype(out[name].dtype)
    return out
```

```python
from contextlib import ExitStack

import numpy as np

import concourse.bass as bass
from concourse import mybir

F32 = mybir.dt.float32
F32R = mybir.dt.float32r
I32 = mybir.dt.int32
ALU = mybir.AluOpType
ACT = mybir.ActivationFunctionType
AX = mybir.AxisListType

P = 128
B, H, W, C = 4, 32, 32, 256
HW = H * W
NT = HW // P
CB = C // P
R, KS = 2, 7
HG_, WG_ = H // R, W // R
S_ = HG_ * WG_
NH = 8
HD = C // NH
HQ = P // HD
NHG = NH // HQ
NJ = HW // C
C8, C2 = C // 8, C // 2
EPS = 1e-5
PADW = W + 2 * (KS // 2)
PLANE = 20
CROWS = HG_ + 2
UNITS = NHG * NJ
NEWTON = 3
RSQRT_STEPS = 3 + 3 * NEWTON
N_ROWS = 21

K_ID = 0
K_REF = K_ID + P
K_XP = K_REF + 2 * S_
K_YP = K_XP + 1
K_M32 = K_YP + NT
K_N = K_M32 + 32


def shape_constants():
    k = np.zeros((P, K_N), np.float32)
    p = np.arange(P)
    k[:, K_ID:K_ID + P] = np.eye(P)
    ref_x = (np.arange(WG_, dtype=np.float32) + np.float32(0.5)) * np.float32(2.0 / WG_) - np.float32(1.0)
    ref_y = (np.arange(HG_, dtype=np.float32) + np.float32(0.5)) * np.float32(2.0 / HG_) - np.float32(1.0)
    k[:, K_REF:K_REF + S_] = np.repeat(ref_x, HG_)[None]
    k[:, K_REF + S_:K_REF + 2 * S_] = np.tile(ref_y, WG_)[None]
    k[:, K_XP] = -(p % W)
    for t in range(NT):
        k[:, K_YP + t] = -((P // W) * t + p // W)
    k[:, K_M32:K_M32 + 32] = (p[:, None] % 32 == np.arange(32)[None])
    return k


class Signal:

    def __init__(self, sem, per, unit=1, credit=False):
        self.sem, self.per, self.unit = sem, per, unit
        self.start = per * unit if credit else 0

    def at(self, b, n):
        return b * (self.per * self.unit) + (self.start + n * self.unit)

    def before(self, b, n):
        assert self.start and n >= 1
        return b * (self.per * self.unit) + (self.start + (n - self.per) * self.unit)


class Bank:

    def __init__(self, tile, filled, drained, uses):
        self.tile, self.filled, self.drained = tile, filled, drained
        self.uses = {key: n for n, key in enumerate(uses)}
        assert len(self.uses) == len(uses)


    def full(self, b, key):
        return b * len(self.uses) + (self.uses[key] + 1 + len(self.uses))

    def full_before(self, b, key):
        return b * len(self.uses) + (self.uses[key] + 1)

    def empty(self, b, key):
        return b * len(self.uses) + (self.uses[key] + len(self.uses))

    def done(self, b, key):
        return b * len(self.uses) + (self.uses[key] + 1 + len(self.uses))

    def done_before(self, b, key):
        return b * len(self.uses) + (self.uses[key] + 1)


def build(nc, a, out):
    x_rows = a["x"].rearrange("b h w c -> b (h w) c")
    out_rows = out.rearrange("b h w c -> b (h w) c")

    ctx = ExitStack()
    with ctx:
        def sb(name, shape, dt=F32):
            return ctx.enter_context(nc.sbuf_tensor(name, shape, dt))

        def sem(name):
            return ctx.enter_context(nc.semaphore(name))

        consts = sb("consts", [P, K_N])
        ident = consts[:, K_ID:K_ID + P]
        refs = consts[:, K_REF:K_REF + 2 * S_]
        wq = sb("wq", [P, CB, C])
        w_qh = sb("w_qh", [P, CB, C])
        w_kh = sb("w_kh", [P, CB, C])
        w_vh = sb("w_vh", [P, CB, C])
        mo = sb("mo", [P, CB, C])
        mlp = sb("mlp", [P, CB, C])
        w_th = sb("w_th", [P, CB, 3 * C8])
        w_ph = sb("w_ph", [P, CB, 3 * C8])
        w_g = sb("w_g", [P, CB, C2])
        w_o = sb("w_o", [P, C])
        bq_all = sb("bq_all", [P, 2, C])
        lng_all = sb("lng_all", [P, C])
        lnb_all = sb("lnb_all", [P, C])
        mob_all = sb("mob_all", [P, C])
        mlpb_all = sb("mlpb_all", [P, C])
        bo_all = sb("bo_all", [P, C])
        bvh_all = sb("bvh_all", [P, C])
        mvb_all = sb("mvb_all", [P, C])
        cols = sb("cols", [P, 32])
        bq_c, bv_c = cols[:, 0:2], cols[:, 2:4]
        mqb_c, mkb_c = cols[:, 4:6], cols[:, 6:8]
        lng_c, lnb_c, dwb_c = cols[:, 8:10], cols[:, 10:12], cols[:, 12:14]
        pw_c = cols[:, 14:18]
        bth_c, bph_c, bg_c, sg_c = cols[:, 18:19], cols[:, 19:20], cols[:, 20:21], cols[:, 21:22]
        bqh_c, bkh_c = cols[:, 22:24], cols[:, 24:26]
        vec_rows = sb("vec_rows", [N_ROWS, P])
        pw_all = sb("pw_all", [P, CB, 2, P])
        dw_g = sb("dw_g", [P, 8, 2, KS])
        conv_w = sb("conv_w", [P, 8, 2, KS, 32])
        ones = sb("ones", [P, 32])

        xa = sb("xa", [P, NT, C])
        xln = sb("xln", [P, NT, C])
        hat = xln
        qpad = sb("qpad", [P, CB, 2, PLANE, PADW])
        cstack = sb("cstack", [P, 4, CROWS, PADW])
        gel = sb("gel", [P, CB, S_])
        pos = sb("pos", [P, 2, S_])
        hat_x = sb("hat_x", [P, S_])
        samp = sb("samp", [P, CB, C])
        k_hi = sb("k_hi", [P, NHG, S_], F32R)
        k_lo = sb("k_lo", [P, NHG, S_], F32R)
        q_hi = sb("q_hi", [P, HW], F32R)
        q_lo = sb("q_lo", [P, HW], F32R)
        st1 = sb("st1", [P, NT, 6])
        mv1 = sb("mv1", [P, NT, 2])
        rs1 = sb("rs1", [P, 4, NT])
        k_st = sb("k_st", [P, NH, S_], F32R)
        q_st = sb("q_st", [P, NH, HW], F32R)
        vh = sb("vh", [P, 2, C])
        mx = sb("mx", [P, 2, HQ])
        mx_hl = sb("mx_hl", [P, 2, 2, HQ], F32R)
        mx_t = sb("mx_t", [2 * HQ, 2, 2 * P], F32R)
        prob = sb("prob", [P, 2, HQ, 2, S_])
        rden = sb("rden", [P, S_])
        att = sb("att", [P, NHG, HW])
        xb = sb("xb", [P, 2, NJ, C])
        z = sb("z", [P, 2, NJ, C])
        zn = sb("zn", [P, NJ, C])
        mid = zn
        st2 = sb("st2", [P, NT, 6])
        mv2 = sb("mv2", [P, NT, 2])
        rs2 = sb("rs2", [P, 2, 4, NJ])
        zt = sb("zt", [P, CB, HW])
        th_st = sb("th_st", [P, HW], F32R)
        ph_pool = sb("ph_pool", [P, S_])
        ph_st = sb("ph_st", [P, S_], F32R)
        g_pool = sb("g_pool", [P, S_])
        g_m = sb("g_m", [P, 2, C2])
        rd1 = sb("rd1", [P, NT])
        prob1 = prob[:, 0].rearrange("p h m s -> p (h m s)").rearrange("p (m l) -> p m l", m=2)

        ag = prob[:, 1].rearrange("p h m s -> p (h m s)")[:, 0:HW]

        tmp = prob[:].rearrange("p a h m s -> p (a h m s)")
        t_wv, t_mq, t_mk, t_mv, t_wqt, t_wvt = [
            tmp[:, n * 512:(n + 1) * 512].rearrange("p (t c) -> p t c", t=2) for n in range(6)]
        t_bv = tmp[:, 3072:3072 + 256].rearrange("p (t c) -> p t c", t=2)

        ps_s = ctx.enter_context(nc.psum_tensor("ps_s", [P, 4, S_], F32))
        ps_t = ctx.enter_context(nc.psum_tensor("ps_t", [P, 4, S_], F32))
        ps_v = ctx.enter_context(nc.psum_tensor("ps_v", [P, 2, S_], F32))
        ps_d = [ctx.enter_context(nc.psum_tensor(f"ps_d{k}", [P, 2, S_], F32)) for k in range(3)]

        dense = [("qimg", cb, jp) for cb in range(CB) for jp in range(2)]
        dense += [("qh", hg, jp) for hg in range(NHG) for jp in range(2)]
        dense += [("conv", cb) for cb in range(CB)] + [("off",), ("samp",), ("kh",), ("vh",)]
        dense += [("mxt", u) for u in range(UNITS)]
        for cb in range(2):
            dense += [("z", cb, jp) for jp in range(2)] + [("znt", cb, k) for k in range(CB)]
            dense += [("mlp", cb, jp) for jp in range(2)]
        dense += [("yt", cb, k) for cb in range(2) for k in range(CB)]
        dense += [("th", lh) for lh in range(2)] + [("ph", lh) for lh in range(2)]
        dense += [("g", lh) for lh in range(2)] + [("gt",)]
        dense += [("mxt1", lh) for lh in range(2)] + [("ag", lh) for lh in range(2)] + [("den",)]
        dense += [("o", cb, jp) for cb in range(2) for jp in range(2)]
        while len(dense) % 3:
            dense.append(("spare", len(dense)))
        d_banks = [Bank(ps_d[k], sem(f"dense{k}_filled"), sem(f"dense{k}_drained"), dense[k::3]) for k in range(3)]
        d_of = {key: d_banks[n % 3] for n, key in enumerate(dense)}
        s_bank = Bank(ps_s, sem("scores_filled"), sem("scores_drained"),
                      [(u, cb) for u in range(UNITS) for cb in range(2)] + [("l1", lh) for lh in range(2)])
        t_bank = Bank(ps_t, sem("shifted_filled"), sem("shifted_drained"),
                      [(u, pr) for u in range(UNITS) for pr in range(2)] + [("l1", lh) for lh in range(2)])
        v_bank = Bank(ps_v, sem("values_filled"), sem("values_drained"), list(range(UNITS)))
        banks = [*d_banks, s_bank, t_bank, v_bank]

        signals = []

        def signal(name, per, unit=1, credit=False):
            s = Signal(sem(name), per, unit, credit)
            signals.append(s)
            return s

        consts_in = sem("consts_in")
        setup_pe = sem("setup_products")
        setup_dve = sem("setup_copies")
        setup_pool = sem("setup_fills")
        minus_rows = sem("minus_rows")
        xa_in = signal("xa_in", 1, 16)
        xb_in = signal("xb_in", 1, 16)
        xb_biased = signal("xb_biased", 1, credit=True)
        ln1_stat = signal("ln1_stat", NT, credit=True)
        ln1_aggr = signal("ln1_aggr", NT)
        rsqrt1 = signal("rsqrt1", RSQRT_STEPS, credit=True)
        ln1_norm = signal("ln1_norm", NT)
        ln1_scaled = signal("ln1_scaled", 2)
        xln_ready = signal("xln_ready", 2, credit=True)
        conv_in = [signal(f"conv_in{cb}", 16, 16) for cb in range(CB)]
        gel_done = signal("gel_done", CB)
        tanh_done = signal("tanh_done", 1)
        pos_step = signal("pos_step", 3)
        hat_dist = signal("hat_dist", 1 + NT)
        hat_relu = signal("hat_relu", 2)
        hat_done = signal("hat_done", 1)
        k_hi_done = signal("k_hi_done", 1)
        k_in = signal("k_in", 3 * NH, 16, credit=True)
        q_hi_done = signal("q_hi_done", NHG * 2)
        q_in = [signal(f"q_in{hg}", 3 * HQ, 16, credit=True) for hg in range(NHG)]
        max_hi = signal("max_hi", UNITS)
        max_split = signal("max_split", UNITS, credit=True)
        max_in = [signal(f"max_in{k}", UNITS // 2, 16, credit=True) for k in range(2)]
        rden_done = signal("rden_done", UNITS)
        ln2_stat = signal("ln2_stat", NT, credit=True)
        ln2_aggr = signal("ln2_aggr", NT)
        rsqrt2 = signal("rsqrt2", 2 * RSQRT_STEPS, credit=True)
        zn_done = signal("zn_done", NT)
        gelu_done = signal("mlp_gelu", 4)
        y_done = signal("y_done", 2)
        ybo_done = signal("ybo_done", 2)
        th_hi = signal("th_hi", 2)
        ph_step = signal("ph_step", 3)
        g_bias = signal("g_bias", 1)
        max1_hi = signal("max1_hi", 2)
        max1_split = signal("max1_split", 2, credit=True)
        max1_in = [signal(f"max1_in{k}", 1, 16) for k in range(2)]
        rd1_step = signal("rd1_step", 1)
        out_stored = signal("out_stored", 1, 16, credit=True)

        N_CONST_IN = 0
        const_dmas = []

        def row2(at, src):
            const_dmas.append((vec_rows[at:at + 2, :], src.rearrange("(t p) -> t p", p=P)))

        def whole(dst, src):
            const_dmas.append((dst, src.rearrange("(a c) -> a c", a=1).broadcast_to([P, C])))

        def mat(dst, src):
            const_dmas.append((dst, src.rearrange("(t p) c -> p t c", p=P)))

        const_dmas.append((consts[:], a["shape_constants"]))
        mat(wq[:], a["L0_conv_wq"])
        mat(t_mq, a["L0_conv_mq_w"])
        mat(t_wv, a["L0_conv_wv"])
        mat(t_mk, a["L0_conv_mk_w"])
        mat(t_mv, a["L0_conv_mv_w"])
        row2(0, a["L0_conv_bq"])
        row2(2, a["L0_conv_bv"])
        row2(4, a["L0_conv_mq_b"])
        row2(6, a["L0_conv_mk_b"])
        row2(8, a["L0_conv_ln_g"])
        row2(10, a["L0_conv_ln_b"])
        row2(12, a["L0_conv_dw_b"])
        whole(lng_all[:], a["L0_conv_ln_g"])
        whole(lnb_all[:], a["L0_conv_ln_b"])
        whole(bq_all[:, 0, :], a["L0_conv_bq"])
        whole(bq_all[:, 1, :], a["L0_conv_bq"])
        whole(mvb_all[:], a["L0_conv_mv_b"])
        for o in range(2):
            for t in range(CB):
                const_dmas.append((vec_rows[14 + 2 * t + o:15 + 2 * t + o, :],
                                   a["L0_conv_pw_w"][o, t * P:(t + 1) * P].rearrange("p h w -> (h w) p")))
        dw = a["L0_conv_dw_w"].rearrange("(k c) o h w -> c k (o h) w", c=32)
        for g in range(4):
            for hi in range(2):
                if g + 4 * hi < KS:
                    const_dmas.append((dw_g[32 * g:32 * g + 32, :, hi, :], dw[:, :, g + 4 * hi, :]))
        mat(mo[:], a["L0_conv_mo_w"])
        mat(mlp[:], a["L0_conv_mlp_w"])
        whole(mob_all[:], a["L0_conv_mo_b"])
        whole(mlpb_all[:], a["L0_conv_mlp_b"])
        for n in range(3):
            mat(w_th[:, :, n * C8:(n + 1) * C8], a["L1_conv_w_theta"])
            mat(w_ph[:, :, n * C8:(n + 1) * C8], a["L1_conv_w_phi"])
            for at, name in ((18, "L1_conv_b_theta"), (19, "L1_conv_b_phi")):
                const_dmas.append((vec_rows[at:at + 1, n * C8:(n + 1) * C8], a[name].rearrange("(a p) -> a p", a=1)))
        mat(w_g[:], a["L1_conv_w_g"])
        const_dmas.append((vec_rows[20:21, :], a["L1_conv_b_g"].rearrange("(a p) -> a p", a=1)))
        const_dmas.append((w_o[:], a["L1_conv_w_o"]))
        whole(bo_all[:], a["L1_conv_b_o"])
        const_dmas.append((sg_c, a["L1_conv_sigma"].rearrange("(a c) -> a c", a=1).broadcast_to([P, 1])))
        N_CONST_IN = 16 * len(const_dmas)

        gates = {n: sem(f"gate_{n}") for n in ("sp", "dve", "pool")}

        def gate(eng, name):
            eng.sem_inc(gates[name], 1)

        def over_rows(row, n):
            return row[:].rearrange("p (a c) -> p a c", a=1).broadcast_to([P, n, C])

        block = ctx.enter_context(nc.Block())

        @block.sync
        def _(sp):
            for s in signals:
                if s.start:
                    sp.sem_inc(s.sem, s.start)
            for k in banks:
                sp.sem_inc(k.filled, len(k.uses))
                sp.sem_inc(k.drained, len(k.uses))
            for dst, src in const_dmas:
                if dst.tensor.name in ("dw_g", "vec_rows"):
                    sp.wait_ge(setup_pool, 2)
                sp.dma_start(dst, src).then_inc(consts_in, 16)

            with sp.Fori(0, B) as b:
                sp.wait_ge(xln_ready.sem, xln_ready.before(b, 2))
                k = d_of["samp",]
                sp.wait_ge(k.drained, k.done_before(b, ("samp",)))
                sp.dma_start(xa[:], x_rows[b].rearrange("(t p) c -> p t c", p=P)).then_inc(xa_in.sem, 16)
                sp.wait_ge(out_stored.sem, out_stored.before(b, 1))
                sp.dma_start(xb[:], x_rows[b].rearrange("(k p j) c -> p k j c", k=2, j=NJ)).then_inc(xb_in.sem, 16)
                for hg in range(NHG):
                    k = d_of["qh", hg, 1]
                    sp.wait_ge(k.drained, k.done(b, ("qh", hg, 1)))
                    for h in range(HQ):
                        for row, src in ((0, q_hi), (1, q_lo), (2, q_hi)):
                            sp.dma_start(q_st[32 * row:32 * row + 32, hg * HQ + h, :].bitcast(F32),
                                         src[32 * h:32 * h + 32, :].bitcast(F32)).then_inc(q_in[hg].sem, 16)
                for cb in range(CB):
                    k = d_of["qimg", cb, 1]
                    sp.wait_ge(k.drained, k.done(b, ("qimg", cb, 1)))
                    if cb:
                        k = d_of["conv", cb - 1]
                        sp.wait_ge(k.filled, k.full(b, ("conv", cb - 1)))
                    for c4 in range(4):
                        for g in range(4):
                            r0 = g // 2 + g % 2
                            sp.dma_start(cstack[32 * g:32 * g + 32, c4, :, :],
                                         qpad[32 * c4:32 * c4 + 32, cb, 1 - g % 2, r0:r0 + CROWS, :]
                                         ).then_inc(conv_in[cb].sem, 16)
                k = d_of["kh",]
                sp.wait_ge(k.drained, k.done(b, ("kh",)))
                for h in range(NH):
                    for row, src in ((0, k_hi), (1, k_hi), (2, k_lo)):
                        sp.dma_start(k_st[32 * row:32 * row + 32, h, :].bitcast(F32),
                                     src[32 * (h % HQ):32 * (h % HQ) + 32, h // HQ, :].bitcast(F32)
                                     ).then_inc(k_in.sem, 16)
                for u in range(UNITS):
                    hg, j = divmod(u, NJ)
                    k = d_of["mxt", u]
                    sp.wait_ge(k.drained, k.done(b, ("mxt", u)))
                    sp.dma_start(q_st[96:98, hg * HQ:(hg + 1) * HQ, j * S_:(j + 1) * S_].bitcast(F32),
                                 mx_t[:, u % 2, :].bitcast(F32)).then_inc(max_in[u % 2].sem, 16)
                for lh in range(2):
                    k = d_of["mxt1", lh]
                    sp.wait_ge(k.drained, k.done(b, ("mxt1", lh)))
                    sp.dma_start(th_st[96:98, lh * 512:(lh + 1) * 512].bitcast(F32),
                                 mx_t[:, lh, 0:P].bitcast(F32)).then_inc(max1_in[lh].sem, 16)
                for cb in range(2):
                    for jp in range(2):
                        k = d_of["o", cb, jp]
                        sp.wait_ge(k.drained, k.done(b, ("o", cb, jp)))
                        gate(sp, "sp")
                sp.dma_start(out_rows[b].rearrange("(k p j) c -> p k j c", k=2, j=NJ), z[:]).then_inc(out_stored.sem, 16)
            sp.wait_ge(out_stored.sem, out_stored.at(B - 1, 1))

        @block.tensor
        def _(pe):
            pe.wait_ge(consts_in, N_CONST_IN)
            for n, (w, ps) in enumerate(((wq, ps_d[0]), (t_wv, ps_d[1]))):
                for nt in range(2):
                    for kt in range(2):
                        ins = pe.transpose(ps[:, nt, kt * P:(kt + 1) * P], w[:, kt, nt * P:(nt + 1) * P], ident)
                ins.then_inc(setup_pe, 1)
            pe.transpose(ps_d[2][:, 0, 0:N_ROWS], vec_rows[:], ident[0:N_ROWS, 0:N_ROWS]).then_inc(setup_pe, 1)
            for n, (wt, m, ps) in enumerate(((t_wqt, t_mq, ps_s[:, 0:2, :]), (t_wvt, t_mk, ps_s[:, 2:4, :]),
                                             (t_wvt, t_mv, ps_t[:, 0:2, :]))):
                pe.wait_ge(setup_dve, 2 if n else 1)
                for kt in range(2):
                    for nt in range(2):
                        ins = pe.matmul(ps[:, kt, :], wt[:, nt, kt * P:(kt + 1) * P], m[:, nt, :],
                                        start=nt == 0, stop=nt == 1)
                ins.then_inc(setup_pe, 1)
            pe.wait_ge(setup_dve, 3)
            for n, (m, bc) in enumerate(((t_mq, bq_c), (t_mk, bv_c))):
                for mb in range(2):
                    for nt in range(2):
                        ins = pe.matmul(ps_v[:, 0, 2 * n + mb:2 * n + mb + 1], m[:, nt, mb * P:(mb + 1) * P],
                                        bc[:, nt:nt + 1], start=nt == 0, stop=nt == 1)
            ins.then_inc(setup_pe, 1)
            pe.wait_ge(setup_pool, 6)
            pe.wait_ge(setup_dve, 6)
            for nt in range(2):
                ins = pe.matmul(ps_t[:, 2, :], t_bv[:, nt, :], t_mv[:, nt, :], start=nt == 0, stop=nt == 1)
            ins.then_inc(setup_pe, 1)
            pe.wait_ge(setup_dve, 9)
            pe.wait_ge(setup_pool, 7)
            pe.wait_ge(minus_rows, 2)

            def open_bank(key, b):
                bank = d_of[key]
                pe.wait_ge(bank.drained, bank.empty(b, key))
                return bank.tile

            def close_bank(key, ins):
                ins.then_inc(d_of[key].filled, 1)

            def front(b):
                for cb in range(CB):
                    for jp in range(2):
                        ps = open_bank(("qimg", cb, jp), b)
                        for jj in range(2):
                            for kt in range(2):
                                t = 4 * jp + 2 * jj + kt
                                if cb == 0 and t % NJ == 0:
                                    pe.wait_ge(xln_ready.sem, xln_ready.at(b, t // NJ + 1))
                                ins = pe.matmul(ps[:, jj, :], xln[:, t, cb * P:(cb + 1) * P], wq[:, kt, :],
                                                start=kt == 0, stop=kt == 1)
                        close_bank(("qimg", cb, jp), ins)
                for hg in range(NHG):
                    for jp in range(2):
                        ps = open_bank(("qh", hg, jp), b)
                        for jj in range(2):
                            for kt in range(2):
                                ins = pe.matmul(ps[:, jj, :], w_qh[:, kt, hg * P:(hg + 1) * P],
                                                xln[:, 4 * jp + 2 * jj + kt, :], start=kt == 0, stop=kt == 1)
                        close_bank(("qh", hg, jp), ins)
                for cb in range(CB):
                    ps = open_bank(("conv", cb), b)
                    pe.wait_ge(conv_in[cb].sem, conv_in[cb].at(b, 16))
                    for hi in range(2):
                        for dx in range(KS):
                            for c4 in range(4):
                                ins = pe.matmul(
                                    ps[32 * c4:32 * c4 + 32, 0, :], conv_w[:, cb * 4 + c4, hi, dx, :],
                                    cstack[:, c4, 2 * hi:2 * hi + HG_, dx:dx + 2 * WG_ - 1:2],
                                    start=hi == 0 and dx == 0, stop=hi == 1 and dx == KS - 1)
                    close_bank(("conv", cb), ins)
                ps = open_bank(("off",), b)
                for o in range(2):
                    for kt in range(CB):
                        pe.wait_ge(gel_done.sem, gel_done.at(b, kt + 1))
                        ins = pe.matmul(ps[:, o, :], pw_all[:, kt, o, :], gel[:, kt, :], start=kt == 0, stop=kt == 1)
                close_bank(("off",), ins)
                ps = open_bank(("samp",), b)
                pe.wait_ge(hat_done.sem, hat_done.at(b, 1))
                for st in range(2):
                    for t in range(NT):
                        ins = pe.matmul(ps[:, st, :], hat[:, t, st * P:(st + 1) * P], xa[:, t, :],
                                        start=t == 0, stop=t == NT - 1)
                close_bank(("samp",), ins)
                ps = open_bank(("kh",), b)
                k = d_of["samp",]
                pe.wait_ge(k.drained, k.done(b, ("samp",)))
                for hg in range(NHG):
                    for st in range(2):
                        ins = pe.matmul(ps[:, hg, :], w_kh[:, st, hg * P:(hg + 1) * P], samp[:, st, :],
                                        start=st == 0, stop=st == 1)
                close_bank(("kh",), ins)
                ps = open_bank(("vh",), b)
                for rb in range(2):
                    for st in range(2):
                        ins = pe.matmul(ps[:, rb, :], samp[:, st, rb * P:(rb + 1) * P], w_vh[:, st, :],
                                        start=st == 0, stop=st == 1)
                close_bank(("vh",), ins)

            def scores(b, u):
                hg, j = divmod(u, NJ)
                if u == 0:
                    pe.wait_ge(k_in.sem, k_in.at(b, 3 * NH))
                if j == 0:
                    pe.wait_ge(q_in[hg].sem, q_in[hg].at(b, 3 * HQ))
                for cb in range(2):
                    pe.wait_ge(s_bank.drained, s_bank.empty(b, (u, cb)))
                    for h in range(HQ):
                        ins = pe.matmul(ps_s[:, h, :], q_st[0:96, hg * HQ + h, j * S_ + cb * P:j * S_ + (cb + 1) * P],
                                        k_st[0:96, hg * HQ + h, :], start=True, stop=True)
                    ins.then_inc(s_bank.filled, 1)

            def max_rows(b, u):
                ps = open_bank(("mxt", u), b)
                pe.wait_ge(max_split.sem, max_split.at(b, u + 1))
                for cb in range(2):
                    ins = pe.transpose(ps[0:2 * HQ, 0, cb * P:(cb + 1) * P],
                                       mx_hl[:, cb].rearrange("p a h -> p (a h)").bitcast(F32), ident)
                close_bank(("mxt", u), ins)

            def shifted(b, u, pr):
                hg, j = divmod(u, NJ)
                if pr == 0:
                    pe.wait_ge(max_in[u % 2].sem, max_in[u % 2].at(b, u // 2 + 1))
                pe.wait_ge(t_bank.drained, t_bank.empty(b, (u, pr)))
                for hh in range(2):
                    h = 2 * pr + hh
                    for mt in range(2):
                        ins = pe.matmul(ps_t[:, 2 * hh + mt, :], k_st[0:98, hg * HQ + h, mt * P:(mt + 1) * P],
                                        q_st[0:98, hg * HQ + h, j * S_:(j + 1) * S_], start=True, stop=True)
                ins.then_inc(t_bank.filled, 1)

            def values(b, u):
                hg = u // NJ
                pe.wait_ge(t_bank.drained, t_bank.done(b, (u, 1)))
                pe.wait_ge(v_bank.drained, v_bank.empty(b, u))
                if u == 0:
                    k = d_of["vh",]
                    pe.wait_ge(k.drained, k.done(b, ("vh",)))
                for den in range(2):
                    for mt in range(2):
                        for h in range(HQ):
                            hh = hg * HQ + h
                            wt = ones[:] if den else vh[:, mt, hh * HD:(hh + 1) * HD]
                            ins = pe.matmul(ps_v[32 * h:32 * h + 32, den, :], wt, prob[:, u % 2, h, mt, :],
                                            start=mt == 0, stop=mt == 1)
                ins.then_inc(v_bank.filled, 1)

            def attn(b):
                for s in range(UNITS + 3):
                    if s < UNITS:
                        scores(b, s)
                    if 1 <= s <= UNITS:
                        max_rows(b, s - 1)
                    if 2 <= s <= UNITS + 1:
                        shifted(b, s - 2, 0)
                    if s >= 3:
                        values(b, s - 3)
                    if 2 <= s <= UNITS + 1:
                        shifted(b, s - 2, 1)

            def post(b):
                for cb in range(2):
                    for jp in range(2):
                        ps = open_bank(("z", cb, jp), b)
                        pe.wait_ge(v_bank.drained, v_bank.done(b, UNITS - 1))
                        for jj in range(2):
                            j = 2 * jp + jj
                            for hg in range(NHG):
                                ins = pe.matmul(ps[:, jj, :], att[:, hg, j * S_ + cb * P:j * S_ + (cb + 1) * P],
                                                mo[:, hg, :], start=hg == 0, stop=hg == 1)
                        close_bank(("z", cb, jp), ins)
                    for kt in range(CB):
                        ps = open_bank(("znt", cb, kt), b)
                        for j in range(NJ):
                            if kt == 0:
                                pe.wait_ge(zn_done.sem, zn_done.at(b, cb * NJ + j + 1))
                            ins = pe.transpose(ps[:, j // 2, (j % 2) * P:(j % 2 + 1) * P],
                                               zn[:, j, kt * P:(kt + 1) * P], ident)
                        close_bank(("znt", cb, kt), ins)
                    for jp in range(2):
                        ps = open_bank(("mlp", cb, jp), b)
                        for jj in range(2):
                            j = 2 * jp + jj
                            for kt in range(CB):
                                k = d_of["znt", cb, kt]
                                if j == 0:
                                    pe.wait_ge(k.drained, k.done(b, ("znt", cb, kt)))
                                ins = pe.matmul(ps[:, jj, :], zt[:, kt, cb * 512 + j * P:cb * 512 + (j + 1) * P],
                                                mlp[:, kt, :], start=kt == 0, stop=kt == 1)
                        close_bank(("mlp", cb, jp), ins)
                for cb in range(2):
                    for kt in range(CB):
                        ps = open_bank(("yt", cb, kt), b)
                        pe.wait_ge(y_done.sem, y_done.at(b, cb + 1))
                        for j in range(NJ):
                            ins = pe.transpose(ps[:, j // 2, (j % 2) * P:(j % 2 + 1) * P],
                                               z[:, cb, j, kt * P:(kt + 1) * P], ident)
                        close_bank(("yt", cb, kt), ins)
                for name, w, m in (("th", w_th, 3 * C8), ("ph", w_ph, 3 * C8), ("g", w_g, C2)):
                    for lh in range(2):
                        ps = open_bank((name, lh), b)
                        for kt in range(CB):
                            k = d_of["yt", lh, kt]
                            pe.wait_ge(k.drained, k.done(b, ("yt", lh, kt)))
                            ins = pe.matmul(ps[0:m].rearrange("p a s -> p (a s)"), w[:, kt, :],
                                            zt[:, kt, lh * 512:(lh + 1) * 512], start=kt == 0, stop=kt == 1)
                        close_bank((name, lh), ins)
                ps = open_bank(("gt",), b)
                pe.wait_ge(g_bias.sem, g_bias.at(b, 1))
                for mt in range(2):
                    ins = pe.transpose(ps[:, 0, mt * P:(mt + 1) * P], g_pool[:, mt * P:(mt + 1) * P], ident)
                close_bank(("gt",), ins)
                pe.wait_ge(ph_step.sem, ph_step.at(b, 3))
                k = d_of["th", 1]
                pe.wait_ge(k.drained, k.done(b, ("th", 1)))
                k = d_of["th", 0]
                pe.wait_ge(k.drained, k.done(b, ("th", 0)))
                for lh in range(2):
                    pe.wait_ge(s_bank.drained, s_bank.empty(b, ("l1", lh)))
                    for n in range(4):
                        ins = pe.matmul(ps_s[:, n, :], th_st[0:96, lh * 512 + n * P:lh * 512 + (n + 1) * P],
                                        ph_st[0:96, :], start=True, stop=True)
                    ins.then_inc(s_bank.filled, 1)
                for lh in range(2):
                    ps = open_bank(("mxt1", lh), b)
                    pe.wait_ge(max1_split.sem, max1_split.at(b, lh + 1))
                    ins = pe.transpose(ps[0:8, 0, 0:P], mx_hl[:, lh].rearrange("p a h -> p (a h)").bitcast(F32), ident)
                    close_bank(("mxt1", lh), ins)
                for lh in range(2):
                    pe.wait_ge(max1_in[lh].sem, max1_in[lh].at(b, 1))
                    pe.wait_ge(t_bank.drained, t_bank.empty(b, ("l1", lh)))
                    for mt in range(2):
                        ins = pe.matmul(ps_t[:, 2 * mt:2 * mt + 2, :].rearrange("p a s -> p (a s)"),
                                        ph_st[0:98, mt * P:(mt + 1) * P], th_st[0:98, lh * 512:(lh + 1) * 512],
                                        start=True, stop=True)
                    ins.then_inc(t_bank.filled, 1)
                for lh in range(2):
                    ps = open_bank(("ag", lh), b)
                    pe.wait_ge(t_bank.drained, t_bank.done(b, ("l1", lh)))
                    if lh == 0:
                        k = d_of["gt",]
                        pe.wait_ge(k.drained, k.done(b, ("gt",)))
                    for mt in range(2):
                        ins = pe.matmul(ps[:].rearrange("p a s -> p (a s)"), g_m[:, mt, :],
                                        prob1[:, mt, lh * 512:(lh + 1) * 512], start=mt == 0, stop=mt == 1)
                    close_bank(("ag", lh), ins)
                ps = open_bank(("den",), b)
                for cb in range(2):
                    for j in range(NJ):
                        n = cb * NJ + j
                        for mt in range(2):
                            ins = pe.matmul(ps[:, 0, n:n + 1], prob1[:, mt, cb * 512 + j:cb * 512 + j + 4 * P - 3:4],
                                            ones[:, 0:1], start=mt == 0, stop=mt == 1)
                close_bank(("den",), ins)
                for cb in range(2):
                    for jp in range(2):
                        ps = open_bank(("o", cb, jp), b)
                        k = d_of["ag", cb]
                        pe.wait_ge(k.drained, k.done(b, ("ag", cb)))
                        for jj in range(2):
                            j = 2 * jp + jj
                            ins = pe.matmul(ps[:, jj, :], ag[:, cb * 512 + j:cb * 512 + j + 4 * P - 3:4], w_o[:],
                                            start=True, stop=True)
                        close_bank(("o", cb, jp), ins)
                for key in dense:
                    if key[0] == "spare":
                        ps = open_bank(key, b)
                        ins = pe.transpose(ps[0:1, 0, 0:P], ones[:, 0:1], ident)
                        close_bank(key, ins)

            with pe.Fori(0, B) as b:
                front(b)
                attn(b)
                post(b)

        def drain(ins, key):
            ins.then_inc(d_of[key].drained, 1)

        def await_bank(eng, key, b):
            eng.wait_ge(d_of[key].filled, d_of[key].full(b, key))
            return d_of[key].tile

        @block.scalar
        def _(act):
            act.wait_ge(consts_in, N_CONST_IN)
            act.wait_ge(setup_dve, 9)

            def front(b):
                for hg in range(NHG):
                    if hg:
                        act.wait_ge(q_in[0].sem, q_in[0].at(b, 3 * HQ))
                    else:
                        act.wait_ge(q_in[1].sem, q_in[1].before(b, 3 * HQ))
                    for jp in range(2):
                        ps = await_bank(act, ("qh", hg, jp), b)
                        act.activation(q_hi[:, jp * 512:(jp + 1) * 512], ps[:].rearrange("p a s -> p (a s)"),
                                       ACT.Identity, bias=bqh_c[:, hg:hg + 1]).then_inc(q_hi_done.sem, 1)
                for cb in range(CB):
                    ps = await_bank(act, ("conv", cb), b)
                    drain(act.activation(gel[:, cb, :], ps[:, 0, :], ACT.Gelu, bias=dwb_c[:, cb:cb + 1]), ("conv", cb))
                for cb in range(CB):
                    k = d_of["conv", cb]
                    act.wait_ge(k.drained, k.done(b, ("conv", cb)))
                    act.sem_inc(gel_done.sem, 1)
                ps = await_bank(act, ("off",), b)
                drain(act.activation(pos[:].rearrange("p a s -> p (a s)"), ps[:].rearrange("p a s -> p (a s)"),
                                     ACT.Tanh), ("off",))
                act.wait_ge(pos_step.sem, pos_step.at(b, 3))
                act.activation(hat_x[:], pos[:, 1, :], ACT.Abs, bias=consts[:, K_XP:K_XP + 1]).then_inc(hat_dist.sem, 1)
                k = d_of["qh", 1, 1]
                act.wait_ge(k.filled, k.full(b, ("qh", 1, 1)))
                for t in range(NT):
                    act.activation(hat[:, t, :], pos[:, 0, :], ACT.Abs,
                                   bias=consts[:, K_YP + t:K_YP + t + 1]).then_inc(hat_dist.sem, 1)
                act.wait_ge(hat_dist.sem, hat_dist.at(b, 1))
                act.activation(hat_x[:], hat_x[:], ACT.Relu, bias=1.0, scale=-1.0).then_inc(hat_relu.sem, 1)
                act.wait_ge(hat_dist.sem, hat_dist.at(b, 1 + NT))
                act.activation(hat[:], hat[:], ACT.Relu, bias=1.0, scale=-1.0).then_inc(hat_relu.sem, 1)
                ps = await_bank(act, ("samp",), b)
                drain(act.activation(samp[:], ps[:], ACT.Copy), ("samp",))
                act.wait_ge(k_in.sem, k_in.before(b, 3 * NH))
                ps = await_bank(act, ("kh",), b)
                for hg in range(NHG):
                    ins = act.activation(k_hi[:, hg, :], ps[:, hg, :], ACT.Identity, bias=bkh_c[:, hg:hg + 1])
                ins.then_inc(k_hi_done.sem, 1)

            def max_out(b, u):
                ps = await_bank(act, ("mxt", u), b)
                if u >= 2:
                    act.wait_ge(max_in[u % 2].sem, max_in[u % 2].at(b, u // 2))
                else:
                    act.wait_ge(max_in[u % 2].sem, max_in[u % 2].before(b, UNITS // 2))
                drain(act.activation(mx_t[:, u % 2, :], ps[0:2 * HQ, 0, :], ACT.Copy), ("mxt", u))

            def exps(b, u):
                for pr in range(2):
                    act.wait_ge(t_bank.filled, t_bank.full(b, (u, pr)))
                    if u < 2 and pr == 0:
                        act.wait_ge(d_of["o", 1, 1].filled, d_of["o", 1, 1].full_before(b, ("o", 1, 1)))
                    if u >= 2 and pr == 0:
                        act.wait_ge(v_bank.filled, v_bank.full(b, u - 2))
                    act.activation(prob[:, u % 2, 2 * pr:2 * pr + 2].rearrange("p h m s -> p (h m) s"), ps_t[:],
                                   ACT.Exp).then_inc(t_bank.drained, 1)

            def attn(b):
                for s in range(UNITS + 3):
                    if 1 <= s <= UNITS:
                        max_out(b, s - 1)
                    if 2 <= s <= UNITS + 1:
                        exps(b, s - 2)

            def post(b):
                for cb in range(2):
                    for kt in range(CB):
                        ps = await_bank(act, ("znt", cb, kt), b)
                        drain(act.activation(zt[:, kt, cb * 512:(cb + 1) * 512], ps[:].rearrange("p a s -> p (a s)"),
                                             ACT.Identity, bias=lnb_c[:, kt:kt + 1], scale=lng_c[:, kt:kt + 1]),
                              ("znt", cb, kt))
                    for jp in range(2):
                        k = d_of["mlp", cb, jp]
                        act.wait_ge(k.drained, k.done(b, ("mlp", cb, jp)))
                        act.activation(mid[:, 2 * jp:2 * jp + 2, :], mid[:, 2 * jp:2 * jp + 2, :],
                                       ACT.Gelu).then_inc(gelu_done.sem, 1)
                for cb in range(2):
                    for kt in range(CB):
                        ps = await_bank(act, ("yt", cb, kt), b)
                        act.wait_ge(d_of["mlp", 1, 1].filled, d_of["mlp", 1, 1].full(b, ("mlp", 1, 1)))
                        drain(act.activation(
                            zt[:, kt, cb * 512:(cb + 1) * 512].rearrange("p (q j) -> p j q", j=NJ),
                            ps[:].rearrange("p a (c q) -> p (a c) q", c=2), ACT.Copy), ("yt", cb, kt))
                for lh in range(2):
                    ps = await_bank(act, ("th", lh), b)
                    act.activation(th_st[0:96, lh * 512:(lh + 1) * 512], ps[0:96].rearrange("p a s -> p (a s)"),
                                   ACT.Identity, bias=bth_c[0:96]).then_inc(th_hi.sem, 1)
                ps = await_bank(act, ("gt",), b)
                drain(act.activation(g_m[:], ps[:, 0, :].rearrange("p (m d) -> p m d", m=2), ACT.Copy), ("gt",))
                for lh in range(2):
                    ps = await_bank(act, ("mxt1", lh), b)
                    act.wait_ge(max_in[lh].sem, max_in[lh].at(b, UNITS // 2))
                    drain(act.activation(mx_t[:, lh, 0:P], ps[0:8, 0, 0:P], ACT.Copy), ("mxt1", lh))
                for lh in range(2):
                    act.wait_ge(t_bank.filled, t_bank.full(b, ("l1", lh)))
                    act.wait_ge(v_bank.filled, v_bank.full(b, UNITS - 1))
                    act.activation(prob1[:, :, lh * 512:(lh + 1) * 512],
                                   ps_t[:].rearrange("p (m a) s -> p m (a s)", m=2), ACT.Exp
                                   ).then_inc(t_bank.drained, 1)
                for lh in range(2):
                    ps = await_bank(act, ("ag", lh), b)
                    drain(act.activation(ag[:, lh * 512:(lh + 1) * 512], ps[:].rearrange("p a s -> p (a s)"),
                                         ACT.Copy), ("ag", lh))

            with act.Fori(0, B) as b:
                front(b)
                attn(b)
                post(b)

        @block.vector
        def _(dve):
            dve.memset(k_st[96:98, :, :].bitcast(F32), -1.0).then_inc(minus_rows, 1)
            dve.memset(ph_st[96:98, :].bitcast(F32), -1.0).then_inc(minus_rows, 1)
            dve.wait_ge(consts_in, N_CONST_IN)
            for n, (dst, ps) in enumerate(((t_wqt, ps_d[0]), (t_wvt, ps_d[1]),
                                           (cols[:, 0:N_ROWS], ps_d[2][:, 0, 0:N_ROWS]), (w_qh, ps_s[:, 0:2, :]),
                                           (w_kh, ps_s[:, 2:4, :]), (w_vh, ps_t[:, 0:2, :]))):
                dve.wait_ge(setup_pe, n + 1)
                dve.tensor_copy(dst[:], ps[:]).then_inc(setup_dve, 1)
            dve.wait_ge(setup_pe, 7)
            dve.tensor_tensor(bqh_c, ps_v[:, 0, 0:2], mqb_c, ALU.add).then_inc(setup_dve, 1)
            dve.tensor_tensor(bkh_c, ps_v[:, 0, 2:4], mkb_c, ALU.add).then_inc(setup_dve, 1)
            dve.wait_ge(setup_pe, 8)
            dve.tensor_tensor(bvh_all[:], ps_t[:, 2, :], mvb_all[:], ALU.add).then_inc(setup_dve, 1)

            def rsqrt(sig, b, first, var, w):
                half, y, t, v = w[:, 0], w[:, 1], w[:, 2], w[:, 3]
                n = [first]

                def step(ins):
                    ins.then_inc(sig.sem, 1)
                    n[0] += 1
                    dve.wait_ge(sig.sem, sig.at(b, n[0]))

                step(dve.tensor_scalar(v, var, EPS, None, ALU.add))
                step(dve.tensor_scalar(t.bitcast(I32), v.bitcast(I32), 1, None, ALU.logical_shift_right))
                step(dve.tensor_scalar(y.bitcast(I32), t.bitcast(I32), -1.0, float(0x5F3759DF), ALU.mult, ALU.add))
                for _ in range(NEWTON):
                    step(dve.tensor_tensor(t, y, y, ALU.mult))
                    step(dve.scalar_tensor_tensor(t, t, -0.5, v, ALU.mult, ALU.mult))
                    step(dve.scalar_tensor_tensor(y, t, 1.5, y, ALU.add, ALU.mult))

            def front(b):
                dve.wait_ge(xa_in.sem, xa_in.at(b, 1))
                dve.wait_ge(xln_ready.sem, xln_ready.before(b, 2))
                for t in range(NT):
                    dve.bn_stats(st1[:, t, :], xa[:, t, :]).then_inc(ln1_stat.sem, 1)
                dve.wait_ge(ln1_stat.sem, ln1_stat.at(b, NT))
                gate(dve, "dve")
                for t in range(NT):
                    dve.bn_aggr(mv1[:, t, :], st1[:, t, :]).then_inc(ln1_aggr.sem, 1)
                dve.wait_ge(ln1_aggr.sem, ln1_aggr.at(b, NT))
                rsqrt(rsqrt1, b, 0, mv1[:, :, 1], rs1)
                for half in range(2):
                    part = xln[:, half * NJ:(half + 1) * NJ, :]
                    dve.wait_ge(ln1_norm.sem, ln1_norm.at(b, (half + 1) * NJ))
                    dve.tensor_tensor(part, part, over_rows(lng_all, NJ), ALU.mult).then_inc(ln1_scaled.sem, 1)
                    dve.wait_ge(ln1_scaled.sem, ln1_scaled.at(b, half + 1))
                    dve.tensor_tensor(part, part, over_rows(lnb_all, NJ), ALU.add).then_inc(xln_ready.sem, 1)
                for cb in range(CB):
                    for jp in range(2):
                        ps = await_bank(dve, ("qimg", cb, jp), b)
                        if jp == 0:
                            dve.wait_ge(d_of["conv", 1].drained, d_of["conv", 1].done_before(b, ("conv", 1)))
                        drain(dve.tensor_tensor(
                            qpad[:, cb, :, 8 * jp + 2:8 * jp + 10, KS // 2:KS // 2 + W],
                            ps[:].rearrange("p a (r q x) -> p q (a r) x", q=2, x=W),
                            bq_all[:].rearrange("p a (r q x) -> p q (a r) x", q=2, x=W), ALU.add), ("qimg", cb, jp))
                for hg in range(NHG):
                    for jp in range(2):
                        ps = await_bank(dve, ("qh", hg, jp), b)
                        n = slice(jp * 512, (jp + 1) * 512)
                        dve.wait_ge(q_hi_done.sem, q_hi_done.at(b, 2 * hg + jp + 1))
                        drain(dve.scalar_tensor_tensor(q_lo[:, n], ps[:].rearrange("p a s -> p (a s)"),
                                                       bqh_c[:, hg:hg + 1], q_hi[:, n].bitcast(F32), ALU.add,
                                                       ALU.subtract), ("qh", hg, jp))
                k = d_of["off",]
                flat = pos[:].rearrange("p a s -> p (a s)")
                dve.wait_ge(k.drained, k.done(b, ("off",)))
                dve.tensor_tensor(flat, flat, refs, ALU.add).then_inc(pos_step.sem, 1)
                dve.wait_ge(pos_step.sem, pos_step.at(b, 1))
                dve.tensor_scalar(flat, flat, 1.0, float(H // R) / 2.0, ALU.add, ALU.mult).then_inc(pos_step.sem, 1)
                dve.wait_ge(pos_step.sem, pos_step.at(b, 2))
                dve.tensor_scalar(flat, flat, 1.0, 0.5 * (W - 1), ALU.add, ALU.mult).then_inc(pos_step.sem, 1)
                dve.wait_ge(hat_relu.sem, hat_relu.at(b, 2))
                dve.tensor_tensor(hat[:], hat[:], hat_x[:].rearrange("p (a s) -> p a s", a=1).broadcast_to([P, NT, S_]),
                                  ALU.mult).then_inc(hat_done.sem, 1)
                ps = await_bank(dve, ("kh",), b)
                dve.wait_ge(k_hi_done.sem, k_hi_done.at(b, 1))
                for hg in range(NHG):
                    ins = dve.scalar_tensor_tensor(k_lo[:, hg, :], ps[:, hg, :], bkh_c[:, hg:hg + 1],
                                                   k_hi[:, hg, :].bitcast(F32), ALU.add, ALU.subtract)
                drain(ins, ("kh",))
                ps = await_bank(dve, ("vh",), b)
                drain(dve.tensor_tensor(vh[:], ps[:], over_rows(bvh_all, 2), ALU.add), ("vh",))

            def maxima(b, u):
                if u:
                    dve.wait_ge(max_split.sem, max_split.at(b, u))
                else:
                    dve.wait_ge(max1_split.sem, max1_split.before(b, 2))
                for cb in range(2):
                    dve.wait_ge(s_bank.filled, s_bank.full(b, (u, cb)))
                    dve.tensor_reduce(mx[:, cb, :], ps_s[:], AX.X, ALU.max).then_inc(s_bank.drained, 1)
                dve.wait_ge(s_bank.drained, s_bank.done(b, (u, 1)))
                if u:
                    k = d_of["mxt", u - 1]
                    dve.wait_ge(k.filled, k.full(b, ("mxt", u - 1)))
                else:
                    k = d_of["mxt1", 1]
                    dve.wait_ge(k.drained, k.done_before(b, ("mxt1", 1)))
                dve.tensor_copy(mx_hl[:, :, 0, :], mx[:]).then_inc(max_hi.sem, 1)
                dve.wait_ge(max_hi.sem, max_hi.at(b, u + 1))
                dve.tensor_tensor(mx_hl[:, :, 1, :], mx[:], mx_hl[:, :, 0, :].bitcast(F32),
                                  ALU.subtract).then_inc(max_split.sem, 1)

            def normalise(b, u):
                hg, j = divmod(u, NJ)
                dve.wait_ge(v_bank.filled, v_bank.full(b, u))
                dve.reciprocal(rden[:], ps_v[:, 1, :]).then_inc(rden_done.sem, 1)
                dve.wait_ge(rden_done.sem, rden_done.at(b, u + 1))
                dve.tensor_tensor(att[:, hg, j * S_:(j + 1) * S_], ps_v[:, 0, :], rden[:],
                                  ALU.mult).then_inc(v_bank.drained, 1)

            def attn(b):
                for s in range(UNITS + 3):
                    if s < UNITS:
                        maxima(b, s)
                    if s >= 3:
                        normalise(b, s - 3)

            def post(b):
                for cb in range(2):
                    for jp in range(2):
                        ps = await_bank(dve, ("z", cb, jp), b)
                        if cb == 0 and jp == 0:
                            dve.wait_ge(xb_biased.sem, xb_biased.at(b, 1))
                            dve.wait_ge(out_stored.sem, out_stored.before(b, 1))
                        drain(dve.tensor_tensor(z[:, cb, 2 * jp:2 * jp + 2, :], ps[:], xb[:, cb, 2 * jp:2 * jp + 2, :],
                                                ALU.add), ("z", cb, jp))
                        k = d_of["z", cb, jp]
                        dve.wait_ge(k.drained, k.done(b, ("z", cb, jp)))
                        for jj in range(2):
                            n = cb * NJ + 2 * jp + jj
                            dve.bn_stats(st2[:, n, :], z[:, cb, 2 * jp + jj, :]).then_inc(ln2_stat.sem, 1)
                        dve.wait_ge(ln2_stat.sem, ln2_stat.at(b, cb * NJ + 2 * jp + 2))
                        gate(dve, "dve")
                        for jj in range(2):
                            n = cb * NJ + 2 * jp + jj
                            dve.bn_aggr(mv2[:, n, :], st2[:, n, :]).then_inc(ln2_aggr.sem, 1)
                    dve.wait_ge(ln2_aggr.sem, ln2_aggr.at(b, (cb + 1) * NJ))
                    rsqrt(rsqrt2, b, cb * RSQRT_STEPS, mv2[:, cb * NJ:(cb + 1) * NJ, 1], rs2[:, cb])
                    if cb:
                        dve.wait_ge(y_done.sem, y_done.at(b, 1))
                    for j in range(NJ):
                        n = cb * NJ + j
                        dve.tensor_scalar(zn[:, j, :], z[:, cb, j, :], mv2[:, n, 0:1], rs2[:, cb, 1, j:j + 1],
                                          ALU.subtract, ALU.mult).then_inc(zn_done.sem, 1)
                    for jp in range(2):
                        ps = await_bank(dve, ("mlp", cb, jp), b)
                        dve.wait_ge(zn_done.sem, zn_done.at(b, (cb + 1) * NJ))
                        drain(dve.tensor_tensor(mid[:, 2 * jp:2 * jp + 2, :], ps[:],
                                                over_rows(mlpb_all, 2),
                                                ALU.add), ("mlp", cb, jp))
                for lh in range(2):
                    ps = await_bank(dve, ("th", lh), b)
                    dve.wait_ge(th_hi.sem, th_hi.at(b, lh + 1))
                    rows = th_st[C8:2 * C8, lh * 512:(lh + 1) * 512]
                    drain(dve.scalar_tensor_tensor(rows, ps[C8:2 * C8].rearrange("p a s -> p (a s)"),
                                                   bth_c[C8:2 * C8], rows.bitcast(F32), ALU.add, ALU.subtract),
                          ("th", lh))
                for name, dst, m in (("ph", ph_pool, 3 * C8), ("g", g_pool, C2)):
                    for lh in range(2):
                        ps = await_bank(dve, (name, lh), b)
                        drain(dve.tensor_reduce(
                            dst[0:m, lh * P:(lh + 1) * P].rearrange("p (y x) -> p y x", x=W // 2),
                            ps[0:m].rearrange("p a s -> p (a s)").rearrange("p (y i x k) -> p y x i k", i=2, k=2, x=W // 2),
                            AX.XY, ALU.max), (name, lh))
                    k = d_of[name, 1]
                    dve.wait_ge(k.drained, k.done(b, (name, 1)))
                    k = d_of[name, 0]
                    dve.wait_ge(k.drained, k.done(b, (name, 0)))
                    if name == "ph":
                        dve.tensor_scalar(ph_pool[0:96], ph_pool[0:96], bph_c[0:96], None, ALU.add).then_inc(ph_step.sem, 1)
                        dve.wait_ge(ph_step.sem, ph_step.at(b, 1))
                        dve.tensor_copy(ph_st[0:96], ph_pool[0:96]).then_inc(ph_step.sem, 1)
                        dve.wait_ge(ph_step.sem, ph_step.at(b, 2))
                        dve.tensor_tensor(ph_st[64:96], ph_pool[64:96], ph_st[64:96].bitcast(F32),
                                          ALU.subtract).then_inc(ph_step.sem, 1)
                    else:
                        dve.tensor_scalar(g_pool[:], g_pool[:], bg_c, None, ALU.add).then_inc(g_bias.sem, 1)
                for lh in range(2):
                    dve.wait_ge(s_bank.filled, s_bank.full(b, ("l1", lh)))
                    k = d_of["mxt", UNITS - 1]
                    dve.wait_ge(k.filled, k.full(b, ("mxt", UNITS - 1)))
                    dve.wait_ge(max_split.sem, max_split.at(b, UNITS))
                    dve.tensor_reduce(mx[:, lh, :], ps_s[:], AX.X, ALU.max).then_inc(s_bank.drained, 1)
                    dve.wait_ge(s_bank.drained, s_bank.done(b, ("l1", lh)))
                    dve.tensor_copy(mx_hl[:, lh, 0, :], mx[:, lh, :]).then_inc(max1_hi.sem, 1)
                    dve.wait_ge(max1_hi.sem, max1_hi.at(b, lh + 1))
                    dve.tensor_tensor(mx_hl[:, lh, 1, :], mx[:, lh, :], mx_hl[:, lh, 0, :].bitcast(F32),
                                      ALU.subtract).then_inc(max1_split.sem, 1)
                ps = await_bank(dve, ("den",), b)
                drain(dve.reciprocal(rd1[:], ps[:, 0, 0:NT]), ("den",))
                k = d_of["den",]
                dve.wait_ge(k.drained, k.done(b, ("den",)))
                dve.tensor_scalar(rd1[:], rd1[:], sg_c, None, ALU.mult).then_inc(rd1_step.sem, 1)
                dve.wait_ge(rd1_step.sem, rd1_step.at(b, 1))
                for cb in range(2):
                    dve.wait_ge(ybo_done.sem, ybo_done.at(b, cb + 1))
                    for jp in range(2):
                        ps = await_bank(dve, ("o", cb, jp), b)
                        for jj in range(2):
                            j = 2 * jp + jj
                            n = cb * NJ + j
                            ins = dve.scalar_tensor_tensor(z[:, cb, j, :], ps[:, jj, :], rd1[:, n:n + 1],
                                                           z[:, cb, j, :], ALU.mult, ALU.add)
                        drain(ins, ("o", cb, jp))
                for key in dense:
                    if key[0] == "spare":
                        ps = await_bank(dve, key, b)
                        drain(dve.tensor_copy(rden[0:1, 0:1], ps[0:1, 0, 0:1]), key)

            with dve.Fori(0, B) as b:
                front(b)
                attn(b)
                post(b)

        @block.gpsimd
        def _(pool):
            pool.memset(dw_g[:], 0.0).then_inc(setup_pool, 1)
            pool.memset(vec_rows[:], 0.0).then_inc(setup_pool, 1)
            pool.memset(qpad[:], 0.0).then_inc(setup_pool, 1)
            pool.memset(ones[:], 1.0).then_inc(setup_pool, 1)
            pool.wait_ge(consts_in, N_CONST_IN)
            pool.wait_ge(setup_dve, 3)
            pool.tensor_copy(t_bv, bv_c.rearrange("p (t a) -> p t a", a=1).broadcast_to([P, 2, P])).then_inc(setup_pool, 1)
            pool.tensor_copy(pw_all[:].rearrange("p t o c -> p (t o) c"),
                             pw_c.rearrange("p (t a) -> p t a", a=1).broadcast_to([P, 4, P])).then_inc(setup_pool, 1)
            pool.tensor_tensor(
                conv_w[:].rearrange("p k h x c -> p (k h x) c"),
                dw_g[:].rearrange("p k h (x a) -> p (k h x) a", a=1).broadcast_to([P, 8 * 2 * KS, 32]),
                consts[:, K_M32:K_M32 + 32].rearrange("p (a c) -> p a c", a=1).broadcast_to([P, 8 * 2 * KS, 32]),
                ALU.mult).then_inc(setup_pool, 1)
            pool.tensor_scalar(bo_all[:], bo_all[:], sg_c, None, ALU.mult).then_inc(setup_pool, 1)
            pool.wait_ge(setup_pool, 8)

            with pool.Fori(0, B) as b:
                pool.wait_ge(rsqrt1.sem, rsqrt1.at(b, RSQRT_STEPS))
                k = d_of["samp",]
                pool.wait_ge(k.drained, k.done_before(b, ("samp",)))
                gate(pool, "pool")
                for t in range(NT):
                    pool.tensor_scalar(xln[:, t, :], xa[:, t, :], mv1[:, t, 0:1], rs1[:, 1, t:t + 1], ALU.subtract,
                                       ALU.mult).then_inc(ln1_norm.sem, 1)
                pool.wait_ge(xb_in.sem, xb_in.at(b, 1))
                flat = xb[:].rearrange("p k j c -> p (k j) c")
                pool.tensor_tensor(flat, flat, over_rows(mob_all, NT),
                                   ALU.add).then_inc(xb_biased.sem, 1)
                for cb in range(2):
                    pool.wait_ge(gelu_done.sem, gelu_done.at(b, 2 * cb + 2))
                    pool.tensor_tensor(z[:, cb], z[:, cb], mid[:], ALU.add).then_inc(y_done.sem, 1)
                for cb in range(2):
                    for kt in range(CB):
                        k = d_of["yt", cb, kt]
                        pool.wait_ge(k.filled, k.full(b, ("yt", cb, kt)))
                    pool.tensor_tensor(z[:, cb], z[:, cb], over_rows(bo_all, NJ), ALU.add).then_inc(ybo_done.sem, 1)


_INS = ['x', 'L0_conv_ln_g', 'L0_conv_ln_b', 'L0_conv_wq', 'L0_conv_bq', 'L0_conv_wv', 'L0_conv_bv', 'L0_conv_dw_w',
        'L0_conv_dw_b', 'L0_conv_pw_w', 'L0_conv_mq_w', 'L0_conv_mq_b', 'L0_conv_mk_w', 'L0_conv_mk_b',
        'L0_conv_mv_w', 'L0_conv_mv_b', 'L0_conv_mo_w', 'L0_conv_mo_b', 'L0_conv_mlp_w', 'L0_conv_mlp_b',
        'L1_conv_w_theta', 'L1_conv_b_theta', 'L1_conv_w_phi', 'L1_conv_b_phi', 'L1_conv_w_g', 'L1_conv_b_g',
        'L1_conv_w_o', 'L1_conv_b_o', 'L1_conv_sigma']


def kernel(**inputs):
    import numpy as _np
    import concourse.bacc as _bacc
    from concourse import mybir as _mybir
    from concourse.bass_utils import run_bass_kernel_spmd as _run

    nc = _bacc.Bacc("TRN2", target_bir_lowering=False, num_devices=1)
    arrays, aps = {}, {}
    given = {name: _np.ascontiguousarray(inputs[name]) for name in _INS}
    given["L1_conv_sigma"] = given["L1_conv_sigma"].reshape(1)
    given["shape_constants"] = shape_constants()
    for name, v in given.items():
        arrays[f"in_{name}_dram"] = v
        aps[name] = nc.dram_tensor(f"in_{name}_dram", v.shape, _mybir.dt.from_np(v.dtype), kind="ExternalInput").ap()
    out = nc.dram_tensor("out_0_dram", (B, H, W, C), F32, kind="ExternalOutput").ap()
    build(nc, aps, out)
    r = _run(nc, [arrays], core_ids=[0])
    return r.results[0]["out_0_dram"]
```

```python
from contextlib import ExitStack

import numpy as np

import concourse.bass as bass
from concourse import mybir

F32 = mybir.dt.float32
F32R = mybir.dt.float32r
I32 = mybir.dt.int32
ALU = mybir.AluOpType
ACT = mybir.ActivationFunctionType
AX = mybir.AxisListType

P = 128
B, H, W, C = 4, 32, 32, 256
HW = H * W
NT = HW // P
CB = C // P
R, KS = 2, 7
HG_, WG_ = H // R, W // R
S_ = HG_ * WG_
NH = 8
HD = C // NH
HQ = P // HD
NHG = NH // HQ
NJ = HW // C
C8, C2 = C // 8, C // 2
EPS = 1e-5
PADW = W + 2 * (KS // 2)
PLANE = 20
CROWS = HG_ + 2
UNITS = NHG * NJ
NEWTON = 3
RSQRT_STEPS = 3 + 3 * NEWTON
QIMG_AT = (3, 4)
CONV_AT = (7, 9)
N_ROWS = 21

K_ID = 0
K_REF = K_ID + P
K_XP = K_REF + 2 * S_
K_YP = K_XP + 1
K_M32 = K_YP + NT
K_N = K_M32 + 32


def shape_constants():
    k = np.zeros((P, K_N), np.float32)
    p = np.arange(P)
    k[:, K_ID:K_ID + P] = np.eye(P)
    ref_x = (np.arange(WG_, dtype=np.float32) + np.float32(0.5)) * np.float32(2.0 / WG_) - np.float32(1.0)
    ref_y = (np.arange(HG_, dtype=np.float32) + np.float32(0.5)) * np.float32(2.0 / HG_) - np.float32(1.0)
    k[:, K_REF:K_REF + S_] = np.repeat(ref_x, HG_)[None]
    k[:, K_REF + S_:K_REF + 2 * S_] = np.tile(ref_y, WG_)[None]
    k[:, K_XP] = -(p % W)
    for t in range(NT):
        k[:, K_YP + t] = -((P // W) * t + p // W)
    k[:, K_M32:K_M32 + 32] = (p[:, None] % 32 == np.arange(32)[None])
    return k


class Signal:

    def __init__(self, sem, per, unit=1, credit=False):
        self.sem, self.per, self.unit = sem, per, unit
        self.start = per * unit if credit else 0

    def at(self, b, n):
        return b * (self.per * self.unit) + (self.start + n * self.unit)

    def before(self, b, n):
        assert self.start and n >= 1
        return b * (self.per * self.unit) + (self.start + (n - self.per) * self.unit)


class Bank:

    def __init__(self, filled, drained, uses):
        self.filled, self.drained = filled, drained
        self.uses = {key: n for n, key in enumerate(uses)}
        assert len(self.uses) == len(uses)

    def full(self, b, key):
        return b * len(self.uses) + (self.uses[key] + 2)

    def empty(self, b, key):
        return b * len(self.uses) + (self.uses[key] + 1)

    def done(self, b, key):
        return b * len(self.uses) + (self.uses[key] + 2)


class Use:

    def __init__(self, tile, filled, drained, before):
        self.tile, self.filled, self.drained = tile, filled, drained
        self.empty = before + 1
        self.full = before + 2
        self.done = before + 2


class Ring:

    def __init__(self, tiles, filled, drained, prologue, body, epilogue):
        self.tiles, self.filled, self.drained = tiles, filled, drained
        n = len(tiles)
        assert len(body) % n == 0
        self.per_turn = len(body) // n
        self.orders = {"prologue": (0, prologue), "body": (len(prologue), body),
                       "epilogue": (len(prologue), epilogue)}
        self.ahead = [len(range(k, len(prologue), n)) for k in range(n)]

    def use(self, key, b):
        n = len(self.tiles)
        is_int = isinstance(b, int)
        if key in self.orders["prologue"][1]:
            name, turn = ("prologue", 0) if is_int and b == 0 else ("body", b - 1)
        else:
            name, turn = ("epilogue" if is_int and b == B - 1 else "body"), b
        first, order = self.orders[name]
        at = first + order.index(key)
        k = at % n
        before = at // n if name == "prologue" else turn * self.per_turn + at // n
        return Use(self.tiles[k], self.filled[k], self.drained[k], before)

    def settled(self, key, b):
        n = len(self.tiles)
        u = self.use(key, b)
        k = [i for i in range(n) if self.tiles[i] is u.tile][0]
        if key in self.orders["prologue"][1]:
            before = 0 if isinstance(b, int) and b == 0 else (b - 1) * self.per_turn + self.ahead[k]
        else:
            before = b * self.per_turn + self.ahead[k]
        return Use(u.tile, u.filled, u.drained, before - 1)


def build(nc, a, out):
    x_rows = a["x"].rearrange("b h w c -> b (h w) c")
    out_rows = out.rearrange("b h w c -> b (h w) c")

    ctx = ExitStack()
    with ctx:
        def sb(name, shape, dt=F32):
            return ctx.enter_context(nc.sbuf_tensor(name, shape, dt))

        def sem(name):
            return ctx.enter_context(nc.semaphore(name))

        consts = sb("consts", [P, K_N])
        ident = consts[:, K_ID:K_ID + P]
        refs = consts[:, K_REF:K_REF + 2 * S_]
        wq = sb("wq", [P, CB, C])
        w_qh = sb("w_qh", [P, CB, C])
        w_kh = sb("w_kh", [P, CB, C])
        w_vh = sb("w_vh", [P, CB, C])
        mo = sb("mo", [P, CB, C])
        mlp = sb("mlp", [P, CB, C])
        w_th = sb("w_th", [P, CB, 3 * C8])
        w_ph = sb("w_ph", [P, CB, 3 * C8])
        w_g = sb("w_g", [P, CB, C2])
        w_o = sb("w_o", [P, C])
        bq_all = sb("bq_all", [P, 2, C])
        lng_all = sb("lng_all", [P, C])
        lnb_all = sb("lnb_all", [P, C])
        mob_all = sb("mob_all", [P, C])
        mlpb_all = sb("mlpb_all", [P, C])
        bo_all = sb("bo_all", [P, C])
        bvh_all = sb("bvh_all", [P, C])
        cols = sb("cols", [P, 3, 32])
        bq_c, bv_c = cols[:, 0, 0:2], cols[:, 0, 2:4]
        mqb_c, mkb_c = cols[:, 1, 4:6], cols[:, 1, 6:8]
        lng_c, lnb_c, dwb_c = cols[:, 0, 8:10], cols[:, 0, 10:12], cols[:, 2, 12:14]
        pw_c = cols[:, 2, 14:18]
        bth_c, bph_c, bg_c, sg_c = cols[:, 0, 18:19], cols[:, 0, 19:20], cols[:, 0, 20:21], cols[:, 0, 31:32]
        bqh_c, bkh_c = cols[:, 0, 22:24], cols[:, 0, 24:26]
        pw_all = sb("pw_all", [P, CB, 2, P])
        conv_w = sb("conv_w", [P, 8, 2, KS, 32])
        ones = sb("ones", [P, 32])

        xa = sb("xa", [P, NT, C])
        xln = sb("xln", [P, NT, C])
        hat = xln
        qpad = sb("qpad", [P, CB, 2, PLANE, PADW])
        cstack = sb("cstack", [P, 4, CROWS, PADW])
        gel = sb("gel", [P, CB, S_])
        pos = sb("pos", [P, 2, S_])
        hat_x = sb("hat_x", [P, S_])
        samp = sb("samp", [P, CB, C])
        q_hi = sb("q_hi", [P, HW], F32R)
        q_lo = sb("q_lo", [P, HW], F32R)
        k_hi = q_hi[:, 0:NHG * S_].rearrange("p (g s) -> p g s", g=NHG)
        k_lo = q_lo[:, 0:NHG * S_].rearrange("p (g s) -> p g s", g=NHG)
        st1 = sb("st1", [P, NT, 6])
        mv1 = sb("mv1", [P, NT, 2])
        rs1 = sb("rs1", [P, 4, NT])
        k_st = sb("k_st", [P, NH, S_], F32R)
        q_st = sb("q_st", [P, NH, HW], F32R)
        vh = sb("vh", [P, 2, C])
        mx = sb("mx", [P, 2, HQ])
        mx_hl = sb("mx_hl", [P, 2, 2, HQ], F32R)
        mx_t = sb("mx_t", [2 * HQ, 2, 2 * P], F32R)
        prob = sb("prob", [P, 2, HQ, 2, S_])
        rden = sb("rden", [P, S_])
        att = sb("att", [P, NHG, HW])
        xb = sb("xb", [P, 2, NJ, C])
        z = sb("z", [P, 2, NJ, C])
        zn = sb("zn", [P, 2, NJ, C])
        mid = zn
        st2 = sb("st2", [P, NT, 6])
        mv2 = sb("mv2", [P, NT, 2])
        rs2 = sb("rs2", [P, 2, 4, NJ])
        zt = sb("zt", [P, CB, HW])
        th_st = sb("th_st", [P, HW], F32R)
        ph_pool = sb("ph_pool", [P, S_])
        ph_st = sb("ph_st", [P, S_], F32R)
        g_pool = sb("g_pool", [P, S_])
        g_m = sb("g_m", [P, 2, C2])
        rd1 = sb("rd1", [P, NT])
        prob1 = prob[:, 0].rearrange("p h m s -> p (h m s)").rearrange("p (m l) -> p m l", m=2)

        ag = prob[:, 1].rearrange("p h m s -> p (h m s)")[:, 0:HW]

        tmp = prob[:].rearrange("p a h m s -> p (a h m s)")
        t_wv, t_mqp, t_mkp, t_mv, t_wqt, t_wvt = [
            tmp[:, n * 512:(n + 1) * 512].rearrange("p (t c) -> p t c", t=2) for n in range(6)]
        t_bv = tmp[:, 3072:3072 + 256].rearrange("p (t c) -> p t c", t=2)
        t_mq = zt[:, 0, 0:512].rearrange("p (t c) -> p t c", t=2)
        t_mk = zt[:, 0, 512:1024].rearrange("p (t c) -> p t c", t=2)
        mvb_all = zt[:, 1, 0:C]
        vec_rows = zt[0:N_ROWS, 1, C:C + 3 * P].rearrange("p (n c) -> p n c", n=3)
        dw_g = zt[:, 1, 640:640 + 16 * KS].rearrange("p (k h x) -> p k h x", k=8, h=2)

        ps_s = ctx.enter_context(nc.psum_tensor("ps_s", [P, 4, S_], F32))
        ps_t = ctx.enter_context(nc.psum_tensor("ps_t", [P, 4, S_], F32))
        ps_v = ctx.enter_context(nc.psum_tensor("ps_v", [P, 2, S_], F32))
        ps_d = [ctx.enter_context(nc.psum_tensor(f"ps_d{k}", [P, 2, S_], F32)) for k in range(3)]

        two = range(2)
        qimg = [[("qimg", cb, jp) for jp in two] for cb in range(CB)]
        qh = [[("qh", hg, jp) for jp in two] for hg in range(NHG)]
        conv = [("conv", cb) for cb in range(CB)]
        front_order = qimg[0] + qimg[1] + conv + [("off",)] + qh[0] + qh[1] + [("samp",), ("kh",), ("vh",)]

        def in_turn(front):
            def side(keys):
                return keys if front else []
            order = []
            for s in range(UNITS + 3):
                if 1 <= s <= UNITS:
                    order.append(("mxt", s - 1))
                order += side({QIMG_AT[0]: qimg[0], QIMG_AT[1]: qimg[1],
                               CONV_AT[0]: conv[0:1], CONV_AT[1]: conv[1:2]}.get(s, []))
            for cb in two:
                order += [("z", cb, jp) for jp in two]
                if cb == 0:
                    order += side([("off",)])
                order += side(qh[cb])
            for cb in two:
                order += [("znt", cb, k) for k in range(CB)]
                order += [("mlp", cb, jp) for jp in two]
            order += side([("samp",)])
            order += [("yt", cb, k) for cb in two for k in range(CB)]
            order += [("th", lh) for lh in two] + [("ph", lh) for lh in two]
            order += side([("kh",)])
            order += [("g", lh) for lh in two] + [("gt",)]
            order += side([("vh",)])
            order += [("mxt1", lh) for lh in two] + [("ag", lh) for lh in two] + [("den",)]
            order += [("o", cb, jp) for cb in two for jp in two]
            return order

        ring = Ring(ps_d, [sem(f"dense{k}_filled") for k in range(3)], [sem(f"dense{k}_drained") for k in range(3)],
                    front_order, in_turn(True), in_turn(False))
        use = ring.use
        s_bank = Bank(sem("scores_filled"), sem("scores_drained"),
                      [(u, cb) for u in range(UNITS) for cb in range(2)] + [("l1", lh) for lh in range(2)])
        t_bank = Bank(sem("shifted_filled"), sem("shifted_drained"),
                      [(u, pr) for u in range(UNITS) for pr in range(2)] + [("l1", lh) for lh in range(2)])
        v_bank = Bank(sem("values_filled"), sem("values_drained"), list(range(UNITS)))

        signals = []

        def signal(name, per, unit=1, credit=False):
            s = Signal(sem(name), per, unit, credit)
            signals.append(s)
            return s

        consts_in = sem("consts_in")
        setup_pe = sem("setup_products")
        setup_dve = sem("setup_copies")
        setup_pool = sem("setup_fills")
        minus_rows = sem("minus_rows")
        xa_in = signal("xa_in", 1, 16)
        xb_in = signal("xb_in", 1, 16)
        xb_biased = signal("xb_biased", 1, credit=True)
        ln1_stat = signal("ln1_stat", NT, credit=True)
        ln1_aggr = signal("ln1_aggr", NT)
        rsqrt1 = signal("rsqrt1", RSQRT_STEPS, credit=True)
        ln1_norm = signal("ln1_norm", NT)
        ln1_scaled = signal("ln1_scaled", 2)
        xln_ready = signal("xln_ready", 2, credit=True)
        conv_in = [signal(f"conv_in{cb}", 4, 16) for cb in range(CB)]
        tanh_done = signal("tanh_done", 1)
        pos_step = signal("pos_step", 3)
        hat_dist = signal("hat_dist", 1 + NT)
        hat_relu = signal("hat_relu", 2)
        hat_done = signal("hat_done", 1)
        k_hi_done = signal("k_hi_done", 1)
        k_in = signal("k_in", 3 * NHG, 16, credit=True)
        q_hi_done = signal("q_hi_done", NHG * 2)
        q_in = [signal(f"q_in{hg}", 3, 16, credit=True) for hg in range(NHG)]
        max_hi = signal("max_hi", UNITS)
        max_split = signal("max_split", UNITS)
        max_in = [signal(f"max_in{k}", UNITS // 2, 16, credit=True) for k in range(2)]
        rden_done = signal("rden_done", UNITS)
        ln2_stat = signal("ln2_stat", NT, credit=True)
        ln2_aggr = signal("ln2_aggr", NT)
        rsqrt2 = signal("rsqrt2", 2 * RSQRT_STEPS, credit=True)
        zn_done = signal("zn_done", NT)
        gelu_done = signal("mlp_gelu", 4)
        y_done = signal("y_done", 2, credit=True)
        ybo_done = signal("ybo_done", 2)
        th_hi = signal("th_hi", 2)
        ph_step = signal("ph_step", 3)
        g_bias = signal("g_bias", 1)
        max1_hi = signal("max1_hi", 2)
        max1_split = signal("max1_split", 2, credit=True)
        max1_in = [signal(f"max1_in{k}", 1, 16, credit=True) for k in range(2)]
        rd1_step = signal("rd1_step", 1)
        out_stored = signal("out_stored", 1, 16, credit=True)

        N_CONST_IN = 0
        const_dmas = []
        zeroed_dmas = []

        def row2(at, src):
            zeroed_dmas.append((vec_rows[at:at + 2, 0, :], src.rearrange("(t p) -> t p", p=P)))

        def whole(dst, src):
            const_dmas.append((dst, src.rearrange("(a c) -> a c", a=1).broadcast_to([P, C])))

        def mat(dst, src):
            const_dmas.append((dst, src.rearrange("(t p) c -> p t c", p=P)))

        const_dmas.append((consts[:], a["shape_constants"]))
        mat(wq[:], a["L0_conv_wq"])
        mat(t_mq, a["L0_conv_mq_w"])
        mat(t_wv, a["L0_conv_wv"])
        mat(t_mk, a["L0_conv_mk_w"])
        mat(t_mv, a["L0_conv_mv_w"])
        row2(0, a["L0_conv_bq"])
        row2(2, a["L0_conv_bv"])
        row2(4, a["L0_conv_mq_b"])
        row2(6, a["L0_conv_mk_b"])
        row2(8, a["L0_conv_ln_g"])
        row2(10, a["L0_conv_ln_b"])
        row2(12, a["L0_conv_dw_b"])
        whole(lng_all[:], a["L0_conv_ln_g"])
        whole(lnb_all[:], a["L0_conv_ln_b"])
        whole(bq_all[:, 0, :], a["L0_conv_bq"])
        whole(bq_all[:, 1, :], a["L0_conv_bq"])
        whole(mvb_all[:], a["L0_conv_mv_b"])
        for o in range(2):
            for t in range(CB):
                zeroed_dmas.append((vec_rows[14 + 2 * t + o:15 + 2 * t + o, 0, :],
                                   a["L0_conv_pw_w"][o, t * P:(t + 1) * P].rearrange("p h w -> (h w) p")))
        dw = a["L0_conv_dw_w"].rearrange("(b c k) o h w -> b c k (o h) w", b=CB, k=4)
        for g in range(4):
            for hi in range(2):
                for cb in range(CB):
                    if g + 4 * hi < KS:
                        zeroed_dmas.append((dw_g[32 * g:32 * g + 32, 4 * cb:4 * cb + 4, hi, :],
                                           dw[cb, :, :, g + 4 * hi, :]))
        mat(mo[:], a["L0_conv_mo_w"])
        mat(mlp[:], a["L0_conv_mlp_w"])
        whole(mob_all[:], a["L0_conv_mo_b"])
        whole(mlpb_all[:], a["L0_conv_mlp_b"])
        for n in range(3):
            mat(w_th[:, :, n * C8:(n + 1) * C8], a["L1_conv_w_theta"])
            mat(w_ph[:, :, n * C8:(n + 1) * C8], a["L1_conv_w_phi"])
            for at, name in ((18, "L1_conv_b_theta"), (19, "L1_conv_b_phi")):
                zeroed_dmas.append((vec_rows[at:at + 1, 0, n * C8:(n + 1) * C8], a[name].rearrange("(a p) -> a p", a=1)))
        mat(w_g[:], a["L1_conv_w_g"])
        zeroed_dmas.append((vec_rows[20:21, 0, :], a["L1_conv_b_g"].rearrange("(a p) -> a p", a=1)))
        const_dmas.append((w_o[:], a["L1_conv_w_o"]))
        whole(bo_all[:], a["L1_conv_b_o"])
        const_dmas.append((sg_c, a["L1_conv_sigma"].rearrange("(a c) -> a c", a=1).broadcast_to([P, 1])))
        N_CONST_IN = 16 * (len(const_dmas) + len(zeroed_dmas))

        gates = {n: sem(f"gate_{n}") for n in ("sp", "dve", "pool")}

        def gate(eng, name):
            eng.sem_inc(gates[name], 1)

        def over_rows(row, n):
            return row[:].rearrange("p (a c) -> p a c", a=1).broadcast_to([P, n, C])

        block = ctx.enter_context(nc.Block())

        @block.sync
        def _(sp):
            for s in signals:
                if s.start:
                    sp.sem_inc(s.sem, s.start)
            for k in (*ring.filled, *ring.drained):
                sp.sem_inc(k, 1)
            for k in (s_bank, t_bank, v_bank):
                sp.sem_inc(k.filled, 1)
                sp.sem_inc(k.drained, 1)
            for dst, src in const_dmas:
                sp.dma_start(dst, src).then_inc(consts_in, 16)
            sp.wait_ge(setup_pool, 2)
            for dst, src in zeroed_dmas:
                sp.dma_start(dst, src).then_inc(consts_in, 16)

            def load_a(b):
                sp.wait_ge(xln_ready.sem, xln_ready.before(b, 2))
                gate(sp, "sp")
                k = ring.settled(("samp",), b)
                sp.wait_ge(k.drained, k.done)
                gate(sp, "sp")
                sp.dma_start(xa[:], x_rows[b].rearrange("(t p) c -> p t c", p=P)).then_inc(xa_in.sem, 16)

            def load_b(b):
                k = ring.settled(("z", 1, 1), b)
                sp.wait_ge(k.drained, k.done)
                gate(sp, "sp")
                k = ring.settled(("z", 0, 1), b)
                sp.wait_ge(k.drained, k.done)
                gate(sp, "sp")
                sp.dma_start(xb[:], x_rows[b].rearrange("(k p j) c -> p k j c", k=2, j=NJ)).then_inc(xb_in.sem, 16)

            def stack_conv(b, cb):
                for jp in range(2):
                    k = use(("qimg", cb, jp), b)
                    sp.wait_ge(k.drained, k.done)
                    gate(sp, "sp")
                if cb:
                    k = use(("conv", 0), b)
                    sp.wait_ge(k.filled, k.full)
                    gate(sp, "sp")
                for g in range(4):
                    r0 = g // 2 + g % 2
                    sp.dma_start(cstack[32 * g:32 * g + 32].rearrange("c k r x -> c k (r x)"),
                                 qpad[:, cb, 1 - g % 2, r0:r0 + CROWS, :].rearrange("c r x -> c (r x)")
                                 ).then_inc(conv_in[cb].sem, 16)

            def stack_q(b, hg):
                k = use(("qh", hg, 1), b)
                sp.wait_ge(k.drained, k.done)
                gate(sp, "sp")
                for row, src in ((0, q_hi), (1, q_lo), (2, q_hi)):
                    sp.dma_start(q_st[32 * row:32 * row + 32, hg * HQ:(hg + 1) * HQ, :].bitcast(F32),
                                 src[:].bitcast(F32)).then_inc(q_in[hg].sem, 16)

            def stack_k(b):
                k = use(("kh",), b)
                sp.wait_ge(k.drained, k.done)
                gate(sp, "sp")
                for hg in range(NHG):
                    for row, src in ((0, k_hi), (1, k_hi), (2, k_lo)):
                        sp.dma_start(k_st[32 * row:32 * row + 32, hg * HQ:(hg + 1) * HQ, :].bitcast(F32),
                                     src[:, hg, :].bitcast(F32)).then_inc(k_in.sem, 16)

            def max_row(b, u):
                hg, j = divmod(u, NJ)
                k = use(("mxt", u), b)
                sp.wait_ge(k.drained, k.done)
                gate(sp, "sp")
                sp.dma_start(q_st[96:98, hg * HQ:(hg + 1) * HQ, j * S_:(j + 1) * S_].bitcast(F32),
                             mx_t[:, u % 2, :].bitcast(F32)).then_inc(max_in[u % 2].sem, 16)

            def turn(b, nb):
                if nb is not None:
                    load_a(nb)
                load_b(b)
                for s in range(UNITS + 3):
                    if 1 <= s <= UNITS:
                        max_row(b, s - 1)
                    if nb is not None and s in QIMG_AT:
                        if s == QIMG_AT[0]:
                            stack_conv(nb, 0)
                    if nb is not None and s == CONV_AT[0]:
                        stack_conv(nb, 1)
                if nb is not None:
                    stack_q(nb, 0)
                    stack_q(nb, 1)
                    stack_k(nb)
                for lh in range(2):
                    k = use(("mxt1", lh), b)
                    sp.wait_ge(k.drained, k.done)
                    gate(sp, "sp")
                    sp.dma_start(th_st[96:98, lh * 512:(lh + 1) * 512].bitcast(F32),
                                 mx_t[:, lh, 0:P].bitcast(F32)).then_inc(max1_in[lh].sem, 16)
                for cb in range(2):
                    for jp in range(2):
                        k = use(("o", cb, jp), b)
                        sp.wait_ge(k.drained, k.done)
                        gate(sp, "sp")
                sp.dma_start(out_rows[b].rearrange("(k p j) c -> p k j c", k=2, j=NJ), z[:]).then_inc(out_stored.sem, 16)

            load_a(0)
            stack_conv(0, 0)
            stack_conv(0, 1)
            stack_q(0, 0)
            stack_q(0, 1)
            stack_k(0)
            with sp.Fori(0, B - 1) as b:
                turn(b, b + 1)
            turn(B - 1, None)
            sp.wait_ge(out_stored.sem, out_stored.at(B - 1, 1))

        @block.tensor
        def _(pe):
            pe.wait_ge(consts_in, N_CONST_IN)
            for w, ps in ((wq, ps_d[0]), (t_wv, ps_d[1])):
                for nt in range(2):
                    for kt in range(2):
                        ins = pe.transpose(ps[:, nt, kt * P:(kt + 1) * P], w[:, kt, nt * P:(nt + 1) * P], ident)
                ins.then_inc(setup_pe, 1)
            pe.wait_ge(setup_dve, 2)
            for n in range(3):
                ins = pe.transpose(ps_d[2][:, 0, 32 * n:32 * n + N_ROWS], vec_rows[:, n, :], ident[0:N_ROWS, 0:N_ROWS])
            ins.then_inc(setup_pe, 1)
            for n, (wt, m, ps) in enumerate(((t_wqt, t_mqp, ps_s[:, 0:2, :]), (t_wvt, t_mkp, ps_s[:, 2:4, :]),
                                             (t_wvt, t_mv, ps_t[:, 0:2, :]))):
                pe.wait_ge(setup_dve, 6 if n else 5)
                for kt in range(2):
                    for nt in range(2):
                        ins = pe.matmul(ps[:, kt, :], wt[:, nt, kt * P:(kt + 1) * P], m[:, nt, :],
                                        start=nt == 0, stop=nt == 1)
                ins.then_inc(setup_pe, 1)
            pe.wait_ge(setup_dve, 7)
            for n, (m, bc) in enumerate(((t_mqp, bq_c), (t_mkp, bv_c))):
                for mb in range(2):
                    for nt in range(2):
                        ins = pe.matmul(ps_v[:, 0, 2 * n + mb:2 * n + mb + 1], m[:, nt, mb * P:(mb + 1) * P],
                                        bc[:, nt:nt + 1], start=nt == 0, stop=nt == 1)
            ins.then_inc(setup_pe, 1)
            pe.wait_ge(setup_pool, 6)
            pe.wait_ge(setup_dve, 10)
            for nt in range(2):
                ins = pe.matmul(ps_t[:, 2, :], t_bv[:, nt, :], t_mv[:, nt, :], start=nt == 0, stop=nt == 1)
            ins.then_inc(setup_pe, 1)
            pe.wait_ge(setup_dve, 13)
            pe.wait_ge(setup_pool, 7)
            pe.wait_ge(minus_rows, 2)

            def open_bank(key, b):
                k = use(key, b)
                pe.wait_ge(k.drained, k.empty)
                return k.tile

            def close_bank(key, b, ins):
                ins.then_inc(use(key, b).filled, 1)

            def read_by(key, b):
                k = use(key, b)
                pe.wait_ge(k.drained, k.done)

            def q_image(b, cb):
                for jp in range(2):
                    ps = open_bank(("qimg", cb, jp), b)
                    if cb == 0:
                        pe.wait_ge(xln_ready.sem, xln_ready.at(b, jp + 1))
                    for jj in range(2):
                        for kt in range(2):
                            t = 4 * jp + 2 * jj + kt
                            ins = pe.matmul(ps[:, jj, :], xln[:, t, cb * P:(cb + 1) * P], wq[:, kt, :],
                                            start=kt == 0, stop=kt == 1)
                    close_bank(("qimg", cb, jp), b, ins)

            def conv_part(b, cb, hi):
                if hi == 0:
                    open_bank(("conv", cb), b)
                    pe.wait_ge(conv_in[cb].sem, conv_in[cb].at(b, 4))
                ps = use(("conv", cb), b).tile
                for dx in range(KS):
                    for k in range(4):
                        ins = pe.matmul(
                            ps[32 * k:32 * k + 32, 0, :], conv_w[:, cb * 4 + k, hi, dx, :],
                            cstack[:, k, 2 * hi:2 * hi + HG_, dx:dx + 2 * WG_ - 1:2],
                            start=hi == 0 and dx == 0, stop=hi == 1 and dx == KS - 1)
                if hi == 1:
                    close_bank(("conv", cb), b, ins)

            def offsets(b):
                ps = open_bank(("off",), b)
                read_by(("conv", 0), b)
                read_by(("conv", 1), b)
                for o in range(2):
                    for kt in range(CB):
                        ins = pe.matmul(ps[:, o, :], pw_all[:, kt, o, :], gel[:, kt, :], start=kt == 0, stop=kt == 1)
                close_bank(("off",), b, ins)

            def queries(b, hg):
                for jp in range(2):
                    ps = open_bank(("qh", hg, jp), b)
                    for jj in range(2):
                        for kt in range(2):
                            ins = pe.matmul(ps[:, jj, :], w_qh[:, kt, hg * P:(hg + 1) * P],
                                            xln[:, 4 * jp + 2 * jj + kt, :], start=kt == 0, stop=kt == 1)
                    close_bank(("qh", hg, jp), b, ins)

            def sample(b):
                ps = open_bank(("samp",), b)
                pe.wait_ge(hat_done.sem, hat_done.at(b, 1))
                for st in range(2):
                    for t in range(NT):
                        ins = pe.matmul(ps[:, st, :], hat[:, t, st * P:(st + 1) * P], xa[:, t, :],
                                        start=t == 0, stop=t == NT - 1)
                close_bank(("samp",), b, ins)

            def keys(b):
                ps = open_bank(("kh",), b)
                read_by(("samp",), b)
                for hg in range(NHG):
                    for st in range(2):
                        ins = pe.matmul(ps[:, hg, :], w_kh[:, st, hg * P:(hg + 1) * P], samp[:, st, :],
                                        start=st == 0, stop=st == 1)
                close_bank(("kh",), b, ins)

            def value_rows(b):
                ps = open_bank(("vh",), b)
                for rb in range(2):
                    for st in range(2):
                        ins = pe.matmul(ps[:, rb, :], samp[:, st, rb * P:(rb + 1) * P], w_vh[:, st, :],
                                        start=st == 0, stop=st == 1)
                close_bank(("vh",), b, ins)

            def scores(b, u):
                hg, j = divmod(u, NJ)
                if u == 0:
                    pe.wait_ge(k_in.sem, k_in.at(b, 3 * NHG))
                if j == 0:
                    pe.wait_ge(q_in[hg].sem, q_in[hg].at(b, 3))
                for cb in range(2):
                    pe.wait_ge(s_bank.drained, s_bank.empty(b, (u, cb)))
                    for h in range(HQ):
                        ins = pe.matmul(ps_s[:, h, :], q_st[0:96, hg * HQ + h, j * S_ + cb * P:j * S_ + (cb + 1) * P],
                                        k_st[0:96, hg * HQ + h, :], start=True, stop=True)
                    ins.then_inc(s_bank.filled, 1)

            def max_rows(b, u):
                ps = open_bank(("mxt", u), b)
                pe.wait_ge(max_split.sem, max_split.at(b, u + 1))
                for cb in range(2):
                    ins = pe.transpose(ps[0:2 * HQ, 0, cb * P:(cb + 1) * P],
                                       mx_hl[:, cb].rearrange("p a h -> p (a h)").bitcast(F32), ident)
                close_bank(("mxt", u), b, ins)

            def shifted(b, u, pr):
                hg, j = divmod(u, NJ)
                if pr == 0:
                    pe.wait_ge(max_in[u % 2].sem, max_in[u % 2].at(b, u // 2 + 1))
                pe.wait_ge(t_bank.drained, t_bank.empty(b, (u, pr)))
                for hh in range(2):
                    h = 2 * pr + hh
                    for mt in range(2):
                        ins = pe.matmul(ps_t[:, 2 * hh + mt, :], k_st[0:98, hg * HQ + h, mt * P:(mt + 1) * P],
                                        q_st[0:98, hg * HQ + h, j * S_:(j + 1) * S_], start=True, stop=True)
                ins.then_inc(t_bank.filled, 1)

            def values(b, u):
                hg = u // NJ
                pe.wait_ge(t_bank.drained, t_bank.done(b, (u, 1)))
                pe.wait_ge(v_bank.drained, v_bank.empty(b, u))
                if u == 0:
                    read_by(("vh",), b)
                for den in range(2):
                    for mt in range(2):
                        for h in range(HQ):
                            hh = hg * HQ + h
                            wt = ones[:] if den else vh[:, mt, hh * HD:(hh + 1) * HD]
                            ins = pe.matmul(ps_v[32 * h:32 * h + 32, den, :], wt, prob[:, u % 2, h, mt, :],
                                            start=mt == 0, stop=mt == 1)
                ins.then_inc(v_bank.filled, 1)

            def project(b, cb):
                for jp in range(2):
                    ps = open_bank(("z", cb, jp), b)
                    pe.wait_ge(v_bank.drained, v_bank.done(b, UNITS - 1))
                    for jj in range(2):
                        j = 2 * jp + jj
                        for hg in range(NHG):
                            ins = pe.matmul(ps[:, jj, :], att[:, hg, j * S_ + cb * P:j * S_ + (cb + 1) * P],
                                            mo[:, hg, :], start=hg == 0, stop=hg == 1)
                    close_bank(("z", cb, jp), b, ins)

            def turn_rows(b, cb):
                for kt in range(CB):
                    ps = open_bank(("znt", cb, kt), b)
                    if kt == 0:
                        pe.wait_ge(zn_done.sem, zn_done.at(b, (cb + 1) * NJ))
                    for j in range(NJ):
                        ins = pe.transpose(ps[:, j // 2, (j % 2) * P:(j % 2 + 1) * P],
                                           zn[:, cb, j, kt * P:(kt + 1) * P], ident)
                    close_bank(("znt", cb, kt), b, ins)

            def mlp_rows(b, cb):
                for jp in range(2):
                    ps = open_bank(("mlp", cb, jp), b)
                    if jp == 0:
                        read_by(("znt", cb, 0), b)
                        read_by(("znt", cb, 1), b)
                    for jj in range(2):
                        j = 2 * jp + jj
                        for kt in range(CB):
                            ins = pe.matmul(ps[:, jj, :], zt[:, kt, cb * 512 + j * P:cb * 512 + (j + 1) * P],
                                            mlp[:, kt, :], start=kt == 0, stop=kt == 1)
                    close_bank(("mlp", cb, jp), b, ins)

            def turn_output(b):
                for cb in range(2):
                    for kt in range(CB):
                        ps = open_bank(("yt", cb, kt), b)
                        if kt == 0:
                            pe.wait_ge(y_done.sem, y_done.at(b, cb + 1))
                        for j in range(NJ):
                            ins = pe.transpose(ps[:, j // 2, (j % 2) * P:(j % 2 + 1) * P],
                                               z[:, cb, j, kt * P:(kt + 1) * P], ident)
                        close_bank(("yt", cb, kt), b, ins)

            def project1(b, name, w, m):
                for lh in range(2):
                    ps = open_bank((name, lh), b)
                    for kt in range(CB):
                        if name == "th":
                            read_by(("yt", lh, kt), b)
                        ins = pe.matmul(ps[0:m].rearrange("p a s -> p (a s)"), w[:, kt, :],
                                        zt[:, kt, lh * 512:(lh + 1) * 512], start=kt == 0, stop=kt == 1)
                    close_bank((name, lh), b, ins)

            def turn_g(b):
                ps = open_bank(("gt",), b)
                pe.wait_ge(g_bias.sem, g_bias.at(b, 1))
                for mt in range(2):
                    ins = pe.transpose(ps[:, 0, mt * P:(mt + 1) * P], g_pool[:, mt * P:(mt + 1) * P], ident)
                close_bank(("gt",), b, ins)

            def scores1(b):
                pe.wait_ge(ph_step.sem, ph_step.at(b, 3))
                read_by(("th", 0), b)
                read_by(("th", 1), b)
                for lh in range(2):
                    pe.wait_ge(s_bank.drained, s_bank.empty(b, ("l1", lh)))
                    for n in range(4):
                        ins = pe.matmul(ps_s[:, n, :], th_st[0:96, lh * 512 + n * P:lh * 512 + (n + 1) * P],
                                        ph_st[0:96, :], start=True, stop=True)
                    ins.then_inc(s_bank.filled, 1)

            def attend1(b):
                for lh in range(2):
                    ps = open_bank(("mxt1", lh), b)
                    pe.wait_ge(max1_split.sem, max1_split.at(b, lh + 1))
                    ins = pe.transpose(ps[0:8, 0, 0:P], mx_hl[:, lh].rearrange("p a h -> p (a h)").bitcast(F32), ident)
                    close_bank(("mxt1", lh), b, ins)
                for lh in range(2):
                    pe.wait_ge(max1_in[lh].sem, max1_in[lh].at(b, 1))
                    pe.wait_ge(t_bank.drained, t_bank.empty(b, ("l1", lh)))
                    for mt in range(2):
                        ins = pe.matmul(ps_t[:, 2 * mt:2 * mt + 2, :].rearrange("p a s -> p (a s)"),
                                        ph_st[0:98, mt * P:(mt + 1) * P], th_st[0:98, lh * 512:(lh + 1) * 512],
                                        start=True, stop=True)
                    ins.then_inc(t_bank.filled, 1)
                for lh in range(2):
                    ps = open_bank(("ag", lh), b)
                    pe.wait_ge(t_bank.drained, t_bank.done(b, ("l1", lh)))
                    if lh == 0:
                        read_by(("gt",), b)
                    for mt in range(2):
                        ins = pe.matmul(ps[:].rearrange("p a s -> p (a s)"), g_m[:, mt, :],
                                        prob1[:, mt, lh * 512:(lh + 1) * 512], start=mt == 0, stop=mt == 1)
                    close_bank(("ag", lh), b, ins)
                ps = open_bank(("den",), b)
                for cb in range(2):
                    for j in range(NJ):
                        n = cb * NJ + j
                        for mt in range(2):
                            ins = pe.matmul(ps[:, 0, n:n + 1], prob1[:, mt, cb * 512 + j:cb * 512 + j + 4 * P - 3:4],
                                            ones[:, 0:1], start=mt == 0, stop=mt == 1)
                close_bank(("den",), b, ins)
                for cb in range(2):
                    for jp in range(2):
                        ps = open_bank(("o", cb, jp), b)
                        if jp == 0:
                            read_by(("ag", cb), b)
                        for jj in range(2):
                            j = 2 * jp + jj
                            ins = pe.matmul(ps[:, jj, :], ag[:, cb * 512 + j:cb * 512 + j + 4 * P - 3:4], w_o[:],
                                            start=True, stop=True)
                        close_bank(("o", cb, jp), b, ins)

            def turn(b, nb):
                front = nb is not None
                for s in range(UNITS + 3):
                    if s < UNITS:
                        scores(b, s)
                    if 1 <= s <= UNITS:
                        max_rows(b, s - 1)
                    if 2 <= s <= UNITS + 1:
                        shifted(b, s - 2, 0)
                    if s >= 3:
                        values(b, s - 3)
                    if 2 <= s <= UNITS + 1:
                        shifted(b, s - 2, 1)
                    if front and s in QIMG_AT:
                        q_image(nb, QIMG_AT.index(s))
                    for cb in range(CB):
                        if front and s in (CONV_AT[cb], CONV_AT[cb] + 1):
                            conv_part(nb, cb, s - CONV_AT[cb])
                for cb in range(2):
                    project(b, cb)
                    if front:
                        if cb == 0:
                            offsets(nb)
                        queries(nb, cb)
                for cb in range(2):
                    turn_rows(b, cb)
                    mlp_rows(b, cb)
                if front:
                    sample(nb)
                turn_output(b)
                project1(b, "th", w_th, 3 * C8)
                project1(b, "ph", w_ph, 3 * C8)
                if front:
                    keys(nb)
                project1(b, "g", w_g, C2)
                turn_g(b)
                scores1(b)
                if front:
                    value_rows(nb)
                attend1(b)

            for cb in range(CB):
                q_image(0, cb)
            for cb in range(CB):
                conv_part(0, cb, 0)
                conv_part(0, cb, 1)
            offsets(0)
            queries(0, 0)
            queries(0, 1)
            sample(0)
            keys(0)
            value_rows(0)
            with pe.Fori(0, B - 1) as b:
                turn(b, b + 1)
            turn(B - 1, None)

        def await_bank(eng, key, b):
            k = use(key, b)
            eng.wait_ge(k.filled, k.full)
            return k.tile

        def drain(ins, key, b):
            ins.then_inc(use(key, b).drained, 1)

        @block.scalar
        def _(act):
            act.wait_ge(consts_in, N_CONST_IN)
            act.wait_ge(setup_dve, 13)

            def conv_gelu(b, cb):
                ps = await_bank(act, ("conv", cb), b)
                drain(act.activation(gel[:, cb, :], ps[:, 0, :], ACT.Gelu, bias=dwb_c[:, cb:cb + 1]), ("conv", cb), b)

            def offset_tanh(b):
                ps = await_bank(act, ("off",), b)
                drain(act.activation(pos[:].rearrange("p a s -> p (a s)"), ps[:].rearrange("p a s -> p (a s)"),
                                     ACT.Tanh), ("off",), b)

            def query_hi(b, hg):
                if hg:
                    act.wait_ge(q_in[0].sem, q_in[0].at(b, 3))
                else:
                    act.wait_ge(k_in.sem, k_in.before(b, 3 * NHG))
                    act.wait_ge(q_in[1].sem, q_in[1].before(b, 3))
                for jp in range(2):
                    ps = await_bank(act, ("qh", hg, jp), b)
                    act.activation(q_hi[:, jp * 512:(jp + 1) * 512], ps[:].rearrange("p a s -> p (a s)"),
                                   ACT.Identity, bias=bqh_c[:, hg:hg + 1]).then_inc(q_hi_done.sem, 1)

            def hats(b):
                act.wait_ge(pos_step.sem, pos_step.at(b, 3))
                act.activation(hat_x[:], pos[:, 1, :], ACT.Abs, bias=consts[:, K_XP:K_XP + 1]).then_inc(hat_dist.sem, 1)
                k = use(("qh", 1, 1), b)
                act.wait_ge(k.filled, k.full)
                for t in range(NT):
                    act.activation(hat[:, t, :], pos[:, 0, :], ACT.Abs,
                                   bias=consts[:, K_YP + t:K_YP + t + 1]).then_inc(hat_dist.sem, 1)
                act.wait_ge(hat_dist.sem, hat_dist.at(b, 1))
                act.activation(hat_x[:], hat_x[:], ACT.Relu, bias=1.0, scale=-1.0).then_inc(hat_relu.sem, 1)
                act.wait_ge(hat_dist.sem, hat_dist.at(b, 1 + NT))
                act.activation(hat[:], hat[:], ACT.Relu, bias=1.0, scale=-1.0).then_inc(hat_relu.sem, 1)

            def sampled(b):
                ps = await_bank(act, ("samp",), b)
                drain(act.activation(samp[:], ps[:], ACT.Copy), ("samp",), b)

            def key_hi(b):
                act.wait_ge(q_in[1].sem, q_in[1].at(b, 3))
                ps = await_bank(act, ("kh",), b)
                for hg in range(NHG):
                    ins = act.activation(k_hi[:, hg, :], ps[:, hg, :], ACT.Identity, bias=bkh_c[:, hg:hg + 1])
                ins.then_inc(k_hi_done.sem, 1)

            def max_out(b, u):
                ps = await_bank(act, ("mxt", u), b)
                if u >= 2:
                    act.wait_ge(max_in[u % 2].sem, max_in[u % 2].at(b, u // 2))
                else:
                    act.wait_ge(max_in[u % 2].sem, max_in[u % 2].before(b, UNITS // 2))
                    act.wait_ge(max1_in[u % 2].sem, max1_in[u % 2].before(b, 1))
                drain(act.activation(mx_t[:, u % 2, :], ps[0:2 * HQ, 0, :], ACT.Copy), ("mxt", u), b)

            def exps(b, u):
                for pr in range(2):
                    act.wait_ge(t_bank.filled, t_bank.full(b, (u, pr)))
                    if u < 2 and pr == 0:
                        for key in (("o", 1, 1), ("o", 1, 0), ("den",)):
                            k = ring.settled(key, b)
                            act.wait_ge(k.filled, k.full)
                    if u >= 2 and pr == 0:
                        act.wait_ge(v_bank.filled, v_bank.full(b, u - 2))
                    act.activation(prob[:, u % 2, 2 * pr:2 * pr + 2].rearrange("p h m s -> p (h m) s"), ps_t[:],
                                   ACT.Exp).then_inc(t_bank.drained, 1)

            def norm_turned(b, cb):
                for kt in range(CB):
                    ps = await_bank(act, ("znt", cb, kt), b)
                    drain(act.activation(zt[:, kt, cb * 512:(cb + 1) * 512], ps[:].rearrange("p a s -> p (a s)"),
                                         ACT.Identity, bias=lnb_c[:, kt:kt + 1], scale=lng_c[:, kt:kt + 1]),
                          ("znt", cb, kt), b)

            def mlp_gelu(b, cb):
                for jp in range(2):
                    k = use(("mlp", cb, jp), b)
                    act.wait_ge(k.drained, k.done)
                    act.activation(mid[:, cb, 2 * jp:2 * jp + 2, :], mid[:, cb, 2 * jp:2 * jp + 2, :],
                                   ACT.Gelu).then_inc(gelu_done.sem, 1)

            def output_turned(b):
                for cb in range(2):
                    for kt in range(CB):
                        ps = await_bank(act, ("yt", cb, kt), b)
                        drain(act.activation(
                            zt[:, kt, cb * 512:(cb + 1) * 512].rearrange("p (q j) -> p j q", j=NJ),
                            ps[:].rearrange("p a (c q) -> p (a c) q", c=2), ACT.Copy), ("yt", cb, kt), b)

            def theta_hi(b):
                for lh in range(2):
                    ps = await_bank(act, ("th", lh), b)
                    act.activation(th_st[0:96, lh * 512:(lh + 1) * 512], ps[0:96].rearrange("p a s -> p (a s)"),
                                   ACT.Identity, bias=bth_c[0:96]).then_inc(th_hi.sem, 1)

            def attend1(b):
                ps = await_bank(act, ("gt",), b)
                drain(act.activation(g_m[:], ps[:, 0, :].rearrange("p (m d) -> p m d", m=2), ACT.Copy), ("gt",), b)
                for lh in range(2):
                    ps = await_bank(act, ("mxt1", lh), b)
                    act.wait_ge(max_in[lh].sem, max_in[lh].at(b, UNITS // 2))
                    drain(act.activation(mx_t[:, lh, 0:P], ps[0:8, 0, 0:P], ACT.Copy), ("mxt1", lh), b)
                for lh in range(2):
                    act.wait_ge(t_bank.filled, t_bank.full(b, ("l1", lh)))
                    act.wait_ge(v_bank.filled, v_bank.full(b, UNITS - 1))
                    act.activation(prob1[:, :, lh * 512:(lh + 1) * 512],
                                   ps_t[:].rearrange("p (m a) s -> p m (a s)", m=2), ACT.Exp
                                   ).then_inc(t_bank.drained, 1)
                for lh in range(2):
                    ps = await_bank(act, ("ag", lh), b)
                    drain(act.activation(ag[:, lh * 512:(lh + 1) * 512], ps[:].rearrange("p a s -> p (a s)"),
                                         ACT.Copy), ("ag", lh), b)

            def turn(b, nb):
                front = nb is not None
                for s in range(UNITS + 3):
                    if 1 <= s <= UNITS:
                        max_out(b, s - 1)
                    if 2 <= s <= UNITS + 1:
                        exps(b, s - 2)
                if front:
                    conv_gelu(nb, 0)
                    conv_gelu(nb, 1)
                    offset_tanh(nb)
                    query_hi(nb, 0)
                    query_hi(nb, 1)
                norm_turned(b, 0)
                mlp_gelu(b, 0)
                norm_turned(b, 1)
                if front:
                    hats(nb)
                mlp_gelu(b, 1)
                if front:
                    sampled(nb)
                output_turned(b)
                theta_hi(b)
                if front:
                    key_hi(nb)
                attend1(b)

            conv_gelu(0, 0)
            conv_gelu(0, 1)
            offset_tanh(0)
            query_hi(0, 0)
            query_hi(0, 1)
            hats(0)
            sampled(0)
            key_hi(0)
            with act.Fori(0, B - 1) as b:
                turn(b, b + 1)
            turn(B - 1, None)

        @block.vector
        def _(dve):
            dve.memset(k_st[96:98, :, :].bitcast(F32), -1.0).then_inc(minus_rows, 1)
            dve.memset(ph_st[96:98, :].bitcast(F32), -1.0).then_inc(minus_rows, 1)
            dve.wait_ge(consts_in, N_CONST_IN)
            dve.tensor_copy(vec_rows[:, 1, :].rearrange("r (d h) -> r d h", h=HQ),
                            vec_rows[:, 0, :].rearrange("r (h d) -> r d h", h=HQ)).then_inc(setup_dve, 1)
            dve.tensor_copy(vec_rows[:, 2, :].rearrange("r (k c) -> r k c", k=4),
                            vec_rows[:, 0, :].rearrange("r (c k) -> r k c", k=4)).then_inc(setup_dve, 1)
            for w, wp in ((t_mq, t_mqp), (t_mk, t_mkp)):
                dve.tensor_copy(wp.rearrange("p t (g d h) -> p (t g) d h", g=NHG, h=HQ),
                                w.rearrange("p t (g h d) -> p (t g) d h", g=NHG, h=HQ)).then_inc(setup_dve, 1)
            for n, (dst, ps) in enumerate(((t_wqt, ps_d[0]), (t_wvt, ps_d[1]),
                                           (cols[:, :, 0:N_ROWS], ps_d[2][:, 0, 0:96].rearrange("p (n r) -> p n r", n=3)[:, :, 0:N_ROWS]),
                                           (w_qh, ps_s[:, 0:2, :]), (w_kh, ps_s[:, 2:4, :]), (w_vh, ps_t[:, 0:2, :]))):
                dve.wait_ge(setup_pe, n + 1)
                dve.tensor_copy(dst[:], ps[:]).then_inc(setup_dve, 1)
            dve.wait_ge(setup_pe, 7)
            dve.tensor_tensor(bqh_c, ps_v[:, 0, 0:2], mqb_c, ALU.add).then_inc(setup_dve, 1)
            dve.tensor_tensor(bkh_c, ps_v[:, 0, 2:4], mkb_c, ALU.add).then_inc(setup_dve, 1)
            dve.wait_ge(setup_pe, 8)
            dve.tensor_tensor(bvh_all[:], ps_t[:, 2, :], mvb_all[:], ALU.add).then_inc(setup_dve, 1)

            def rsqrt(sig, b, first, var, w):
                y, t, v = w[:, 1], w[:, 2], w[:, 3]
                n = [first]

                def step(ins):
                    ins.then_inc(sig.sem, 1)
                    n[0] += 1
                    dve.wait_ge(sig.sem, sig.at(b, n[0]))

                step(dve.tensor_scalar(v, var, EPS, None, ALU.add))
                step(dve.tensor_scalar(t.bitcast(I32), v.bitcast(I32), 1, None, ALU.logical_shift_right))
                step(dve.tensor_scalar(y.bitcast(I32), t.bitcast(I32), -1.0, float(0x5F3759DF), ALU.mult, ALU.add))
                for _ in range(NEWTON):
                    step(dve.tensor_tensor(t, y, y, ALU.mult))
                    step(dve.scalar_tensor_tensor(t, t, -0.5, v, ALU.mult, ALU.mult))
                    step(dve.scalar_tensor_tensor(y, t, 1.5, y, ALU.add, ALU.mult))

            def row_stats(b):
                dve.wait_ge(xa_in.sem, xa_in.at(b, 1))
                dve.wait_ge(xln_ready.sem, xln_ready.before(b, 2))
                for t in range(NT):
                    dve.bn_stats(st1[:, t, :], xa[:, t, :]).then_inc(ln1_stat.sem, 1)

            def row_deviation(b):
                dve.wait_ge(ln1_stat.sem, ln1_stat.at(b, NT))
                gate(dve, "dve")
                for t in range(NT):
                    dve.bn_aggr(mv1[:, t, :], st1[:, t, :]).then_inc(ln1_aggr.sem, 1)
                dve.wait_ge(ln1_aggr.sem, ln1_aggr.at(b, NT))
                rsqrt(rsqrt1, b, 0, mv1[:, :, 1], rs1)

            def row_norm(b, half):
                part = xln[:, half * NJ:(half + 1) * NJ, :]
                dve.wait_ge(ln1_norm.sem, ln1_norm.at(b, (half + 1) * NJ))
                dve.tensor_tensor(part, part, over_rows(lng_all, NJ), ALU.mult).then_inc(ln1_scaled.sem, 1)
                dve.wait_ge(ln1_scaled.sem, ln1_scaled.at(b, half + 1))
                dve.tensor_tensor(part, part, over_rows(lnb_all, NJ), ALU.add).then_inc(xln_ready.sem, 1)

            def q_image(b, cb):
                for jp in range(2):
                    if jp == 0:
                        for c in range(CB):
                            k = ring.settled(("conv", c), b)
                            dve.wait_ge(k.filled, k.full)
                    ps = await_bank(dve, ("qimg", cb, jp), b)
                    drain(dve.tensor_tensor(
                        qpad[:, cb, :, 8 * jp + 2:8 * jp + 10, KS // 2:KS // 2 + W],
                        ps[:].rearrange("p a (r q x) -> p q (a r) x", q=2, x=W),
                        bq_all[:].rearrange("p a (r q x) -> p q (a r) x", q=2, x=W), ALU.add), ("qimg", cb, jp), b)

            def query_lo(b, hg):
                for jp in range(2):
                    ps = await_bank(dve, ("qh", hg, jp), b)
                    n = slice(jp * 512, (jp + 1) * 512)
                    dve.wait_ge(q_hi_done.sem, q_hi_done.at(b, 2 * hg + jp + 1))
                    drain(dve.scalar_tensor_tensor(q_lo[:, n], ps[:].rearrange("p a s -> p (a s)"),
                                                   bqh_c[:, hg:hg + 1], q_hi[:, n].bitcast(F32), ALU.add,
                                                   ALU.subtract), ("qh", hg, jp), b)

            def positions(b):
                k = use(("off",), b)
                flat = pos[:].rearrange("p a s -> p (a s)")
                dve.wait_ge(k.drained, k.done)
                dve.tensor_tensor(flat, flat, refs, ALU.add).then_inc(pos_step.sem, 1)
                dve.wait_ge(pos_step.sem, pos_step.at(b, 1))
                dve.tensor_scalar(flat, flat, 1.0, float(H // R) / 2.0, ALU.add, ALU.mult).then_inc(pos_step.sem, 1)
                dve.wait_ge(pos_step.sem, pos_step.at(b, 2))
                dve.tensor_scalar(flat, flat, 1.0, 0.5 * (W - 1), ALU.add, ALU.mult).then_inc(pos_step.sem, 1)

            def hats(b):
                dve.wait_ge(hat_relu.sem, hat_relu.at(b, 2))
                dve.tensor_tensor(hat[:], hat[:], hat_x[:].rearrange("p (a s) -> p a s", a=1).broadcast_to([P, NT, S_]),
                                  ALU.mult).then_inc(hat_done.sem, 1)

            def key_lo(b):
                ps = await_bank(dve, ("kh",), b)
                dve.wait_ge(k_hi_done.sem, k_hi_done.at(b, 1))
                for hg in range(NHG):
                    ins = dve.scalar_tensor_tensor(k_lo[:, hg, :], ps[:, hg, :], bkh_c[:, hg:hg + 1],
                                                   k_hi[:, hg, :].bitcast(F32), ALU.add, ALU.subtract)
                drain(ins, ("kh",), b)

            def value_rows(b):
                ps = await_bank(dve, ("vh",), b)
                drain(dve.tensor_tensor(vh[:], ps[:], over_rows(bvh_all, 2), ALU.add), ("vh",), b)

            def maxima(b, u):
                if u:
                    dve.wait_ge(max_split.sem, max_split.at(b, u))
                else:
                    dve.wait_ge(max1_split.sem, max1_split.before(b, 2))
                for cb in range(2):
                    dve.wait_ge(s_bank.filled, s_bank.full(b, (u, cb)))
                    dve.tensor_reduce(mx[:, cb, :], ps_s[:], AX.X, ALU.max).then_inc(s_bank.drained, 1)
                dve.wait_ge(s_bank.drained, s_bank.done(b, (u, 1)))
                if u:
                    k = use(("mxt", u - 1), b)
                    dve.wait_ge(k.filled, k.full)
                else:
                    for lh in range(2):
                        k = ring.settled(("mxt1", lh), b)
                        dve.wait_ge(k.filled, k.full)
                dve.tensor_copy(mx_hl[:, :, 0, :], mx[:]).then_inc(max_hi.sem, 1)
                dve.wait_ge(max_hi.sem, max_hi.at(b, u + 1))
                dve.tensor_tensor(mx_hl[:, :, 1, :], mx[:], mx_hl[:, :, 0, :].bitcast(F32),
                                  ALU.subtract).then_inc(max_split.sem, 1)

            def normalise(b, u):
                hg, j = divmod(u, NJ)
                dve.wait_ge(v_bank.filled, v_bank.full(b, u))
                dve.reciprocal(rden[:], ps_v[:, 1, :]).then_inc(rden_done.sem, 1)
                dve.wait_ge(rden_done.sem, rden_done.at(b, u + 1))
                dve.tensor_tensor(att[:, hg, j * S_:(j + 1) * S_], ps_v[:, 0, :], rden[:],
                                  ALU.mult).then_inc(v_bank.drained, 1)

            def residual(b, cb):
                for jp in range(2):
                    ps = await_bank(dve, ("z", cb, jp), b)
                    if cb == 0 and jp == 0:
                        dve.wait_ge(xb_biased.sem, xb_biased.at(b, 1))
                        dve.wait_ge(out_stored.sem, out_stored.before(b, 1))
                    ins = dve.tensor_tensor(z[:, cb, 2 * jp:2 * jp + 2, :], ps[:], xb[:, cb, 2 * jp:2 * jp + 2, :],
                                            ALU.add)
                    drain(ins, ("z", cb, jp), b)
                    k = use(("z", cb, jp), b)
                    dve.wait_ge(k.drained, k.done)
                    for jj in range(2):
                        n = cb * NJ + 2 * jp + jj
                        dve.bn_stats(st2[:, n, :], z[:, cb, 2 * jp + jj, :]).then_inc(ln2_stat.sem, 1)
                dve.wait_ge(ln2_stat.sem, ln2_stat.at(b, (cb + 1) * NJ))
                gate(dve, "dve")
                for j in range(NJ):
                    n = cb * NJ + j
                    dve.bn_aggr(mv2[:, n, :], st2[:, n, :]).then_inc(ln2_aggr.sem, 1)
                dve.wait_ge(ln2_aggr.sem, ln2_aggr.at(b, (cb + 1) * NJ))
                rsqrt(rsqrt2, b, cb * RSQRT_STEPS, mv2[:, cb * NJ:(cb + 1) * NJ, 1], rs2[:, cb])
                dve.wait_ge(y_done.sem, y_done.before(b, cb + 1))
                for j in range(NJ):
                    n = cb * NJ + j
                    dve.tensor_scalar(zn[:, cb, j, :], z[:, cb, j, :], mv2[:, n, 0:1], rs2[:, cb, 1, j:j + 1],
                                      ALU.subtract, ALU.mult).then_inc(zn_done.sem, 1)

            def mlp_bias(b, cb):
                for jp in range(2):
                    ps = await_bank(dve, ("mlp", cb, jp), b)
                    drain(dve.tensor_tensor(mid[:, cb, 2 * jp:2 * jp + 2, :], ps[:], over_rows(mlpb_all, 2),
                                            ALU.add), ("mlp", cb, jp), b)

            def theta_lo(b):
                for lh in range(2):
                    ps = await_bank(dve, ("th", lh), b)
                    dve.wait_ge(th_hi.sem, th_hi.at(b, lh + 1))
                    rows = th_st[C8:2 * C8, lh * 512:(lh + 1) * 512]
                    drain(dve.scalar_tensor_tensor(rows, ps[C8:2 * C8].rearrange("p a s -> p (a s)"),
                                                   bth_c[C8:2 * C8], rows.bitcast(F32), ALU.add, ALU.subtract),
                          ("th", lh), b)

            def pooled(b, name, dst, m):
                for lh in range(2):
                    ps = await_bank(dve, (name, lh), b)
                    drain(dve.tensor_reduce(
                        dst[0:m, lh * P:(lh + 1) * P].rearrange("p (y x) -> p y x", x=W // 2),
                        ps[0:m].rearrange("p a s -> p (a s)").rearrange("p (y i x k) -> p y x i k", i=2, k=2, x=W // 2),
                        AX.XY, ALU.max), (name, lh), b)
                for lh in range(2):
                    k = use((name, lh), b)
                    dve.wait_ge(k.drained, k.done)

            def phi(b):
                pooled(b, "ph", ph_pool, 3 * C8)
                dve.tensor_scalar(ph_pool[0:96], ph_pool[0:96], bph_c[0:96], None, ALU.add).then_inc(ph_step.sem, 1)
                dve.wait_ge(ph_step.sem, ph_step.at(b, 1))
                dve.tensor_copy(ph_st[0:96], ph_pool[0:96]).then_inc(ph_step.sem, 1)
                dve.wait_ge(ph_step.sem, ph_step.at(b, 2))
                dve.tensor_tensor(ph_st[64:96], ph_pool[64:96], ph_st[64:96].bitcast(F32),
                                  ALU.subtract).then_inc(ph_step.sem, 1)

            def g_rows(b):
                pooled(b, "g", g_pool, C2)
                dve.tensor_scalar(g_pool[:], g_pool[:], bg_c, None, ALU.add).then_inc(g_bias.sem, 1)

            def maxima1(b):
                for lh in range(2):
                    dve.wait_ge(s_bank.filled, s_bank.full(b, ("l1", lh)))
                    k = use(("mxt", UNITS - 1), b)
                    dve.wait_ge(k.filled, k.full)
                    dve.wait_ge(max_split.sem, max_split.at(b, UNITS))
                    dve.tensor_reduce(mx[:, lh, :], ps_s[:], AX.X, ALU.max).then_inc(s_bank.drained, 1)
                    dve.wait_ge(s_bank.drained, s_bank.done(b, ("l1", lh)))
                    dve.tensor_copy(mx_hl[:, lh, 0, :], mx[:, lh, :]).then_inc(max1_hi.sem, 1)
                    dve.wait_ge(max1_hi.sem, max1_hi.at(b, lh + 1))
                    dve.tensor_tensor(mx_hl[:, lh, 1, :], mx[:, lh, :], mx_hl[:, lh, 0, :].bitcast(F32),
                                      ALU.subtract).then_inc(max1_split.sem, 1)

            def result(b):
                ps = await_bank(dve, ("den",), b)
                drain(dve.reciprocal(rd1[:], ps[:, 0, 0:NT]), ("den",), b)
                k = use(("den",), b)
                dve.wait_ge(k.drained, k.done)
                dve.tensor_scalar(rd1[:], rd1[:], sg_c, None, ALU.mult).then_inc(rd1_step.sem, 1)
                dve.wait_ge(rd1_step.sem, rd1_step.at(b, 1))
                for cb in range(2):
                    dve.wait_ge(ybo_done.sem, ybo_done.at(b, cb + 1))
                    for jp in range(2):
                        ps = await_bank(dve, ("o", cb, jp), b)
                        for jj in range(2):
                            j = 2 * jp + jj
                            n = cb * NJ + j
                            ins = dve.scalar_tensor_tensor(z[:, cb, j, :], ps[:, jj, :], rd1[:, n:n + 1],
                                                           z[:, cb, j, :], ALU.mult, ALU.add)
                        drain(ins, ("o", cb, jp), b)

            def turn(b, nb):
                front = nb is not None
                for s in range(UNITS + 3):
                    if s < UNITS:
                        maxima(b, s)
                    if s >= 3:
                        normalise(b, s - 3)
                    if front:
                        if s == 0:
                            row_stats(nb)
                        if s == 1:
                            row_deviation(nb)
                        if s == 2:
                            row_norm(nb, 0)
                            row_norm(nb, 1)
                        if s in QIMG_AT:
                            q_image(nb, QIMG_AT.index(s))
                residual(b, 0)
                if front:
                    positions(nb)
                    query_lo(nb, 0)
                residual(b, 1)
                if front:
                    query_lo(nb, 1)
                mlp_bias(b, 0)
                if front:
                    hats(nb)
                mlp_bias(b, 1)
                theta_lo(b)
                phi(b)
                if front:
                    key_lo(nb)
                g_rows(b)
                maxima1(b)
                if front:
                    value_rows(nb)
                result(b)

            row_stats(0)
            row_deviation(0)
            row_norm(0, 0)
            row_norm(0, 1)
            q_image(0, 0)
            q_image(0, 1)
            positions(0)
            query_lo(0, 0)
            query_lo(0, 1)
            hats(0)
            key_lo(0)
            value_rows(0)
            with dve.Fori(0, B - 1) as b:
                turn(b, b + 1)
            turn(B - 1, None)

        @block.gpsimd
        def _(pool):
            pool.memset(dw_g[:], 0.0).then_inc(setup_pool, 1)
            pool.memset(vec_rows[:], 0.0).then_inc(setup_pool, 1)
            pool.memset(qpad[:], 0.0).then_inc(setup_pool, 1)
            pool.memset(ones[:], 1.0).then_inc(setup_pool, 1)
            pool.wait_ge(consts_in, N_CONST_IN)
            pool.wait_ge(setup_dve, 7)
            pool.tensor_copy(t_bv, bv_c.rearrange("p (t a) -> p t a", a=1).broadcast_to([P, 2, P])).then_inc(setup_pool, 1)
            pool.tensor_copy(pw_all[:].rearrange("p t o c -> p (t o) c"),
                             pw_c.rearrange("p (t a) -> p t a", a=1).broadcast_to([P, 4, P])).then_inc(setup_pool, 1)
            pool.tensor_tensor(
                conv_w[:].rearrange("p k h x c -> p (k h x) c"),
                dw_g[:].rearrange("p k h (x a) -> p (k h x) a", a=1).broadcast_to([P, 8 * 2 * KS, 32]),
                consts[:, K_M32:K_M32 + 32].rearrange("p (a c) -> p a c", a=1).broadcast_to([P, 8 * 2 * KS, 32]),
                ALU.mult).then_inc(setup_pool, 1)
            pool.tensor_scalar(bo_all[:], bo_all[:], sg_c, None, ALU.mult).then_inc(setup_pool, 1)
            pool.wait_ge(setup_pool, 8)

            def row_norm(b):
                pool.wait_ge(rsqrt1.sem, rsqrt1.at(b, RSQRT_STEPS))
                k = ring.settled(("samp",), b)
                pool.wait_ge(k.drained, k.done)
                gate(pool, "pool")
                for t in range(NT):
                    pool.tensor_scalar(xln[:, t, :], xa[:, t, :], mv1[:, t, 0:1], rs1[:, 1, t:t + 1], ALU.subtract,
                                       ALU.mult).then_inc(ln1_norm.sem, 1)

            def turn(b, nb):
                if nb is not None:
                    row_norm(nb)
                pool.wait_ge(xb_in.sem, xb_in.at(b, 1))
                flat = xb[:].rearrange("p k j c -> p (k j) c")
                pool.tensor_tensor(flat, flat, over_rows(mob_all, NT), ALU.add).then_inc(xb_biased.sem, 1)
                for cb in range(2):
                    pool.wait_ge(gelu_done.sem, gelu_done.at(b, 2 * cb + 2))
                    pool.tensor_tensor(z[:, cb], z[:, cb], mid[:, cb], ALU.add).then_inc(y_done.sem, 1)
                for cb in range(2):
                    for kt in range(CB):
                        k = use(("yt", cb, kt), b)
                        pool.wait_ge(k.filled, k.full)
                        gate(pool, "pool")
                    pool.tensor_tensor(z[:, cb], z[:, cb], over_rows(bo_all, NJ), ALU.add).then_inc(ybo_done.sem, 1)

            row_norm(0)
            with pool.Fori(0, B - 1) as b:
                turn(b, b + 1)
            turn(B - 1, None)


_INS = ['x', 'L0_conv_ln_g', 'L0_conv_ln_b', 'L0_conv_wq', 'L0_conv_bq', 'L0_conv_wv', 'L0_conv_bv', 'L0_conv_dw_w',
        'L0_conv_dw_b', 'L0_conv_pw_w', 'L0_conv_mq_w', 'L0_conv_mq_b', 'L0_conv_mk_w', 'L0_conv_mk_b',
        'L0_conv_mv_w', 'L0_conv_mv_b', 'L0_conv_mo_w', 'L0_conv_mo_b', 'L0_conv_mlp_w', 'L0_conv_mlp_b',
        'L1_conv_w_theta', 'L1_conv_b_theta', 'L1_conv_w_phi', 'L1_conv_b_phi', 'L1_conv_w_g', 'L1_conv_b_g',
        'L1_conv_w_o', 'L1_conv_b_o', 'L1_conv_sigma']


def kernel(**inputs):
    import numpy as _np
    import concourse.bacc as _bacc
    from concourse import mybir as _mybir
    from concourse.bass_utils import run_bass_kernel_spmd as _run

    nc = _bacc.Bacc("TRN2", target_bir_lowering=False, num_devices=1)
    arrays, aps = {}, {}
    given = {name: _np.ascontiguousarray(inputs[name]) for name in _INS}
    given["L1_conv_sigma"] = given["L1_conv_sigma"].reshape(1)
    given["shape_constants"] = shape_constants()
    for name, v in given.items():
        arrays[f"in_{name}_dram"] = v
        aps[name] = nc.dram_tensor(f"in_{name}_dram", v.shape, _mybir.dt.from_np(v.dtype), kind="ExternalInput").ap()
    out = nc.dram_tensor("out_0_dram", (B, H, W, C), F32, kind="ExternalOutput").ap()
    build(nc, aps, out)
    r = _run(nc, [arrays], core_ids=[0])
    return r.results[0]["out_0_dram"]
```

```python
from contextlib import ExitStack

import numpy as np

import concourse.bass as bass
from concourse import mybir

F32 = mybir.dt.float32
F32R = mybir.dt.float32r
I32 = mybir.dt.int32
ALU = mybir.AluOpType
ACT = mybir.ActivationFunctionType
AX = mybir.AxisListType

P = 128
B, H, W, C = 4, 32, 32, 256
HW = H * W
NT = HW // P
CB = C // P
R, KS = 2, 7
HG_, WG_ = H // R, W // R
S_ = HG_ * WG_
NH = 8
HD = C // NH
HQ = P // HD
NHG = NH // HQ
NJ = HW // C
C8, C2 = C // 8, C // 2
EPS = 1e-5
PADW = W + 2 * (KS // 2)
PLANE = 20
CROWS = HG_ + 2
UNITS = NHG * NJ
STEPS = UNITS + 3
NEWTON = 3
RSQRT_STEPS = 3 + 3 * NEWTON
QIMG_AT = (3, 4)
CONV_AT = (5, 8)
QUERY_AT = {6: (0, 0), 7: (0, 1)}
MLP_AT = (-1, 1)
MLP_GELU_AT = (0, 1)
NORM_TURN_AT = 0
OUT_TURN_AT = 2
THETA_PHI_AT = 3
G_AT, G_TURN_AT = 5, 6
SCORES1_AT = (5, 6)
MAX1_AT = 7
SHIFTED1_AT = (8, 9)
ATTEND1_AT = STEPS - 1
N_ROWS = 21

K_ID = 0
K_REF = K_ID + P
K_XP = K_REF + 2 * S_
K_YP = K_XP + 1
K_M32 = K_YP + NT
K_N = K_M32 + 32


def shape_constants():
    k = np.zeros((P, K_N), np.float32)
    p = np.arange(P)
    k[:, K_ID:K_ID + P] = np.eye(P)
    ref_x = (np.arange(WG_, dtype=np.float32) + np.float32(0.5)) * np.float32(2.0 / WG_) - np.float32(1.0)
    ref_y = (np.arange(HG_, dtype=np.float32) + np.float32(0.5)) * np.float32(2.0 / HG_) - np.float32(1.0)
    k[:, K_REF:K_REF + S_] = np.repeat(ref_x, HG_)[None]
    k[:, K_REF + S_:K_REF + 2 * S_] = np.tile(ref_y, WG_)[None]
    k[:, K_XP] = -(p % W)
    for t in range(NT):
        k[:, K_YP + t] = -((P // W) * t + p // W)
    k[:, K_M32:K_M32 + 32] = (p[:, None] % 32 == np.arange(32)[None])
    return k


class Signal:

    def __init__(self, sem, per, unit=1, credit=False):
        self.sem, self.per, self.unit = sem, per, unit
        self.start = per * unit if credit else 0

    def at(self, b, n):
        return b * (self.per * self.unit) + (self.start + n * self.unit)

    def before(self, b, n):
        assert self.start and n >= 1
        return b * (self.per * self.unit) + (self.start + (n - self.per) * self.unit)


class Bank:

    def __init__(self, filled, drained, uses):
        self.filled, self.drained = filled, drained
        self.uses = {key: n for n, key in enumerate(uses)}
        assert len(self.uses) == len(uses)

    def full(self, b, key):
        return b * len(self.uses) + (self.uses[key] + 2)

    def empty(self, b, key):
        return b * len(self.uses) + (self.uses[key] + 1)

    def done(self, b, key):
        return b * len(self.uses) + (self.uses[key] + 2)


class Use:

    def __init__(self, tile, filled, drained, before):
        self.tile, self.filled, self.drained = tile, filled, drained
        self.empty = before + 1
        self.full = before + 2
        self.done = before + 2


class Ring:

    def __init__(self, tiles, filled, drained, first, body, last, held=None):
        self.filled, self.drained = filled, drained
        self.tiles = tiles
        self.bank, holds, k = {}, {}, 0
        for key, _ in body:
            holds = {bank: until for bank, until in holds.items() if until != key}
            while k in holds:
                k = (k + 1) % len(tiles)
            self.bank[key] = k
            if key in (held or {}):
                holds[k] = held[key]
            k = (k + 1) % len(tiles)
        self.segments = {"first": first, "body": body, "last": last}
        self.delta = dict(body)

    def count(self, segment, k, until=None):
        order = self.segments[segment]
        return sum(self.bank[key] == k for key, _ in (order if until is None else order[:order.index(until)]))

    def turns_before(self, turn, k):
        if isinstance(turn, int) and turn == 0:
            return 0
        return (turn - 1) * self.count("body", k) + self.count("first", k)

    def make(self, k, before):
        return Use(self.tiles[k], self.filled[k], self.drained[k], before)

    def use(self, key, image):
        k = self.bank[key]
        turn, delta = image - self.delta[key], self.delta[key]
        if isinstance(image, int):
            if delta == 1 and image == 0:
                turn, delta = 0, 0
            if delta == -1 and image == B - 1:
                turn, delta = B - 1, 0
            segment = "first" if turn == 0 else "last" if turn == B - 1 else "body"
        else:
            segment = "body"
        return self.make(k, self.count(segment, k, (key, delta)) + self.turns_before(turn, k))

    def previous(self, key, image):
        k = self.bank[key]
        if isinstance(image, int):
            return self.make(k, -1) if image == 0 else self.use(key, image - 1)
        entry = (key, self.delta[key])
        after = min(self.count(segment, k) - self.count(segment, k, entry) for segment in ("first", "body")
                    if entry in self.segments[segment])
        return self.make(k, self.turns_before(image - self.delta[key], k) - after)


def build(nc, a, out):
    x_rows = a["x"].rearrange("b h w c -> b (h w) c")
    out_rows = out.rearrange("b h w c -> b (h w) c")

    ctx = ExitStack()
    with ctx:
        def sb(name, shape, dt=F32):
            return ctx.enter_context(nc.sbuf_tensor(name, shape, dt))

        def sem(name):
            return ctx.enter_context(nc.semaphore(name))

        consts = sb("consts", [P, K_N])
        ident = consts[:, K_ID:K_ID + P]
        refs = consts[:, K_REF:K_REF + 2 * S_]
        wq = sb("wq", [P, CB, C])
        w_qh = sb("w_qh", [P, CB, C])
        w_kh = sb("w_kh", [P, CB, C])
        w_vh = sb("w_vh", [P, CB, C])
        mo = sb("mo", [P, CB, C])
        mlp = sb("mlp", [P, CB, C])
        w_tp = sb("w_tp", [P, CB, 2 * C8])
        w_g = sb("w_g", [P, CB, C2])
        w_o = sb("w_o", [P, C])
        bq_all = sb("bq_all", [P, 2, C])
        lng_all = sb("lng_all", [P, C])
        lnb_all = sb("lnb_all", [P, C])
        mob_all = sb("mob_all", [P, C])
        mlpb_all = sb("mlpb_all", [P, C])
        bo_all = sb("bo_all", [P, C])
        bvh_all = sb("bvh_all", [P, C])
        cols = sb("cols", [P, 3, 32])
        bq_c, bv_c = cols[:, 0, 0:2], cols[:, 0, 2:4]
        mqb_c, mkb_c = cols[:, 1, 4:6], cols[:, 1, 6:8]
        lng_c, lnb_c, dwb_c = cols[:, 0, 8:10], cols[:, 0, 10:12], cols[:, 2, 12:14]
        pw_c = cols[:, 2, 14:18]
        bth_c, bph_c, bg_c = cols[:, 0, 18:19], cols[:, 0, 19:20], cols[:, 0, 20:21]
        sigma = sb("sigma", [P, 1])
        bqh_c, bkh_c = cols[:, 0, 22:24], cols[:, 0, 24:26]
        pw_all = sb("pw_all", [P, CB, 2, P])
        conv_w = sb("conv_w", [P, 8, 2, KS, 32])
        ones = sb("ones", [P, 32])

        xa = sb("xa", [P, NT, C])
        xln = sb("xln", [P, NT, C])
        hat = xln
        qpad = sb("qpad", [P, CB, 2, PLANE, PADW])
        cstack = sb("cstack", [P, 4, CROWS, PADW])
        gel = sb("gel", [P, CB, S_])
        pos = sb("pos", [P, 2, S_])
        hat_x = sb("hat_x", [P, S_])
        samp = sb("samp", [P, CB, C])
        q_hi = sb("q_hi", [P, HW], F32R)
        q_lo = sb("q_lo", [P, HW], F32R)
        q_hi1, q_lo1 = [cstack[:].rearrange("p k r x -> p (k r x)")[:, n * HW:(n + 1) * HW].bitcast(F32R) for n in range(2)]
        q_parts = [(q_hi[:], q_lo[:]), (q_hi1, q_lo1)]
        k_hi = q_hi[:, 0:NHG * S_].rearrange("p (g s) -> p g s", g=NHG)
        k_lo = q_lo[:, 0:NHG * S_].rearrange("p (g s) -> p g s", g=NHG)
        st1 = sb("st1", [P, NT, 6])
        mv1 = sb("mv1", [P, NT, 2])
        rs1 = sb("rs1", [P, 4, NT])
        k_st = sb("k_st", [P, HQ, NHG, S_], F32R)
        q_st = sb("q_st", [P, NH, HW], F32R)
        vh = sb("vh", [P, 2, C])
        mx = sb("mx", [P, 2, HQ])
        mx_hl = sb("mx_hl", [P, 2, 2, HQ], F32R)
        mx_t = sb("mx_t", [2 * HQ, 2, 2 * P], F32R)
        prob = sb("prob", [P, 2, HQ, 2, S_])
        rden = sb("rden", [P, S_])
        rden_one = sb("rden_one", [P, S_ // 32])
        rden_cols = sb("rden_cols", [P, S_])
        att = sb("att", [P, NHG, HW])
        xb = sb("xb", [P, 2, NJ, C])
        z = sb("z", [P, 2, NJ, C])
        zn = sb("zn", [P, 2, NJ, C])
        mid = zn
        st2 = sb("st2", [P, NT, 6])
        mv2 = sb("mv2", [P, NT, 2])
        rs2 = sb("rs2", [P, 4, NT])
        zt = sb("zt", [P, CB, HW])
        th_st = sb("th_st", [P, HW], F32R)
        ph_pool = sb("ph_pool", [P, S_])
        ph_st = sb("ph_st", [P, S_], F32R)
        g_pool = ph_pool
        g_m = sb("g_m", [P, 2, C2])
        rd1 = sb("rd1", [P, NT])
        mx1 = sb("mx1", [P, 2, 4])
        mx1_hl = sb("mx1_hl", [P, 2, 2, 4], F32R)
        mx1_t = sb("mx1_t", [8, 2, P], F32R)
        prob1 = zn[:].rearrange("p m j c -> p m (j c)")
        ag = zt[:, 0, :]

        prob_sum = [samp, pos]

        tmp = prob[:].rearrange("p a h m s -> p (a h m s)")
        t_wv, t_mqp, t_mkp, t_mv, t_wqt, t_wvt = [
            tmp[:, n * 512:(n + 1) * 512].rearrange("p (t c) -> p t c", t=2) for n in range(6)]
        t_bv = tmp[:, 3072:3072 + 256].rearrange("p (t c) -> p t c", t=2)
        t_mq = zt[:, 0, 0:512].rearrange("p (t c) -> p t c", t=2)
        t_mk = zt[:, 0, 512:1024].rearrange("p (t c) -> p t c", t=2)
        mvb_all = zt[:, 1, 0:C]
        vec_rows = zt[0:N_ROWS, 1, C:C + 3 * P].rearrange("p (n c) -> p n c", n=3)
        dw_g = zt[:, 1, 640:640 + 16 * KS].rearrange("p (k h x) -> p k h x", k=8, h=2)

        ps_s = ctx.enter_context(nc.psum_tensor("ps_s", [P, 4, S_], F32))
        ps_t = ctx.enter_context(nc.psum_tensor("ps_t", [P, 4, S_], F32))
        ps_v = ctx.enter_context(nc.psum_tensor("ps_v", [P, 2, S_], F32))
        ps_d = [ctx.enter_context(nc.psum_tensor(f"ps_d{k}", [P, 2, S_], F32)) for k in range(3)]

        two = range(2)
        qimg = [[("qimg", cb, jp) for jp in two] for cb in range(CB)]
        qh = [[("qh", hg, jp) for jp in two] for hg in range(NHG)]
        conv = [("conv", cb) for cb in range(CB)]
        front_order = qimg[0] + qimg[1] + conv + qh[0] + [("off",)] + qh[1] + [("samp",), ("kh",), ("vh",)]
        l1_order = {MLP_AT[0]: [("mlp", 0, jp) for jp in two], NORM_TURN_AT: [("znt", 1, k) for k in range(CB)],
                    MLP_AT[1]: [("mlp", 1, jp) for jp in two],
                    OUT_TURN_AT: [("yt", cb, k) for cb in two for k in range(CB)],
                    THETA_PHI_AT: [("tp", lh) for lh in two], G_AT: [("g", lh) for lh in two],
                    G_TURN_AT: [("gt",)], MAX1_AT: [("mxt1", lh) for lh in two],
                    ATTEND1_AT: ([("ag", lh) for lh in two] + [("den",)] +
                                 [("o", cb, jp) for cb in two for jp in two])}

        def keyed(keys, delta):
            return [(key, delta) for key in keys]

        def in_turn(l1, front):
            order = keyed(l1_order[MLP_AT[0]] if l1 else [], -1)
            for s in range(STEPS):
                order += keyed([("mxt", s - 1)] if 1 <= s <= UNITS else [], 0)
                if l1 and s == THETA_PHI_AT:
                    order += keyed(l1_order[s], -1)
                if front:
                    for cb in range(CB):
                        order += keyed(qimg[cb] if s == QIMG_AT[cb] else [], 1)
                        order += keyed([conv[cb]] if s == CONV_AT[cb] else [], 1)
                    order += keyed([("qh", *QUERY_AT[s])] if s in QUERY_AT else [], 1)
                    order += keyed(qh[1] + [("off",)] if s == STEPS - 1 else [], 1)
                if l1 and s != THETA_PHI_AT:
                    order += keyed(l1_order.get(s, []), -1)
            order += keyed([("z", cb, jp) for cb in two for jp in two], 0)
            order += keyed([("samp",)] if front else [], 1)
            order += keyed([("znt", 0, k) for k in range(CB)], 0)
            order += keyed([("kh",), ("vh",)] if front else [], 1)
            return order

        def score_order(units, l1):
            return [x for s in range(STEPS) for x in keyed(units.get(s, []), 0) + keyed(l1.get(s, []), -1)]

        s_units = {s: [("s", s, cb) for cb in two] for s in range(UNITS)}
        t_units = {s: [("t", s - 2, pr) for pr in two] for s in range(2, UNITS + 2)}
        s_l1 = {SCORES1_AT[lh]: [("s1", lh)] for lh in two}
        t_l1 = {SHIFTED1_AT[lh]: [("t1", lh)] for lh in two}
        l1_last = keyed([key for s in sorted(l1_order) for key in l1_order[s]], 0)
        ring = Ring(ps_d, [sem(f"dense{k}_filled") for k in range(3)], [sem(f"dense{k}_drained") for k in range(3)],
                    keyed(front_order, 0) + in_turn(False, True), in_turn(True, True), in_turn(True, False) + l1_last,
                    held={("conv", 0): ("qh", 0, 0), ("conv", 1): ("qh", 1, 0)})
        use = ring.use
        s_ring, t_ring = [
            Ring([ps], [sem(f"{name}_filled")], [sem(f"{name}_drained")], score_order(units, {}),
                 score_order(units, l1), score_order(units, l1) + keyed([key for n in sorted(l1) for key in l1[n]], 0))
            for ps, name, units, l1 in ((ps_s, "scores", s_units, s_l1), (ps_t, "shifted", t_units, t_l1))]
        v_bank = Bank(sem("values_filled"), sem("values_drained"), list(range(UNITS)))

        signals = []

        def signal(name, per, unit=1, credit=False):
            s = Signal(sem(name), per, unit, credit)
            signals.append(s)
            return s

        setup_pe = sem("setup_products")
        setup_dve = sem("setup_copies")
        setup_pool = sem("setup_fills")
        minus_rows = sem("minus_rows")
        D_ORDERS, D_WQT, D_COLS, D_MKP, D_WVT, D_QUERY, D_ALL = 2, 3, 4, 6, 7, 10, 13
        xa_in = signal("xa_in", 1, 16)
        xb_in = signal("xb_in", 1, 16)
        xb_biased = signal("xb_biased", 2)
        ln1_stat = signal("ln1_stat", NT, credit=True)
        ln1_aggr = signal("ln1_aggr", NT)
        rsqrt1 = signal("rsqrt1", RSQRT_STEPS + 1, credit=True)
        ln1_norm = signal("ln1_norm", NT)
        ln1_scaled = signal("ln1_scaled", 2)
        xln_ready = signal("xln_ready", 2, credit=True)
        conv_in = [signal(f"conv_in{cb}", 4, 16) for cb in range(CB)]
        conv_done = signal("conv_gelu", CB)
        pos_step = signal("pos_step", 3)
        hat_dist = signal("hat_dist", 1 + NT)
        hat_relu = signal("hat_relu", 2)
        hat_done = signal("hat_done", 1)
        k_hi_done = signal("k_hi_done", 1)
        k_in = signal("k_in", 3, 16, credit=True)
        q_hi_done = signal("q_hi_done", NHG * 2)
        q_in = [signal(f"q_in{hg}", 3, 16, credit=True) for hg in range(NHG)]
        max_hi = signal("max_hi", UNITS)
        max_split = signal("max_split", UNITS, credit=True)
        max_in = [signal(f"max_in{k}", UNITS // 2, 16, credit=True) for k in range(2)]
        prob_summed = signal("prob_summed", 2 * UNITS)
        den_turned = signal("den_turned", UNITS)
        den_inv = signal("den_inv", UNITS)
        den_spread = signal("den_spread", UNITS)
        rden_done = signal("rden_done", UNITS)
        ln2_stat = signal("ln2_stat", NT, credit=True)
        ln2_aggr = signal("ln2_aggr", NT)
        rsqrt2 = signal("rsqrt2", RSQRT_STEPS, credit=True)
        zn_done = signal("zn_done", NT)
        gelu_done = signal("mlp_gelu", 4)
        y_done = signal("y_done", 2, credit=True)
        ybo_done = signal("ybo_done", 2)
        th_hi = signal("th_hi", 4)
        th_lo = signal("th_lo", 2)
        ph_step = signal("ph_step", 4)
        g_bias = signal("g_bias", 1)
        max1_hi = signal("max1_hi", 2)
        max1_split = signal("max1_split", 2, credit=True)
        max1_in = [signal(f"max1_in{k}", 1, 16, credit=True) for k in range(2)]
        rd1_step = signal("rd1_step", 2)
        out_stored = signal("out_stored", 2, 16, credit=True)

        class Loads:

            def __init__(self, name):
                self.sem, self.pairs = sem(name), []

            def add(self, dst, src):
                self.pairs.append((dst, src))

            def add_matrix(self, dst, src):
                self.add(dst, src.rearrange("(t p) c -> p t c", p=P))

            def add_to_all_rows(self, dst, src):
                self.add(dst, src.rearrange("(a c) -> a c", a=1).broadcast_to([P, C]))

            def start(self, sp):
                for dst, src in self.pairs:
                    sp.dma_start(dst, src).then_inc(self.sem, 16)

            def wait(self, eng):
                eng.wait_ge(self.sem, 16 * len(self.pairs))

        for_q, for_norm, for_conv, for_fused, for_rest = [
            Loads(f"loaded_for_{name}") for name in ("q", "norm", "conv", "fused", "rest")]
        for_q.add(consts[:], a["shape_constants"])
        for_q.add_matrix(wq[:], a["L0_conv_wq"])
        for_norm.add_to_all_rows(lng_all[:], a["L0_conv_ln_g"])
        for_norm.add_to_all_rows(lnb_all[:], a["L0_conv_ln_b"])
        for n in range(2):
            for_norm.add_to_all_rows(bq_all[:, n, :], a["L0_conv_bq"])
        for at, name in ((0, "bq"), (2, "bv"), (4, "mq_b"), (6, "mk_b"), (8, "ln_g"), (10, "ln_b"), (12, "dw_b")):
            for_conv.add(vec_rows[at:at + 2, 0, :], a["L0_conv_" + name].rearrange("(t p) -> t p", p=P))
        for_conv.add(vec_rows[14:18, 0, :], a["L0_conv_pw_w"].rearrange("o (t p) h w -> (o t) (h w p)", p=P))
        for at, name in ((18, "b_theta"), (19, "b_phi")):
            for_conv.add(vec_rows[at:at + 1, 0, 0:C8], a["L1_conv_" + name].rearrange("(a p) -> a p", a=1))
        for_conv.add(vec_rows[20:21, 0, :], a["L1_conv_b_g"].rearrange("(a p) -> a p", a=1))
        dw = a["L0_conv_dw_w"].rearrange("(b c k) o h w -> c b k (o h) w", b=CB, k=4)
        for dy in range(KS):
            hi, g = divmod(dy, 4)
            for cb in range(CB):
                for_conv.add(dw_g[32 * g:32 * g + 32, 4 * cb:4 * cb + 4, hi, :], dw[:, cb, :, dy, :])
        for_fused.add_matrix(t_mq, a["L0_conv_mq_w"])
        for_fused.add_matrix(t_wv, a["L0_conv_wv"])
        for_fused.add_matrix(t_mk, a["L0_conv_mk_w"])
        for_fused.add_matrix(t_mv, a["L0_conv_mv_w"])
        for_fused.add_to_all_rows(mvb_all[:], a["L0_conv_mv_b"])
        for_rest.add_matrix(mo[:], a["L0_conv_mo_w"])
        for_rest.add_to_all_rows(mob_all[:], a["L0_conv_mo_b"])
        for_rest.add_matrix(mlp[:], a["L0_conv_mlp_w"])
        for_rest.add_to_all_rows(mlpb_all[:], a["L0_conv_mlp_b"])
        for_rest.add_matrix(w_tp[:, :, 0:C8], a["L1_conv_w_theta"])
        for_rest.add_matrix(w_tp[:, :, C8:2 * C8], a["L1_conv_w_phi"])
        for_rest.add_matrix(w_g[:], a["L1_conv_w_g"])
        for_rest.add(w_o[:], a["L1_conv_w_o"])
        for_rest.add_to_all_rows(bo_all[:], a["L1_conv_b_o"])
        for_rest.add(sigma[:], a["L1_conv_sigma"].rearrange("(a c) -> a c", a=1).broadcast_to([P, 1]))

        gates = {n: sem(f"gate_{n}") for n in ("sp", "dve", "pool")}

        def gate(eng, name):
            eng.sem_inc(gates[name], 1)

        def conv_tile(b, cb):
            if isinstance(b, int) and b == 0 and cb:
                return q_st[:, HQ:2 * HQ].rearrange("p h s -> p (h s)").bitcast(F32)[:, 0:4 * CROWS * PADW].rearrange(
                    "p (k r x) -> p k r x", k=4, r=CROWS)
            return cstack[:]

        def over_rows(row, n):
            return row[:].rearrange("p (a c) -> p a c", a=1).broadcast_to([P, n, C])

        block = ctx.enter_context(nc.Block())

        @block.sync
        def _(sp):
            for s in signals:
                if s.start:
                    sp.sem_inc(s.sem, s.start)
            for k in (*ring.filled, *ring.drained):
                sp.sem_inc(k, 1)
            for k in (s_ring.filled[0], s_ring.drained[0], t_ring.filled[0], t_ring.drained[0], v_bank.filled,
                      v_bank.drained):
                sp.sem_inc(k, 1)
            def load_a(b):
                sp.wait_ge(xln_ready.sem, xln_ready.before(b, 2))
                gate(sp, "sp")
                k = ring.previous(("samp",), b)
                sp.wait_ge(k.drained, k.done)
                gate(sp, "sp")
                sp.dma_start(xa[:], x_rows[b].rearrange("(t p) c -> p t c", p=P)).then_inc(xa_in.sem, 16)

            def load_b(b):
                k = ring.previous(("z", 1, 1), b)
                sp.wait_ge(k.drained, k.done)
                gate(sp, "sp")
                k = ring.previous(("z", 0, 1), b)
                sp.wait_ge(k.drained, k.done)
                gate(sp, "sp")
                sp.dma_start(xb[:], x_rows[b].rearrange("(k p j) c -> p k j c", k=2, j=NJ)).then_inc(xb_in.sem, 16)

            def stack_conv(b, cb):
                for jp in range(2):
                    k = use(("qimg", cb, jp), b)
                    sp.wait_ge(k.drained, k.done)
                    gate(sp, "sp")
                if isinstance(b, int) and b == 0:
                    pass
                elif cb:
                    k = use(("conv", 0), b)
                    sp.wait_ge(k.filled, k.full)
                    gate(sp, "sp")
                else:
                    sp.wait_ge(q_in[1].sem, q_in[1].before(b, 3))
                    gate(sp, "sp")
                for g in range(4):
                    r0 = g // 2 + g % 2
                    sp.dma_start(conv_tile(b, cb)[32 * g:32 * g + 32].rearrange("c k r x -> c k (r x)"),
                                 qpad[:, cb, 1 - g % 2, r0:r0 + CROWS, :].rearrange("c r x -> c (r x)")
                                 ).then_inc(conv_in[cb].sem, 16)

            def stack_q(b, hg):
                for jp in range(2):
                    k = use(("qh", hg, jp), b)
                    sp.wait_ge(k.drained, k.done)
                    gate(sp, "sp")
                if not (isinstance(b, int) and b == 0):
                    k = t_ring.use(("t", hg * NJ + NJ - 1, 1), b - 1)
                    sp.wait_ge(k.filled, k.full)
                    gate(sp, "sp")
                hi, lo = q_parts[hg]
                for row, src in ((0, hi), (1, lo), (2, hi)):
                    sp.dma_start(q_st[32 * row:32 * row + 32, hg * HQ:(hg + 1) * HQ, :].bitcast(F32),
                                 src.bitcast(F32)).then_inc(q_in[hg].sem, 16)

            def stack_k(b):
                k = use(("kh",), b)
                sp.wait_ge(k.drained, k.done)
                gate(sp, "sp")
                for row, src in ((0, k_hi), (1, k_hi), (2, k_lo)):
                    sp.dma_start(k_st[32 * row:32 * row + 32].rearrange("p h g s -> p h (g s)").bitcast(F32),
                                 src.rearrange("p g s -> p (g s)").bitcast(F32)).then_inc(k_in.sem, 16)

            def max_row(b, u):
                hg, j = divmod(u, NJ)
                k = use(("mxt", u), b)
                sp.wait_ge(k.drained, k.done)
                gate(sp, "sp")
                sp.dma_start(q_st[96:98, hg * HQ:(hg + 1) * HQ, j * S_:(j + 1) * S_].bitcast(F32),
                             mx_t[:, u % 2, :].bitcast(F32)).then_inc(max_in[u % 2].sem, 16)

            def max_rows1(b):
                for lh in range(2):
                    k = use(("mxt1", lh), b)
                    sp.wait_ge(k.drained, k.done)
                    gate(sp, "sp")
                    sp.dma_start(th_st[96:98, lh * 512:(lh + 1) * 512].bitcast(F32),
                                 mx1_t[:, lh].bitcast(F32)).then_inc(max1_in[lh].sem, 16)

            def store(b):
                rows = out_rows[b].rearrange("(k p j) c -> p k j c", k=2, j=NJ)
                for cb in range(2):
                    for jp in range(2):
                        k = use(("o", cb, jp), b)
                        sp.wait_ge(k.drained, k.done)
                        gate(sp, "sp")
                    sp.dma_start(rows[:, cb], z[:, cb]).then_inc(out_stored.sem, 16)

            def turn(pb, b, nb):
                if nb is not None:
                    load_a(nb)
                stack_k(b)
                load_b(b)
                for s in range(STEPS):
                    if 1 <= s <= UNITS:
                        max_row(b, s - 1)
                    if nb is not None and s == CONV_AT[0] - 1:
                        stack_conv(nb, 0)
                    if nb is not None and s == CONV_AT[1] - 1:
                        stack_conv(nb, 1)
                    if pb is not None and s == MAX1_AT:
                        max_rows1(pb)
                    if nb is not None and s == 8:
                        stack_q(nb, 0)
                if nb is not None:
                    stack_q(nb, 1)
                if pb is not None:
                    store(pb)

            for_q.start(sp)
            load_a(0)
            for_norm.start(sp)
            sp.wait_ge(setup_pool, 2)
            for_conv.start(sp)
            for_fused.start(sp)
            for_rest.start(sp)
            stack_conv(0, 0)
            stack_conv(0, 1)
            stack_q(0, 0)
            stack_q(0, 1)
            turn(None, 0, 1)
            with sp.Fori(1, B - 1) as b:
                turn(b - 1, b, b + 1)
            turn(B - 2, B - 1, None)
            max_rows1(B - 1)
            store(B - 1)
            sp.wait_ge(out_stored.sem, out_stored.at(B - 1, 2))

        @block.tensor
        def _(pe):
            def turn_weights(w, ps):
                for nt in range(2):
                    for kt in range(2):
                        ins = pe.transpose(ps[:, nt, kt * P:(kt + 1) * P], w[:, kt, nt * P:(nt + 1) * P], ident)
                ins.then_inc(setup_pe, 1)

            def multiply_weights(wt, m, ps):
                for kt in range(2):
                    for nt in range(2):
                        ins = pe.matmul(ps[:, kt, :], wt[:, nt, kt * P:(kt + 1) * P], m[:, nt, :],
                                        start=nt == 0, stop=nt == 1)
                ins.then_inc(setup_pe, 1)

            def setup_vectors():
                for_q.wait(pe)
                turn_weights(wq, ps_s[:, 0:2, :])
                pe.wait_ge(setup_dve, D_ORDERS)
                for n in range(3):
                    ins = pe.transpose(ps_v[:, 0, 32 * n:32 * n + N_ROWS], vec_rows[:, n, :],
                                       ident[0:N_ROWS, 0:N_ROWS])
                ins.then_inc(setup_pe, 1)

            def setup_queries():
                for_fused.wait(pe)
                turn_weights(t_wv, ps_s[:, 2:4, :])
                pe.wait_ge(setup_dve, D_MKP)
                multiply_weights(t_wqt, t_mqp, ps_t[:, 0:2, :])
                for n, (m, bc) in enumerate(((t_mqp, bq_c), (t_mkp, bv_c))):
                    for mb in range(2):
                        for nt in range(2):
                            ins = pe.matmul(ps_v[:, 1, 2 * n + mb:2 * n + mb + 1], m[:, nt, mb * P:(mb + 1) * P],
                                            bc[:, nt:nt + 1], start=nt == 0, stop=nt == 1)
                ins.then_inc(setup_pe, 1)

            def setup_values():
                pe.wait_ge(setup_dve, D_WVT)
                multiply_weights(t_wvt, t_mkp, ps_t[:, 2:4, :])
                multiply_weights(t_wvt, t_mv, ps_s[:, 0:2, :])
                pe.wait_ge(setup_pool, 6)
                for nt in range(2):
                    ins = pe.matmul(ps_s[:, 2, :], t_bv[:, nt, :], t_mv[:, nt, :], start=nt == 0, stop=nt == 1)
                ins.then_inc(setup_pe, 1)

            def open_bank(key, b):
                k = use(key, b)
                pe.wait_ge(k.drained, k.empty)
                return k.tile

            def close_bank(key, b, ins):
                ins.then_inc(use(key, b).filled, 1)

            def read_by(key, b):
                k = use(key, b)
                pe.wait_ge(k.drained, k.done)

            def q_image(b, cb, jp):
                ps = open_bank(("qimg", cb, jp), b)
                if cb == 0:
                    pe.wait_ge(xln_ready.sem, xln_ready.at(b, jp + 1))
                for jj in range(2):
                    for kt in range(2):
                        t = 4 * jp + 2 * jj + kt
                        ins = pe.matmul(ps[:, jj, :], xln[:, t, cb * P:(cb + 1) * P], wq[:, kt, :],
                                        start=kt == 0, stop=kt == 1)
                close_bank(("qimg", cb, jp), b, ins)

            def conv_part(b, cb, hi, shifts):
                if hi == 0 and 0 in shifts:
                    open_bank(("conv", cb), b)
                    pe.wait_ge(conv_in[cb].sem, conv_in[cb].at(b, 4))
                ps = use(("conv", cb), b).tile
                for dx in shifts:
                    for k in range(4):
                        ins = pe.matmul(
                            ps[32 * k:32 * k + 32, 0, :], conv_w[:, cb * 4 + k, hi, dx, :],
                            conv_tile(b, cb)[:, k, 2 * hi:2 * hi + HG_, dx:dx + 2 * WG_ - 1:2],
                            start=hi == 0 and dx == 0, stop=hi == 1 and dx == KS - 1)
                if hi == 1 and KS - 1 in shifts:
                    close_bank(("conv", cb), b, ins)

            def offsets(b):
                ps = open_bank(("off",), b)
                pe.wait_ge(conv_done.sem, conv_done.at(b, CB))
                for o in range(2):
                    for kt in range(CB):
                        ins = pe.matmul(ps[:, o, :], pw_all[:, kt, o, :], gel[:, kt, :], start=kt == 0, stop=kt == 1)
                close_bank(("off",), b, ins)

            def queries(b, hg, jp):
                ps = open_bank(("qh", hg, jp), b)
                for jj in range(2):
                    for kt in range(2):
                        ins = pe.matmul(ps[:, jj, :], w_qh[:, kt, hg * P:(hg + 1) * P],
                                        xln[:, 4 * jp + 2 * jj + kt, :], start=kt == 0, stop=kt == 1)
                close_bank(("qh", hg, jp), b, ins)

            def sample(b):
                ps = open_bank(("samp",), b)
                pe.wait_ge(hat_done.sem, hat_done.at(b, 1))
                for st in range(2):
                    for t in range(NT):
                        ins = pe.matmul(ps[:, st, :], hat[:, t, st * P:(st + 1) * P], xa[:, t, :],
                                        start=t == 0, stop=t == NT - 1)
                close_bank(("samp",), b, ins)

            def keys(b):
                ps = open_bank(("kh",), b)
                read_by(("samp",), b)
                for hg in range(NHG):
                    for st in range(2):
                        ins = pe.matmul(ps[:, hg, :], w_kh[:, st, hg * P:(hg + 1) * P], samp[:, st, :],
                                        start=st == 0, stop=st == 1)
                close_bank(("kh",), b, ins)

            def value_rows(b):
                ps = open_bank(("vh",), b)
                for rb in range(2):
                    for st in range(2):
                        ins = pe.matmul(ps[:, rb, :], samp[:, st, rb * P:(rb + 1) * P], w_vh[:, st, :],
                                        start=st == 0, stop=st == 1)
                close_bank(("vh",), b, ins)

            def scores(b, u, cb):
                hg, j = divmod(u, NJ)
                if u == 0 and cb == 0:
                    pe.wait_ge(k_in.sem, k_in.at(b, 3))
                if j == 0 and cb == 0:
                    pe.wait_ge(q_in[hg].sem, q_in[hg].at(b, 3))
                k = s_ring.use(("s", u, cb), b)
                pe.wait_ge(k.drained, k.empty)
                for h in range(HQ):
                    ins = pe.matmul(ps_s[:, h, :], q_st[0:96, hg * HQ + h, j * S_ + cb * P:j * S_ + (cb + 1) * P],
                                    k_st[0:96, h, hg, :], start=True, stop=True)
                ins.then_inc(k.filled, 1)

            def max_rows(b, u):
                ps = open_bank(("mxt", u), b)
                pe.wait_ge(max_split.sem, max_split.at(b, u + 1))
                for cb in range(2):
                    ins = pe.transpose(ps[0:2 * HQ, 0, cb * P:(cb + 1) * P],
                                       mx_hl[:, cb].rearrange("p a h -> p (a h)").bitcast(F32), ident)
                close_bank(("mxt", u), b, ins)

            def shifted(b, u, pr):
                hg, j = divmod(u, NJ)
                if pr == 0:
                    pe.wait_ge(max_in[u % 2].sem, max_in[u % 2].at(b, u // 2 + 1))
                k = t_ring.use(("t", u, pr), b)
                pe.wait_ge(k.drained, k.empty)
                for hh in range(2):
                    h = 2 * pr + hh
                    for mt in range(2):
                        ins = pe.matmul(ps_t[:, 2 * hh + mt, :], k_st[0:98, h, hg, mt * P:(mt + 1) * P],
                                        q_st[0:98, hg * HQ + h, j * S_:(j + 1) * S_], start=True, stop=True)
                ins.then_inc(k.filled, 1)

            def values(b, u):
                hg = u // NJ
                k = t_ring.use(("t", u, 1), b)
                pe.wait_ge(k.drained, k.done)
                pe.wait_ge(v_bank.drained, v_bank.empty(b, u))
                if u == 0:
                    read_by(("vh",), b)
                for mt in range(2):
                    for h in range(HQ):
                        hh = hg * HQ + h
                        pe.matmul(ps_v[32 * h:32 * h + 32, 0, :], vh[:, mt, hh * HD:(hh + 1) * HD],
                                  prob[:, u % 2, h, mt, :], start=mt == 0, stop=mt == 1)
                pe.wait_ge(prob_summed.sem, prob_summed.at(b, 2 * u + 2))
                for h in range(HQ):
                    ins = pe.matmul(ps_v[32 * h:32 * h + 32, 1, :], ones[:], prob_sum[h // 2][:, h % 2, :],
                                    start=True, stop=True)
                ins.then_inc(v_bank.filled, 1)

            def project(b, cb):
                for jp in range(2):
                    ps = open_bank(("z", cb, jp), b)
                    pe.wait_ge(v_bank.drained, v_bank.done(b, UNITS - 1))
                    for jj in range(2):
                        j = 2 * jp + jj
                        for hg in range(NHG):
                            ins = pe.matmul(ps[:, jj, :], att[:, hg, j * S_ + cb * P:j * S_ + (cb + 1) * P],
                                            mo[:, hg, :], start=hg == 0, stop=hg == 1)
                    close_bank(("z", cb, jp), b, ins)

            def turn_rows(b, cb):
                for kt in range(CB):
                    ps = open_bank(("znt", cb, kt), b)
                    if kt == 0:
                        pe.wait_ge(zn_done.sem, zn_done.at(b, (cb + 1) * NJ))
                    for j in range(NJ):
                        ins = pe.transpose(ps[:, j // 2, (j % 2) * P:(j % 2 + 1) * P],
                                           zn[:, cb, j, kt * P:(kt + 1) * P], ident)
                    close_bank(("znt", cb, kt), b, ins)

            def mlp_rows(b, cb):
                for jp in range(2):
                    ps = open_bank(("mlp", cb, jp), b)
                    if jp == 0:
                        read_by(("znt", cb, 0), b)
                        read_by(("znt", cb, 1), b)
                    for jj in range(2):
                        j = 2 * jp + jj
                        for kt in range(CB):
                            ins = pe.matmul(ps[:, jj, :], zt[:, kt, cb * 512 + j * P:cb * 512 + (j + 1) * P],
                                            mlp[:, kt, :], start=kt == 0, stop=kt == 1)
                    close_bank(("mlp", cb, jp), b, ins)

            def turn_output(b, cb):
                for kt in range(CB):
                    ps = open_bank(("yt", cb, kt), b)
                    if kt == 0:
                        pe.wait_ge(y_done.sem, y_done.at(b, cb + 1))
                    for j in range(NJ):
                        ins = pe.transpose(ps[:, j // 2, (j % 2) * P:(j % 2 + 1) * P],
                                           z[:, cb, j, kt * P:(kt + 1) * P], ident)
                    close_bank(("yt", cb, kt), b, ins)

            def project1(b, name, w, m):
                for lh in range(2):
                    ps = open_bank((name, lh), b)
                    for kt in range(CB):
                        if name == "tp":
                            read_by(("yt", lh, kt), b)
                        ins = pe.matmul(ps[0:m].rearrange("p a s -> p (a s)"), w[:, kt, :],
                                        zt[:, kt, lh * 512:(lh + 1) * 512], start=kt == 0, stop=kt == 1)
                    close_bank((name, lh), b, ins)

            def turn_g(b):
                ps = open_bank(("gt",), b)
                pe.wait_ge(g_bias.sem, g_bias.at(b, 1))
                for mt in range(2):
                    ins = pe.transpose(ps[:, 0, mt * P:(mt + 1) * P], g_pool[:, mt * P:(mt + 1) * P], ident)
                close_bank(("gt",), b, ins)

            def scores1(b, lh):
                if lh == 0:
                    pe.wait_ge(ph_step.sem, ph_step.at(b, 4))
                    pe.wait_ge(th_lo.sem, th_lo.at(b, 2))
                    read_by(("tp", 0), b)
                    read_by(("tp", 1), b)
                k = s_ring.use(("s1", lh), b)
                pe.wait_ge(k.drained, k.empty)
                for n in range(4):
                    ins = pe.matmul(ps_s[:, n, :], th_st[0:96, lh * 512 + n * P:lh * 512 + (n + 1) * P],
                                    ph_st[0:96, :], start=True, stop=True)
                ins.then_inc(k.filled, 1)

            def max_rows1(b):
                for lh in range(2):
                    ps = open_bank(("mxt1", lh), b)
                    pe.wait_ge(max1_split.sem, max1_split.at(b, lh + 1))
                    ins = pe.transpose(ps[0:8, 0, 0:P], mx1_hl[:, lh].rearrange("p a h -> p (a h)").bitcast(F32), ident)
                    close_bank(("mxt1", lh), b, ins)

            def shifted1(b, lh):
                pe.wait_ge(max1_in[lh].sem, max1_in[lh].at(b, 1))
                k = t_ring.use(("t1", lh), b)
                pe.wait_ge(k.drained, k.empty)
                for mt in range(2):
                    ins = pe.matmul(ps_t[:, 2 * mt:2 * mt + 2, :].rearrange("p a s -> p (a s)"),
                                    ph_st[0:98, mt * P:(mt + 1) * P], th_st[0:98, lh * 512:(lh + 1) * 512],
                                    start=True, stop=True)
                ins.then_inc(k.filled, 1)

            def attend1(b):
                for lh in range(2):
                    ps = open_bank(("ag", lh), b)
                    k = t_ring.use(("t1", lh), b)
                    pe.wait_ge(k.drained, k.done)
                    if lh == 0:
                        read_by(("gt",), b)
                    for mt in range(2):
                        ins = pe.matmul(ps[:].rearrange("p a s -> p (a s)"), g_m[:, mt, :],
                                        prob1[:, mt, lh * 512:(lh + 1) * 512], start=mt == 0, stop=mt == 1)
                    close_bank(("ag", lh), b, ins)
                ps = open_bank(("den",), b)
                for mt in range(2):
                    for q in range(4):
                        rows = prob1[:, mt].rearrange("p (cb q r j) -> p q cb j r", cb=2, q=4, j=NJ)[:, q]
                        ins = pe.matmul(ps[32 * q:32 * q + 32, 0, :], ones[:], rows, start=mt == 0, stop=mt == 1)
                close_bank(("den",), b, ins)
                for cb in range(2):
                    for jp in range(2):
                        ps = open_bank(("o", cb, jp), b)
                        if jp == 0:
                            read_by(("ag", cb), b)
                        for jj in range(2):
                            j = 2 * jp + jj
                            ins = pe.matmul(ps[:, jj, :], ag[:, cb * 512 + j:cb * 512 + j + 4 * P - 3:4], w_o[:],
                                            start=True, stop=True)
                        close_bank(("o", cb, jp), b, ins)

            def l1_step(b, s):
                if s in MLP_AT:
                    mlp_rows(b, MLP_AT.index(s))
                if s == NORM_TURN_AT:
                    turn_rows(b, 1)
                if s == OUT_TURN_AT:
                    turn_output(b, 0)
                    turn_output(b, 1)
                if s == THETA_PHI_AT:
                    project1(b, "tp", w_tp, 2 * C8)
                if s == G_AT:
                    project1(b, "g", w_g, C2)
                if s == G_TURN_AT:
                    turn_g(b)
                if s == MAX1_AT:
                    max_rows1(b)
                if s == ATTEND1_AT:
                    attend1(b)

            def turn(pb, b, nb):
                front = nb is not None
                if pb is not None:
                    l1_step(pb, MLP_AT[0])
                for s in range(STEPS):
                    if s < UNITS:
                        scores(b, s, 0)
                    if 2 <= s <= UNITS + 1:
                        shifted(b, s - 2, 0)
                    if 1 <= s <= UNITS:
                        max_rows(b, s - 1)
                    if s >= 3:
                        values(b, s - 3)
                    if pb is not None and s in (NORM_TURN_AT, MLP_AT[1]):
                        l1_step(pb, s)
                    if s < UNITS:
                        scores(b, s, 1)
                    if 2 <= s <= UNITS + 1:
                        shifted(b, s - 2, 1)
                    if pb is not None and s == THETA_PHI_AT:
                        l1_step(pb, s)
                    for cb in range(CB):
                        if front and s == QIMG_AT[cb]:
                            q_image(nb, cb, 0)
                            q_image(nb, cb, 1)
                        if front and s in (CONV_AT[cb], CONV_AT[cb] + 1):
                            conv_part(nb, cb, s - CONV_AT[cb], range(4))
                    if pb is not None and s in SCORES1_AT:
                        scores1(pb, SCORES1_AT.index(s))
                    if pb is not None and s in SHIFTED1_AT:
                        shifted1(pb, SHIFTED1_AT.index(s))
                    for cb in range(CB):
                        if front and s in (CONV_AT[cb], CONV_AT[cb] + 1):
                            conv_part(nb, cb, s - CONV_AT[cb], range(4, KS))
                    if front and s in QUERY_AT:
                        queries(nb, *QUERY_AT[s])
                    if front and s == STEPS - 1:
                        queries(nb, 1, 0)
                        queries(nb, 1, 1)
                        offsets(nb)
                    if pb is not None and s not in (NORM_TURN_AT, MLP_AT[1], THETA_PHI_AT):
                        l1_step(pb, s)
                project(b, 0)
                project(b, 1)
                if front:
                    sample(nb)
                turn_rows(b, 0)
                if front:
                    keys(nb)
                    value_rows(nb)

            setup_vectors()
            for cb in range(CB):
                q_image(0, cb, 0)
                q_image(0, cb, 1)
            setup_queries()
            pe.wait_ge(setup_pool, 5)
            for cb in range(CB):
                conv_part(0, cb, 0, range(KS))
                conv_part(0, cb, 1, range(KS))
            pe.wait_ge(setup_dve, D_QUERY)
            queries(0, 0, 0)
            queries(0, 0, 1)
            pe.wait_ge(setup_pool, 7)
            offsets(0)
            queries(0, 1, 0)
            queries(0, 1, 1)
            setup_values()
            pe.wait_ge(setup_dve, D_ALL)
            sample(0)
            keys(0)
            value_rows(0)
            for_rest.wait(pe)
            pe.wait_ge(minus_rows, 2)
            turn(None, 0, 1)
            with pe.Fori(1, B - 1) as b:
                turn(b - 1, b, b + 1)
            turn(B - 2, B - 1, None)
            for s in range(MLP_AT[0], STEPS):
                if s == G_AT:
                    l1_step(B - 1, s)
                if s in SCORES1_AT:
                    scores1(B - 1, SCORES1_AT.index(s))
                if s in SHIFTED1_AT:
                    shifted1(B - 1, SHIFTED1_AT.index(s))
                if s != G_AT:
                    l1_step(B - 1, s)

        def await_bank(eng, key, b):
            k = use(key, b)
            eng.wait_ge(k.filled, k.full)
            return k.tile

        def drain(ins, key, b):
            ins.then_inc(use(key, b).drained, 1)

        @block.scalar
        def _(act):
            def row_norm(b):
                act.wait_ge(rsqrt1.sem, rsqrt1.at(b, RSQRT_STEPS + 1))
                k = ring.previous(("samp",), b)
                act.wait_ge(k.drained, k.done)
                for t in range(NT):
                    act.activation(xln[:, t, :], xa[:, t, :], ACT.Identity, bias=rs1[:, 0, t:t + 1],
                                   scale=rs1[:, 1, t:t + 1]).then_inc(ln1_norm.sem, 1)

            def conv_gelu(b, cb):
                k = use(("conv", cb), b)
                act.wait_ge(k.drained, k.done)
                act.activation(gel[:, cb, :], gel[:, cb, :], ACT.Gelu).then_inc(conv_done.sem, 1)

            def offset_tanh(b):
                ps = await_bank(act, ("off",), b)
                drain(act.activation(pos[:].rearrange("p a s -> p (a s)"), ps[:].rearrange("p a s -> p (a s)"),
                                     ACT.Tanh), ("off",), b)

            def query_hi(b, hg, jp):
                if hg == 0 and jp == 0:
                    act.wait_ge(k_in.sem, k_in.before(b, 3))
                if hg == 1 and jp == 0:
                    k = use(("conv", 1), b)
                    act.wait_ge(k.filled, k.full)
                ps = await_bank(act, ("qh", hg, jp), b)
                act.activation(q_parts[hg][0][:, jp * 512:(jp + 1) * 512], ps[:].rearrange("p a s -> p (a s)"),
                               ACT.Identity, bias=bqh_c[:, hg:hg + 1]).then_inc(q_hi_done.sem, 1)

            def hats(b):
                act.wait_ge(pos_step.sem, pos_step.at(b, 3))
                act.activation(hat_x[:], pos[:, 1, :], ACT.Abs, bias=consts[:, K_XP:K_XP + 1]).then_inc(hat_dist.sem, 1)
                k = use(("qh", 1, 1), b)
                act.wait_ge(k.filled, k.full)
                for t in range(NT):
                    act.activation(hat[:, t, :], pos[:, 0, :], ACT.Abs,
                                   bias=consts[:, K_YP + t:K_YP + t + 1]).then_inc(hat_dist.sem, 1)
                act.wait_ge(hat_dist.sem, hat_dist.at(b, 1))
                act.activation(hat_x[:], hat_x[:], ACT.Relu, bias=1.0, scale=-1.0).then_inc(hat_relu.sem, 1)
                act.wait_ge(hat_dist.sem, hat_dist.at(b, 1 + NT))
                act.activation(hat[:], hat[:], ACT.Relu, bias=1.0, scale=-1.0).then_inc(hat_relu.sem, 1)

            def sampled(b):
                ps = await_bank(act, ("samp",), b)
                drain(act.activation(samp[:], ps[:], ACT.Copy), ("samp",), b)

            def key_hi(b):
                act.wait_ge(q_in[0].sem, q_in[0].at(b, 3))
                ps = await_bank(act, ("kh",), b)
                for hg in range(NHG):
                    ins = act.activation(k_hi[:, hg, :], ps[:, hg, :], ACT.Identity, bias=bkh_c[:, hg:hg + 1])
                ins.then_inc(k_hi_done.sem, 1)

            def max_out(b, u):
                ps = await_bank(act, ("mxt", u), b)
                if u >= 2:
                    act.wait_ge(max_in[u % 2].sem, max_in[u % 2].at(b, u // 2))
                else:
                    act.wait_ge(max_in[u % 2].sem, max_in[u % 2].before(b, UNITS // 2))
                drain(act.activation(mx_t[:, u % 2, :], ps[0:2 * HQ, 0, :], ACT.Copy), ("mxt", u), b)

            def exps(b, u):
                for pr in range(2):
                    k = t_ring.use(("t", u, pr), b)
                    act.wait_ge(k.filled, k.full)
                    if u >= 2 and pr == 0:
                        act.wait_ge(v_bank.filled, v_bank.full(b, u - 2))
                    act.activation(prob[:, u % 2, 2 * pr:2 * pr + 2].rearrange("p h m s -> p (h m) s"), ps_t[:],
                                   ACT.Exp).then_inc(k.drained, 1)

            def norm_turned(b, cb):
                for kt in range(CB):
                    ps = await_bank(act, ("znt", cb, kt), b)
                    drain(act.activation(zt[:, kt, cb * 512:(cb + 1) * 512], ps[:].rearrange("p a s -> p (a s)"),
                                         ACT.Identity, bias=lnb_c[:, kt:kt + 1], scale=lng_c[:, kt:kt + 1]),
                          ("znt", cb, kt), b)

            def mlp_gelu(b, cb):
                for jp in range(2):
                    k = use(("mlp", cb, jp), b)
                    act.wait_ge(k.drained, k.done)
                    act.activation(mid[:, cb, 2 * jp:2 * jp + 2, :], mid[:, cb, 2 * jp:2 * jp + 2, :],
                                   ACT.Gelu).then_inc(gelu_done.sem, 1)

            def output_turned(b, cb):
                for kt in range(CB):
                    ps = await_bank(act, ("yt", cb, kt), b)
                    drain(act.activation(
                        zt[:, kt, cb * 512:(cb + 1) * 512].rearrange("p (q j) -> p j q", j=NJ),
                        ps[:].rearrange("p a (c q) -> p (a c) q", c=2), ACT.Copy), ("yt", cb, kt), b)

            def theta_hi(b):
                for lh in range(2):
                    ps = await_bank(act, ("tp", lh), b)
                    for row in (0, 2):
                        act.activation(th_st[row * C8:(row + 1) * C8, lh * 512:(lh + 1) * 512],
                                       ps[0:C8].rearrange("p a s -> p (a s)"),
                                       ACT.Identity, bias=bth_c[0:C8]).then_inc(th_hi.sem, 1)

            def g_turned(b):
                ps = await_bank(act, ("gt",), b)
                drain(act.activation(g_m[:], ps[:, 0, :].rearrange("p (m d) -> p m d", m=2), ACT.Copy), ("gt",), b)

            def max_out1(b):
                for lh in range(2):
                    ps = await_bank(act, ("mxt1", lh), b)
                    act.wait_ge(max1_in[lh].sem, max1_in[lh].before(b, 1))
                    drain(act.activation(mx1_t[:, lh], ps[0:8, 0, 0:P], ACT.Copy), ("mxt1", lh), b)

            def exps1(b, lh):
                k = t_ring.use(("t1", lh), b)
                act.wait_ge(k.filled, k.full)
                act.activation(prob1[:, :, lh * 512:(lh + 1) * 512],
                               ps_t[:].rearrange("p (m a) s -> p m (a s)", m=2), ACT.Exp).then_inc(k.drained, 1)

            def mixed(b):
                for lh in range(2):
                    ps = await_bank(act, ("ag", lh), b)
                    drain(act.activation(ag[:, lh * 512:(lh + 1) * 512], ps[:].rearrange("p a s -> p (a s)"),
                                         ACT.Copy), ("ag", lh), b)

            def l1_step(b, s):
                if s == NORM_TURN_AT:
                    norm_turned(b, 1)
                if s in MLP_GELU_AT:
                    mlp_gelu(b, MLP_GELU_AT.index(s))
                if s == OUT_TURN_AT:
                    output_turned(b, 0)
                    output_turned(b, 1)
                if s == THETA_PHI_AT:
                    theta_hi(b)
                if s == G_TURN_AT:
                    g_turned(b)
                if s == MAX1_AT:
                    max_out1(b)
                if s in SHIFTED1_AT:
                    exps1(b, SHIFTED1_AT.index(s))
                if s == ATTEND1_AT:
                    mixed(b)

            def turn(pb, b, nb):
                front = nb is not None
                if pb is not None:
                    l1_step(pb, MLP_AT[0])
                for s in range(STEPS):
                    if 1 <= s <= UNITS:
                        max_out(b, s - 1)
                    if 2 <= s <= UNITS + 1:
                        exps(b, s - 2)
                    if front and s in QUERY_AT:
                        query_hi(nb, *QUERY_AT[s])
                    if front and s == STEPS - 1:
                        conv_gelu(nb, 0)
                        conv_gelu(nb, 1)
                        query_hi(nb, 1, 0)
                        query_hi(nb, 1, 1)
                        offset_tanh(nb)
                    if front and s == 1:
                        row_norm(nb)
                    if pb is not None:
                        l1_step(pb, s)
                if front:
                    hats(nb)
                    sampled(nb)
                norm_turned(b, 0)
                if front:
                    key_hi(nb)

            row_norm(0)
            conv_gelu(0, 0)
            conv_gelu(0, 1)
            act.wait_ge(setup_dve, D_QUERY)
            query_hi(0, 0, 0)
            query_hi(0, 0, 1)
            offset_tanh(0)
            query_hi(0, 1, 0)
            query_hi(0, 1, 1)
            for_q.wait(act)
            hats(0)
            sampled(0)
            key_hi(0)
            turn(None, 0, 1)
            with act.Fori(1, B - 1) as b:
                turn(b - 1, b, b + 1)
            turn(B - 2, B - 1, None)
            for s in range(MLP_AT[0], STEPS):
                l1_step(B - 1, s)

        @block.vector
        def _(dve):
            dve.memset(k_st[96:98].bitcast(F32), -1.0).then_inc(minus_rows, 1)
            dve.memset(ph_st[96:98, :].bitcast(F32), -1.0).then_inc(minus_rows, 1)

            def setup_copy(dst, src):
                dve.tensor_copy(dst, src).then_inc(setup_dve, 1)

            def setup_orders():
                for_conv.wait(dve)
                setup_copy(vec_rows[:, 1, :].rearrange("r (d h) -> r d h", h=HQ),
                           vec_rows[:, 0, :].rearrange("r (h d) -> r d h", h=HQ))
                setup_copy(vec_rows[:, 2, :].rearrange("r (k c) -> r k c", k=4),
                           vec_rows[:, 0, :].rearrange("r (c k) -> r k c", k=4))
                dve.wait_ge(setup_pe, 1)
                setup_copy(t_wqt, ps_s[:, 0:2, :])

            def setup_columns():
                dve.wait_ge(setup_pe, 2)
                setup_copy(cols[:, :, 0:N_ROWS], ps_v[:, 0, 0:96].rearrange("p (n r) -> p n r", n=3)[:, :, 0:N_ROWS])

            def setup_queries():
                for_fused.wait(dve)
                for w, wp in ((t_mq, t_mqp), (t_mk, t_mkp)):
                    setup_copy(wp.rearrange("p t (g d h) -> p (t g) d h", g=NHG, h=HQ),
                               w.rearrange("p t (g h d) -> p (t g) d h", g=NHG, h=HQ))
                dve.wait_ge(setup_pe, 3)
                setup_copy(t_wvt, ps_s[:, 2:4, :])
                dve.wait_ge(setup_pe, 4)
                setup_copy(w_qh[:], ps_t[:, 0:2, :])
                dve.wait_ge(setup_pe, 5)
                dve.tensor_tensor(bqh_c, ps_v[:, 1, 0:2], mqb_c, ALU.add).then_inc(setup_dve, 1)
                dve.tensor_tensor(bkh_c, ps_v[:, 1, 2:4], mkb_c, ALU.add).then_inc(setup_dve, 1)

            def setup_values():
                dve.wait_ge(setup_pe, 6)
                setup_copy(w_kh[:], ps_t[:, 2:4, :])
                dve.wait_ge(setup_pe, 7)
                setup_copy(w_vh[:], ps_s[:, 0:2, :])
                dve.wait_ge(setup_pe, 8)
                dve.tensor_tensor(bvh_all[:], ps_s[:, 2, :], mvb_all[:], ALU.add).then_inc(setup_dve, 1)

            def rsqrt(sig, b, first, var, w):
                y, t, v = w[:, 1], w[:, 2], w[:, 3]
                n = [first]

                def step(ins):
                    ins.then_inc(sig.sem, 1)
                    n[0] += 1
                    dve.wait_ge(sig.sem, sig.at(b, n[0]))

                step(dve.tensor_scalar(v, var, EPS, None, ALU.add))
                step(dve.tensor_scalar(t.bitcast(I32), v.bitcast(I32), 1, None, ALU.logical_shift_right))
                step(dve.tensor_scalar(y.bitcast(I32), t.bitcast(I32), -1.0, float(0x5F3759DF), ALU.mult, ALU.add))
                for _ in range(NEWTON):
                    step(dve.tensor_tensor(t, y, y, ALU.mult))
                    step(dve.scalar_tensor_tensor(t, t, -0.5, v, ALU.mult, ALU.mult))
                    step(dve.scalar_tensor_tensor(y, t, 1.5, y, ALU.add, ALU.mult))

            def row_stats(b):
                dve.wait_ge(xa_in.sem, xa_in.at(b, 1))
                dve.wait_ge(xln_ready.sem, xln_ready.before(b, 2))
                for t in range(NT):
                    dve.bn_stats(st1[:, t, :], xa[:, t, :]).then_inc(ln1_stat.sem, 1)

            def row_deviation(b):
                dve.wait_ge(ln1_stat.sem, ln1_stat.at(b, NT))
                gate(dve, "dve")
                for t in range(NT):
                    dve.bn_aggr(mv1[:, t, :], st1[:, t, :]).then_inc(ln1_aggr.sem, 1)
                dve.wait_ge(ln1_aggr.sem, ln1_aggr.at(b, NT))
                rsqrt(rsqrt1, b, 0, mv1[:, :, 1], rs1)
                dve.scalar_tensor_tensor(rs1[:, 0], mv1[:, :, 0], -1.0, rs1[:, 1], ALU.mult,
                                         ALU.mult).then_inc(rsqrt1.sem, 1)

            def row_norm(b, half):
                part = xln[:, half * NJ:(half + 1) * NJ, :]
                dve.wait_ge(ln1_norm.sem, ln1_norm.at(b, (half + 1) * NJ))
                dve.tensor_tensor(part, part, over_rows(lng_all, NJ), ALU.mult).then_inc(ln1_scaled.sem, 1)
                dve.wait_ge(ln1_scaled.sem, ln1_scaled.at(b, half + 1))
                dve.tensor_tensor(part, part, over_rows(lnb_all, NJ), ALU.add).then_inc(xln_ready.sem, 1)

            def q_image(b, cb, jp):
                if jp == 0:
                    for c in range(CB):
                        k = ring.previous(("conv", c), b)
                        dve.wait_ge(k.filled, k.full)
                        gate(dve, "dve")
                ps = await_bank(dve, ("qimg", cb, jp), b)
                drain(dve.tensor_tensor(
                    qpad[:, cb, :, 8 * jp + 2:8 * jp + 10, KS // 2:KS // 2 + W],
                    ps[:].rearrange("p a (r q x) -> p q (a r) x", q=2, x=W),
                    bq_all[:].rearrange("p a (r q x) -> p q (a r) x", q=2, x=W), ALU.add), ("qimg", cb, jp), b)

            def query_lo(b, hg, jp):
                ps = await_bank(dve, ("qh", hg, jp), b)
                hi, lo = [part[:, jp * 512:(jp + 1) * 512] for part in q_parts[hg]]
                dve.wait_ge(q_hi_done.sem, q_hi_done.at(b, 2 * hg + jp + 1))
                drain(dve.scalar_tensor_tensor(lo, ps[:].rearrange("p a s -> p (a s)"), bqh_c[:, hg:hg + 1],
                                               hi.bitcast(F32), ALU.add, ALU.subtract), ("qh", hg, jp), b)

            def conv_out(b, cb):
                ps = await_bank(dve, ("conv", cb), b)
                drain(dve.tensor_scalar(gel[:, cb, :], ps[:, 0, :], dwb_c[:, cb:cb + 1], None, ALU.add), ("conv", cb), b)

            def positions(b):
                k = use(("off",), b)
                flat = pos[:].rearrange("p a s -> p (a s)")
                dve.wait_ge(k.drained, k.done)
                dve.tensor_tensor(flat, flat, refs, ALU.add).then_inc(pos_step.sem, 1)
                dve.wait_ge(pos_step.sem, pos_step.at(b, 1))
                dve.tensor_scalar(flat, flat, 1.0, float(H // R) / 2.0, ALU.add, ALU.mult).then_inc(pos_step.sem, 1)
                dve.wait_ge(pos_step.sem, pos_step.at(b, 2))
                dve.tensor_scalar(flat, flat, 1.0, 0.5 * (W - 1), ALU.add, ALU.mult).then_inc(pos_step.sem, 1)

            def hats(b):
                dve.wait_ge(hat_relu.sem, hat_relu.at(b, 2))
                dve.tensor_tensor(hat[:], hat[:], hat_x[:].rearrange("p (a s) -> p a s", a=1).broadcast_to([P, NT, S_]),
                                  ALU.mult).then_inc(hat_done.sem, 1)

            def key_lo(b):
                ps = await_bank(dve, ("kh",), b)
                dve.wait_ge(k_hi_done.sem, k_hi_done.at(b, 1))
                for hg in range(NHG):
                    ins = dve.scalar_tensor_tensor(k_lo[:, hg, :], ps[:, hg, :], bkh_c[:, hg:hg + 1],
                                                   k_hi[:, hg, :].bitcast(F32), ALU.add, ALU.subtract)
                drain(ins, ("kh",), b)

            def value_rows(b):
                ps = await_bank(dve, ("vh",), b)
                drain(dve.tensor_tensor(vh[:], ps[:], over_rows(bvh_all, 2), ALU.add), ("vh",), b)

            def maxima(b, u, cb):
                if cb == 0 and u:
                    dve.wait_ge(max_split.sem, max_split.at(b, u))
                elif cb == 0:
                    dve.wait_ge(max_split.sem, max_split.before(b, UNITS))
                k = s_ring.use(("s", u, cb), b)
                dve.wait_ge(k.filled, k.full)
                dve.tensor_reduce(mx[:, cb, :], ps_s[:], AX.X, ALU.max).then_inc(k.drained, 1)

            def split_maxima(b, u):
                k = s_ring.use(("s", u, 1), b)
                dve.wait_ge(k.drained, k.done)
                if u:
                    k = use(("mxt", u - 1), b)
                    dve.wait_ge(k.filled, k.full)
                else:
                    k = ring.previous(("mxt", UNITS - 1), b)
                    dve.wait_ge(k.filled, k.full)
                dve.tensor_copy(mx_hl[:, :, 0, :], mx[:]).then_inc(max_hi.sem, 1)
                dve.wait_ge(max_hi.sem, max_hi.at(b, u + 1))
                dve.tensor_tensor(mx_hl[:, :, 1, :], mx[:], mx_hl[:, :, 0, :].bitcast(F32),
                                  ALU.subtract).then_inc(max_split.sem, 1)

            def sum_blocks(b, u):
                for pr in range(2):
                    k = t_ring.use(("t", u, pr), b)
                    dve.wait_ge(k.drained, k.done)
                    blocks = prob[:, u % 2, 2 * pr:2 * pr + 2]
                    dve.tensor_tensor(prob_sum[pr][:], blocks[:, :, 0, :], blocks[:, :, 1, :],
                                      ALU.add).then_inc(prob_summed.sem, 1)

            def denominators(b, u):
                dve.wait_ge(v_bank.filled, v_bank.full(b, u))
                dve.transpose(rden[:], ps_v[:, 1, :]).then_inc(den_turned.sem, 1)
                dve.wait_ge(den_turned.sem, den_turned.at(b, u + 1))
                dve.reciprocal(rden_one[:], rden[:, 0:S_:32]).then_inc(den_inv.sem, 1)

            def normalise(b, u):
                hg, j = divmod(u, NJ)
                dve.wait_ge(den_spread.sem, den_spread.at(b, u + 1))
                dve.transpose(rden[:], rden_cols[:]).then_inc(rden_done.sem, 1)
                dve.wait_ge(rden_done.sem, rden_done.at(b, u + 1))
                dve.tensor_tensor(att[:, hg, j * S_:(j + 1) * S_], ps_v[:, 0, :], rden[:],
                                  ALU.mult).then_inc(v_bank.drained, 1)

            def residual(b, blocks):
                if 0 in blocks:
                    dve.wait_ge(xb_biased.sem, xb_biased.at(b, 2))
                    dve.wait_ge(out_stored.sem, out_stored.before(b, 2))
                for cb in blocks:
                    for jp in range(2):
                        ps = await_bank(dve, ("z", cb, jp), b)
                        ins = dve.tensor_tensor(z[:, cb, 2 * jp:2 * jp + 2, :], ps[:], xb[:, cb, 2 * jp:2 * jp + 2, :],
                                                ALU.add)
                        drain(ins, ("z", cb, jp), b)
                for cb in blocks:
                    for jp in range(2):
                        k = use(("z", cb, jp), b)
                        dve.wait_ge(k.drained, k.done)
                        for jj in range(2):
                            n = cb * NJ + 2 * jp + jj
                            dve.bn_stats(st2[:, n, :], z[:, cb, 2 * jp + jj, :]).then_inc(ln2_stat.sem, 1)

            def residual_norm(b, blocks):
                first, last = blocks[0] * NJ, (blocks[-1] + 1) * NJ
                dve.wait_ge(ln2_stat.sem, ln2_stat.at(b, last))
                gate(dve, "dve")
                for n in range(first, last):
                    dve.bn_aggr(mv2[:, n, :], st2[:, n, :]).then_inc(ln2_aggr.sem, 1)
                dve.wait_ge(ln2_aggr.sem, ln2_aggr.at(b, last))
                rsqrt(rsqrt2, b, RSQRT_STEPS * (blocks[0] > 0), mv2[:, first:last, 1], rs2[:, :, first:last])
                dve.wait_ge(y_done.sem, y_done.before(b, 2))
                for n in range(first, last):
                    cb, j = divmod(n, NJ)
                    dve.tensor_scalar(zn[:, cb, j, :], z[:, cb, j, :], mv2[:, n, 0:1], rs2[:, 1, n:n + 1],
                                      ALU.subtract, ALU.mult).then_inc(zn_done.sem, 1)

            def mlp_bias(b, cb):
                for jp in range(2):
                    ps = await_bank(dve, ("mlp", cb, jp), b)
                    drain(dve.tensor_tensor(mid[:, cb, 2 * jp:2 * jp + 2, :], ps[:], over_rows(mlpb_all, 2),
                                            ALU.add), ("mlp", cb, jp), b)

            def pooled(src, dst, lh):
                return dve.tensor_reduce(
                    dst[:, lh * P:(lh + 1) * P].rearrange("p (y x) -> p y x", x=W // 2),
                    src.rearrange("p a s -> p (a s)").rearrange("p (y i x k) -> p y x i k", i=2, k=2, x=W // 2),
                    AX.XY, ALU.max)

            def theta_phi(b):
                for lh in range(2):
                    ps = await_bank(dve, ("tp", lh), b)
                    dve.wait_ge(th_hi.sem, th_hi.at(b, 2 * lh + 2))
                    n = slice(lh * 512, (lh + 1) * 512)
                    dve.scalar_tensor_tensor(th_st[C8:2 * C8, n], ps[0:C8].rearrange("p a s -> p (a s)"),
                                             bth_c[0:C8], th_st[0:C8, n].bitcast(F32), ALU.add,
                                             ALU.subtract).then_inc(th_lo.sem, 1)
                    drain(pooled(ps[C8:2 * C8], ph_pool[0:C8], lh), ("tp", lh), b)
                for lh in range(2):
                    k = use(("tp", lh), b)
                    dve.wait_ge(k.drained, k.done)
                phi = ph_pool[0:C8]
                dve.tensor_scalar(phi, phi, bph_c[0:C8], None, ALU.add).then_inc(ph_step.sem, 1)
                dve.wait_ge(ph_step.sem, ph_step.at(b, 1))
                dve.tensor_copy(ph_st[0:C8], phi).then_inc(ph_step.sem, 1)
                dve.tensor_copy(ph_st[C8:2 * C8], phi).then_inc(ph_step.sem, 1)
                dve.wait_ge(ph_step.sem, ph_step.at(b, 3))
                dve.tensor_tensor(ph_st[2 * C8:3 * C8], phi, ph_st[0:C8].bitcast(F32),
                                  ALU.subtract).then_inc(ph_step.sem, 1)

            def g_rows(b):
                dve.wait_ge(ph_step.sem, ph_step.at(b, 4))
                for lh in range(2):
                    ps = await_bank(dve, ("g", lh), b)
                    drain(pooled(ps[:], g_pool[:], lh), ("g", lh), b)
                for lh in range(2):
                    k = use(("g", lh), b)
                    dve.wait_ge(k.drained, k.done)
                dve.tensor_scalar(g_pool[:], g_pool[:], bg_c, None, ALU.add).then_inc(g_bias.sem, 1)

            def maxima1(b, lh):
                k = s_ring.use(("s1", lh), b)
                dve.wait_ge(k.filled, k.full)
                dve.wait_ge(max1_split.sem, max1_split.before(b, lh + 1))
                dve.tensor_reduce(mx1[:, lh, :], ps_s[:], AX.X, ALU.max).then_inc(k.drained, 1)
                dve.wait_ge(k.drained, k.done)
                k = ring.previous(("mxt1", lh), b)
                dve.wait_ge(k.filled, k.full)
                dve.tensor_copy(mx1_hl[:, lh, 0, :], mx1[:, lh, :]).then_inc(max1_hi.sem, 1)
                dve.wait_ge(max1_hi.sem, max1_hi.at(b, lh + 1))
                dve.tensor_tensor(mx1_hl[:, lh, 1, :], mx1[:, lh, :], mx1_hl[:, lh, 0, :].bitcast(F32),
                                  ALU.subtract).then_inc(max1_split.sem, 1)

            def result(b):
                ps = await_bank(dve, ("den",), b)
                beside = b if isinstance(b, int) and b == B - 1 else b + 1
                dve.wait_ge(v_bank.drained, v_bank.done(beside, UNITS - 1))
                drain(dve.transpose(rden[:], ps[:, 0, :]), ("den",), b)
                k = use(("den",), b)
                dve.wait_ge(k.drained, k.done)
                dve.reciprocal(rd1[:], rden[:, 0:S_:32]).then_inc(rd1_step.sem, 1)
                dve.wait_ge(rd1_step.sem, rd1_step.at(b, 1))
                dve.tensor_scalar(rd1[:], rd1[:], sigma[:], None, ALU.mult).then_inc(rd1_step.sem, 1)
                dve.wait_ge(rd1_step.sem, rd1_step.at(b, 2))
                for cb in range(2):
                    dve.wait_ge(ybo_done.sem, ybo_done.at(b, cb + 1))
                    for jp in range(2):
                        ps = await_bank(dve, ("o", cb, jp), b)
                        for jj in range(2):
                            j = 2 * jp + jj
                            n = cb * NJ + j
                            ins = dve.scalar_tensor_tensor(z[:, cb, j, :], ps[:, jj, :], rd1[:, n:n + 1],
                                                           z[:, cb, j, :], ALU.mult, ALU.add)
                        drain(ins, ("o", cb, jp), b)

            def l1_step(b, s):
                if s in MLP_AT:
                    mlp_bias(b, MLP_AT.index(s))
                if s == THETA_PHI_AT:
                    theta_phi(b)
                if s in SCORES1_AT:
                    maxima1(b, SCORES1_AT.index(s))
                if s == G_AT:
                    g_rows(b)
                if s == ATTEND1_AT:
                    result(b)

            def turn(pb, b, nb):
                front = nb is not None
                if front:
                    row_stats(nb)
                if pb is not None:
                    l1_step(pb, MLP_AT[0])
                for s in range(STEPS):
                    if s < UNITS:
                        maxima(b, s, 0)
                    if s >= 3:
                        denominators(b, s - 3)
                    if pb is not None and s == MLP_AT[1]:
                        l1_step(pb, s)
                    if s < UNITS:
                        maxima(b, s, 1)
                        split_maxima(b, s)
                    if s >= 3:
                        normalise(b, s - 3)
                    if 2 <= s <= UNITS + 1:
                        sum_blocks(b, s - 2)
                    if front and s == 0:
                        row_deviation(nb)
                    if pb is not None and s in (THETA_PHI_AT, SCORES1_AT[1]):
                        l1_step(pb, s)
                    if front:
                        if s in (1, 2):
                            row_norm(nb, s - 1)
                        for cb in range(CB):
                            if s == QIMG_AT[cb]:
                                q_image(nb, cb, 0)
                                q_image(nb, cb, 1)
                            if s == CONV_AT[cb] + 1:
                                conv_out(nb, cb)
                        if s in QUERY_AT:
                            query_lo(nb, *QUERY_AT[s])
                        if s == STEPS - 1:
                            query_lo(nb, 1, 0)
                            query_lo(nb, 1, 1)
                            positions(nb)
                    if pb is not None and s not in (MLP_AT[1], THETA_PHI_AT, SCORES1_AT[1]):
                        l1_step(pb, s)
                if front:
                    hats(nb)
                    residual(b, (0, 1))
                    residual_norm(b, (0, 1))
                else:
                    for cb in range(2):
                        residual(b, (cb,))
                        residual_norm(b, (cb,))
                if front:
                    key_lo(nb)
                    value_rows(nb)

            row_stats(0)
            row_deviation(0)
            for_norm.wait(dve)
            row_norm(0, 0)
            row_norm(0, 1)
            setup_orders()
            dve.wait_ge(setup_pool, 3)
            q_image(0, 0, 0)
            q_image(0, 0, 1)
            setup_columns()
            q_image(0, 1, 0)
            q_image(0, 1, 1)
            setup_queries()
            dve.wait_ge(setup_dve, D_QUERY)
            conv_out(0, 0)
            conv_out(0, 1)
            query_lo(0, 0, 0)
            query_lo(0, 0, 1)
            positions(0)
            query_lo(0, 1, 0)
            query_lo(0, 1, 1)
            setup_values()
            dve.wait_ge(setup_dve, D_ALL)
            hats(0)
            key_lo(0)
            value_rows(0)
            for_rest.wait(dve)
            turn(None, 0, 1)
            with dve.Fori(1, B - 1) as b:
                turn(b - 1, b, b + 1)
            turn(B - 2, B - 1, None)
            for s in range(MLP_AT[0], STEPS):
                if s == OUT_TURN_AT:
                    for cb in range(2):
                        dve.wait_ge(gelu_done.sem, gelu_done.at(B - 1, 2 * cb + 2))
                        dve.tensor_tensor(z[:, cb], z[:, cb], mid[:, cb], ALU.add).then_inc(y_done.sem, 1)
                l1_step(B - 1, s)

        @block.gpsimd
        def _(pool):
            pool.memset(dw_g[:], 0.0).then_inc(setup_pool, 1)
            pool.memset(vec_rows[:], 0.0).then_inc(setup_pool, 1)
            pool.memset(qpad[:], 0.0).then_inc(setup_pool, 1)
            pool.memset(ones[:], 1.0).then_inc(setup_pool, 1)
            for_conv.wait(pool)
            for_q.wait(pool)
            pool.tensor_tensor(
                conv_w[:].rearrange("p k h x c -> p (k h x) c"),
                dw_g[:].rearrange("p k h (x a) -> p (k h x) a", a=1).broadcast_to([P, 8 * 2 * KS, 32]),
                consts[:, K_M32:K_M32 + 32].rearrange("p (a c) -> p a c", a=1).broadcast_to([P, 8 * 2 * KS, 32]),
                ALU.mult).then_inc(setup_pool, 1)
            pool.wait_ge(setup_dve, D_COLS)
            pool.tensor_copy(t_bv, bv_c.rearrange("p (t a) -> p t a", a=1).broadcast_to([P, 2, P])).then_inc(setup_pool, 1)
            pool.tensor_copy(pw_all[:].rearrange("p t o c -> p o t c"),
                             pw_c.rearrange("p (o t a) -> p o t a", o=2, a=1).broadcast_to([P, 2, CB, P])
                             ).then_inc(setup_pool, 1)
            for_rest.wait(pool)
            pool.tensor_scalar(bo_all[:], bo_all[:], sigma[:], None, ALU.mult).then_inc(setup_pool, 1)
            pool.wait_ge(setup_pool, 8)

            def spread(b, u):
                pool.wait_ge(den_inv.sem, den_inv.at(b, u + 1))
                gate(pool, "pool")
                pool.tensor_copy(rden_cols[:].rearrange("p (k r) -> p k r", r=32),
                                 rden_one[:].rearrange("p (k r) -> p k r", r=1).broadcast_to([P, S_ // 32, 32])
                                 ).then_inc(den_spread.sem, 1)

            def outputs(b):
                for cb in range(2):
                    if not (isinstance(b, int) and b == B - 1):
                        pool.wait_ge(gelu_done.sem, gelu_done.at(b, 2 * cb + 2))
                        pool.tensor_tensor(z[:, cb], z[:, cb], mid[:, cb], ALU.add).then_inc(y_done.sem, 1)
                for cb in range(2):
                    for kt in range(CB):
                        k = use(("yt", cb, kt), b)
                        pool.wait_ge(k.filled, k.full)
                        gate(pool, "pool")
                    pool.tensor_tensor(z[:, cb], z[:, cb], over_rows(bo_all, NJ), ALU.add).then_inc(ybo_done.sem, 1)

            def turn(pb, b):
                if pb is not None:
                    outputs(pb)
                for u in range(UNITS):
                    spread(b, u)
                    if u in (3, 5):
                        if u == 3:
                            pool.wait_ge(xb_in.sem, xb_in.at(b, 1))
                        half = xb[:, (u - 3) // 2]
                        pool.tensor_tensor(half, half, over_rows(mob_all, NJ), ALU.add).then_inc(xb_biased.sem, 1)

            turn(None, 0)
            with pool.Fori(1, B - 1) as b:
                turn(b - 1, b)
            turn(B - 2, B - 1)
            outputs(B - 1)


_INS = ['x', 'L0_conv_ln_g', 'L0_conv_ln_b', 'L0_conv_wq', 'L0_conv_bq', 'L0_conv_wv', 'L0_conv_bv', 'L0_conv_dw_w',
        'L0_conv_dw_b', 'L0_conv_pw_w', 'L0_conv_mq_w', 'L0_conv_mq_b', 'L0_conv_mk_w', 'L0_conv_mk_b',
        'L0_conv_mv_w', 'L0_conv_mv_b', 'L0_conv_mo_w', 'L0_conv_mo_b', 'L0_conv_mlp_w', 'L0_conv_mlp_b',
        'L1_conv_w_theta', 'L1_conv_b_theta', 'L1_conv_w_phi', 'L1_conv_b_phi', 'L1_conv_w_g', 'L1_conv_b_g',
        'L1_conv_w_o', 'L1_conv_b_o', 'L1_conv_sigma']


def kernel(**inputs):
    import numpy as _np
    import concourse.bacc as _bacc
    from concourse import mybir as _mybir
    from concourse.bass_utils import run_bass_kernel_spmd as _run

    nc = _bacc.Bacc("TRN2", target_bir_lowering=False, num_devices=1)
    arrays, aps = {}, {}
    given = {name: _np.ascontiguousarray(inputs[name]) for name in _INS}
    given["L1_conv_sigma"] = given["L1_conv_sigma"].reshape(1)
    given["shape_constants"] = shape_constants()
    for name, v in given.items():
        arrays[f"in_{name}_dram"] = v
        aps[name] = nc.dram_tensor(f"in_{name}_dram", v.shape, _mybir.dt.from_np(v.dtype), kind="ExternalInput").ap()
    out = nc.dram_tensor("out_0_dram", (B, H, W, C), F32, kind="ExternalOutput").ap()
    build(nc, aps, out)
    r = _run(nc, [arrays], core_ids=[0])
    return r.results[0]["out_0_dram"]
```
